# Optimizing a Trainium2 kernel written in Bass

```python
import numpy as np
import jax
import jax.numpy as jnp

def _softmax(x, axis=-1):
    return jax.nn.softmax(x, axis=axis)

def _gelu(x):
    return jax.nn.gelu(x, approximate=True)

def _silu(x):
    return jax.nn.silu(x)

def _sigmoid(x):
    return jax.nn.sigmoid(x)

def _layernorm(x, axis=-1, eps=1e-05):
    m = jnp.mean(x, axis=axis, keepdims=True)
    v = jnp.var(x, axis=axis, keepdims=True)
    return (x - m) / jnp.sqrt(v + eps)

def _scatter_add(tgt, idx, src, axis=0):
    return tgt.at[idx].add(src)

def _segment_sum(src, seg, n):
    return jax.ops.segment_sum(src, seg, n)
kernel_name = 'mk_adaln_attn_ffn_d2_seqx_r8_f7a60d'

def setup_inputs(seed: int=0):
    np.random.seed(seed)
    _w = jnp.asarray

    def _rec_inputs():
        import jax
        import jax.numpy as jnp
        _rk = jax.random.key(seed)
        x = 0.5 + 0.2887 * jax.random.normal(jax.random.fold_in(_rk, 1), (8, 256, 128), jnp.float32)
        _lenS = 256 - jax.random.randint(jax.random.fold_in(_rk, 7), (8,), 0, max(1, 256 // 4) + 1, jnp.int32)
        _lenS2 = 256 - jax.random.randint(jax.random.fold_in(_rk, 8), (8,), 0, max(1, 256 // 4) + 1, jnp.int32)
        condB_zX = jax.random.uniform(jax.random.fold_in(_rk, 11), (8,), jnp.float32, 0.0, 0.983423)
        condB_zY = jax.random.uniform(jax.random.fold_in(_rk, 12), (8,), jnp.float32, 0.0, 0.979075)
        condB_zR = jax.random.uniform(jax.random.fold_in(_rk, 13), (8,), jnp.float32, 0.0, 0.9968)
        itok_B_0_7 = jax.random.randint(jax.random.fold_in(_rk, 14), (8,), 0, 8, jnp.int32)
        itok_B_0_2 = jax.random.randint(jax.random.fold_in(_rk, 15), (8,), 0, 3, jnp.int32)
        return (x, condB_zX, condB_zY, condB_zR, itok_B_0_7, itok_B_0_2)
    x, condB_zX, condB_zY, condB_zR, itok_B_0_7, itok_B_0_2 = _rec_inputs()

    def _L0_cond_setup():
        import jax, jax.numpy as jnp
        import numpy as np
        key = jax.random.key(seed)
        k1, k2, k3, k4 = jax.random.split(key, 4)
        B, H, W = (64, 128, 128)
        return {'y': jax.random.uniform(k1, (B, H, W), dtype=jnp.float32), 'zX': jax.random.uniform(k2, (B, 1), dtype=jnp.float32), 'zY': jax.random.uniform(k3, (B, 1), dtype=jnp.float32), 'zR': jax.random.uniform(k4, (B, 1), dtype=jnp.float32), 'dx': 1, 'dy': 1}
    _L0_cond_all = _L0_cond_setup()
    _L0_cond_in = {k: v for k, v in _L0_cond_all.items() if k in ()}
    del _L0_cond_all

    def _L0_attn_setup():
        import jax, jax.numpy as jnp
        import numpy as np
        D_MODEL = 128
        D_STATE = 16
        D_CONV = 4
        EXPAND = 2
        N_LAYERS = 4
        D_INNER = EXPAND * D_MODEL
        DT_RANK = (D_MODEL + 15) // 16
        BATCH, SEQ = (2, 128)
        LN_EPS = 1e-05

        def _layer_norm(x, g, b):
            mu = jnp.mean(x, axis=-1, keepdims=True)
            var = jnp.mean(jnp.square(x - mu), axis=-1, keepdims=True)
            return (x - mu) * jax.lax.rsqrt(var + LN_EPS) * g + b

        def _scan_combine(e1, e2):
            a1, b1 = e1
            a2, b2 = e2
            return (a1 * a2, a2 * b1 + b2)

        def _mamba_block(x, in_w, cw, cb, xp_w, dt_w, dt_b, A_log, D_skip, out_w):
            xz = jnp.einsum('bld,ed->ble', x, in_w)
            xm, z = jnp.split(xz, 2, axis=-1)
            xc = jnp.transpose(xm, (0, 2, 1))
            xc = jax.lax.conv_general_dilated(xc, cw[:, None, :], window_strides=(1,), padding=[(D_CONV - 1, 0)], feature_group_count=D_INNER, dimension_numbers=('NCH', 'OIH', 'NCH'))
            xm = jax.nn.silu(jnp.transpose(xc, (0, 2, 1)) + cb[None, None, :])
            xdbl = jnp.einsum('bld,ed->ble', xm, xp_w)
            dt, Bm, Cm = jnp.split(xdbl, [DT_RANK, DT_RANK + D_STATE], axis=-1)
            dt = jax.nn.softplus(jnp.einsum('blr,dr->bld', dt, dt_w) + dt_b)
            A = -jnp.exp(A_log)
            dA = jnp.exp(dt[..., None] * A)
            dBu = dt[..., None] * Bm[:, :, None, :] * xm[..., None]
            _, h = jax.lax.associative_scan(_scan_combine, (dA, dBu), axis=1)
            y = jnp.einsum('blds,bls->bld', h, Cm) + xm * D_skip
            y = y * jax.nn.silu(z)
            return jnp.einsum('bld,od->blo', y, out_w)
        key = jax.random.key(seed)
        ks = jax.random.split(key, 10)
        s = 0.02
        A_log = jnp.log(jnp.broadcast_to(jnp.arange(1, D_STATE + 1, dtype=jnp.float32), (N_LAYERS, D_INNER, D_STATE)))
        return {'x': jax.random.normal(ks[0], (BATCH, SEQ, D_MODEL), jnp.float32), 'in_proj_w': jax.random.normal(ks[1], (N_LAYERS, 2 * D_INNER, D_MODEL), jnp.float32) * s, 'conv_w': jax.random.normal(ks[2], (N_LAYERS, D_INNER, D_CONV), jnp.float32) * s, 'conv_b': jnp.zeros((N_LAYERS, D_INNER), jnp.float32), 'x_proj_w': jax.random.normal(ks[3], (N_LAYERS, DT_RANK + 2 * D_STATE, D_INNER), jnp.float32) * s, 'dt_proj_w': jax.random.normal(ks[4], (N_LAYERS, D_INNER, DT_RANK), jnp.float32) * s, 'dt_proj_b': jax.random.uniform(ks[5], (N_LAYERS, D_INNER), jnp.float32, -5.0, -3.0), 'A_log': A_log, 'D_skip': jnp.ones((N_LAYERS, D_INNER), jnp.float32), 'out_proj_w': jax.random.normal(ks[6], (N_LAYERS, D_MODEL, D_INNER), jnp.float32) * s, 'ln_g': jnp.ones((D_MODEL,), jnp.float32), 'ln_b': jnp.zeros((D_MODEL,), jnp.float32)}
    _L0_attn_all = _L0_attn_setup()
    _L0_attn_in = {k: v for k, v in _L0_attn_all.items() if k in ('in_proj_w', 'conv_w', 'conv_b', 'x_proj_w', 'dt_proj_w', 'dt_proj_b', 'A_log', 'D_skip', 'out_proj_w', 'ln_g', 'ln_b')}
    del _L0_attn_all

    def _L0_cond2_setup():
        import jax, jax.numpy as jnp
        import numpy as np
        IN, HID, OUT, PART, E = (128, 512, 128, 32, 8)
        B, N = (16, 256)
        key = jax.random.key(seed)
        ks = jax.random.split(key, 8)
        s1 = 1.0 / np.sqrt(IN)
        s2 = 1.0 / np.sqrt(HID)
        return {'x': jax.random.normal(ks[0], (B, N, IN), dtype=jnp.float32), 'indices': jax.random.randint(ks[1], (B,), 0, E, dtype=jnp.int64), 'W1': jax.random.uniform(ks[2], (IN, HID), jnp.float32, -s1, s1), 'b1': jax.random.uniform(ks[3], (HID,), jnp.float32, -s1, s1), 'W2': jax.random.uniform(ks[4], (HID, OUT - PART), jnp.float32, -s2, s2), 'b2': jax.random.uniform(ks[5], (OUT - PART,), jnp.float32, -s2, s2), 'We': jax.random.uniform(ks[6], (E, HID, PART), jnp.float32, -s2, s2), 'be': jax.random.uniform(ks[7], (E, PART), jnp.float32, -s2, s2)}
    _L0_cond2_all = _L0_cond2_setup()
    _L0_cond2_in = {k: v for k, v in _L0_cond2_all.items() if k in ('W1', 'b1', 'W2', 'b2', 'We', 'be')}
    del _L0_cond2_all

    def _L0_ffn_setup():
        import jax, jax.numpy as jnp
        import numpy as np
        E = 8
        TOPK = 2
        D = 128
        F = 512
        B, S = (2, 64)

        def _gmm(x, W, expert_onehot):
            return jnp.einsum('te,td,edf->tf', expert_onehot, x, W)
        key = jax.random.key(seed)
        k1, k2, k3, k4, k5 = jax.random.split(key, 5)
        scale_d = 1.0 / np.sqrt(D)
        scale_f = 1.0 / np.sqrt(F)
        return {'inputs': jax.random.normal(k1, (B, S, D), jnp.float32), 'gate_kernel': jax.random.normal(k2, (D, E), jnp.float32) * scale_d, 'w0': jax.random.normal(k3, (E, D, F), jnp.float32) * scale_d, 'w1': jax.random.normal(k4, (E, D, F), jnp.float32) * scale_d, 'wo': jax.random.normal(k5, (E, F, D), jnp.float32) * scale_f}
    _L0_ffn_all = _L0_ffn_setup()
    _L0_ffn_in = {k: v for k, v in _L0_ffn_all.items() if k in ('gate_kernel', 'w0', 'w1', 'wo')}
    del _L0_ffn_all

    def _L1_cond_setup():
        import jax, jax.numpy as jnp
        import numpy as np
        NEG_INF = -1e+30
        key = jax.random.key(seed)
        k1, k2, k3, k4, k5 = jax.random.split(key, 5)
        B, S, D, A = (16, 128, 128, 32)
        hidden = jax.random.normal(k1, (B, S, D), dtype=jnp.float32)
        W1 = jax.random.normal(k2, (D, A), dtype=jnp.float32) / np.sqrt(D)
        b1 = jax.random.normal(k3, (A,), dtype=jnp.float32) * 0.01
        v = jax.random.normal(k4, (A,), dtype=jnp.float32) / np.sqrt(A)
        prompt_type_ids = jax.random.randint(k5, (B,), 0, 3, dtype=jnp.int32)
        return {'hidden': hidden, 'W1': W1, 'b1': b1, 'v': v, 'prompt_type_ids': prompt_type_ids}
    _L1_cond_all = _L1_cond_setup()
    _L1_cond_in = {k: v for k, v in _L1_cond_all.items() if k in ('W1', 'b1', 'v')}
    del _L1_cond_all

    def _L1_attn_setup():
        import jax, jax.numpy as jnp
        import numpy as np
        B, T, C = (64, 32, 128)
        N_HEAD, HEAD_SIZE, KV_RANK = (16, 64, 128)
        BLOCK_SIZE = 32
        key = jax.random.key(seed)
        ks = jax.random.split(key, 5)
        HD = N_HEAD * HEAD_SIZE

        def init(k, shape):
            fan_in = shape[0]
            bound = 1.0 / np.sqrt(fan_in)
            return jax.random.uniform(k, shape, jnp.float32, -bound, bound)
        return {'x': jax.random.normal(ks[0], (B, T, C), jnp.float32), 'w_kv_down': init(ks[1], (C, KV_RANK)), 'w_kv_up': init(ks[2], (KV_RANK, 2 * HD)), 'w_q': init(ks[3], (C, HD)), 'w_out': init(ks[4], (HD, C))}
    _L1_attn_all = _L1_attn_setup()
    _L1_attn_in = {k: v for k, v in _L1_attn_all.items() if k in ('w_kv_down', 'w_kv_up', 'w_q', 'w_out')}
    del _L1_attn_all

    def _L1_cond2_setup():
        import jax, jax.numpy as jnp
        import numpy as np
        S, O, H = (8, 128, 128)
        B, N = (32, 64)
        key = jax.random.key(seed)
        k1, k2, k3, k4 = jax.random.split(key, 4)
        x = jax.random.normal(k1, (B, N, H), dtype=jnp.float32)
        subject_id = jax.random.randint(k2, (B,), 0, S)
        wbound = jnp.sqrt(2.0 / 6.0) * jnp.sqrt(3.0 / H)
        weight = jax.random.uniform(k3, (S, O, H), minval=-wbound, maxval=wbound, dtype=jnp.float32)
        bbound = 1.0 / jnp.sqrt(H)
        bias = jax.random.uniform(k4, (S, O), minval=-bbound, maxval=bbound, dtype=jnp.float32)
        return {'x': x, 'subject_id': subject_id, 'weight': weight, 'bias': bias}
    _L1_cond2_all = _L1_cond2_setup()
    _L1_cond2_in = {k: v for k, v in _L1_cond2_all.items() if k in ('weight', 'bias')}
    del _L1_cond2_all

    def _L1_ffn_setup():
        import jax, jax.numpy as jnp
        import numpy as np
        EMBED_DIM = 128
        HIDDEN = 4 * EMBED_DIM
        BATCH, SEQ = (4, 512)
        EPS = 1e-05

        def _quant_weight(w):
            s = jnp.clip(jnp.mean(jnp.abs(w)), EPS, None)
            wq = jnp.clip(jnp.round(w / s), -1.0, 1.0) * s
            return w + jax.lax.stop_gradient(wq - w)

        def _quant_act(x):
            scale = 127.0 / jnp.clip(jnp.max(jnp.abs(x), axis=-1, keepdims=True), EPS, None)
            xq = jnp.clip(jnp.round(x * scale), -128.0, 127.0) / scale
            return x + jax.lax.stop_gradient(xq - x)

        def _bitlinear(x, w):
            return jnp.einsum('bsi,oi->bso', _quant_act(x), _quant_weight(w))
        key = jax.random.key(seed)
        k1, k2, k3 = jax.random.split(key, 3)
        x = jax.random.normal(k1, (BATCH, SEQ, EMBED_DIM), dtype=jnp.float32)
        w1 = jax.random.normal(k2, (HIDDEN, EMBED_DIM), dtype=jnp.float32) * (1.0 / np.sqrt(EMBED_DIM))
        w2 = jax.random.normal(k3, (EMBED_DIM, HIDDEN), dtype=jnp.float32) * (1.0 / np.sqrt(HIDDEN))
        return {'x': x, 'w1': w1, 'w2': w2}
    _L1_ffn_all = _L1_ffn_setup()
    _L1_ffn_in = {k: v for k, v in _L1_ffn_all.items() if k in ('w1', 'w2')}
    del _L1_ffn_all
    return {'x': x, 'condB_zX': condB_zX, 'condB_zY': condB_zY, 'condB_zR': condB_zR, 'itok_B_0_7': itok_B_0_7, 'itok_B_0_2': itok_B_0_2, 'L0_attn_in_proj_w': _L0_attn_in['in_proj_w'], 'L0_attn_conv_w': _L0_attn_in['conv_w'], 'L0_attn_conv_b': _L0_attn_in['conv_b'], 'L0_attn_x_proj_w': _L0_attn_in['x_proj_w'], 'L0_attn_dt_proj_w': _L0_attn_in['dt_proj_w'], 'L0_attn_dt_proj_b': _L0_attn_in['dt_proj_b'], 'L0_attn_A_log': _L0_attn_in['A_log'], 'L0_attn_D_skip': _L0_attn_in['D_skip'], 'L0_attn_out_proj_w': _L0_attn_in['out_proj_w'], 'L0_attn_ln_g': _L0_attn_in['ln_g'], 'L0_attn_ln_b': _L0_attn_in['ln_b'], 'L0_cond2_W1': _L0_cond2_in['W1'], 'L0_cond2_b1': _L0_cond2_in['b1'], 'L0_cond2_W2': _L0_cond2_in['W2'], 'L0_cond2_b2': _L0_cond2_in['b2'], 'L0_cond2_We': _L0_cond2_in['We'], 'L0_cond2_be': _L0_cond2_in['be'], 'L0_ffn_gate_kernel': _L0_ffn_in['gate_kernel'], 'L0_ffn_w0': _L0_ffn_in['w0'], 'L0_ffn_w1': _L0_ffn_in['w1'], 'L0_ffn_wo': _L0_ffn_in['wo'], 'L1_cond_W1': _L1_cond_in['W1'], 'L1_cond_b1': _L1_cond_in['b1'], 'L1_cond_v': _L1_cond_in['v'], 'L1_attn_w_kv_down': _L1_attn_in['w_kv_down'], 'L1_attn_w_kv_up': _L1_attn_in['w_kv_up'], 'L1_attn_w_q': _L1_attn_in['w_q'], 'L1_attn_w_out': _L1_attn_in['w_out'], 'L1_cond2_weight': _L1_cond2_in['weight'], 'L1_cond2_bias': _L1_cond2_in['bias'], 'L1_ffn_w1': _L1_ffn_in['w1'], 'L1_ffn_w2': _L1_ffn_in['w2']}

def reference(x, condB_zX, condB_zY, condB_zR, itok_B_0_7, itok_B_0_2, L0_attn_in_proj_w, L0_attn_conv_w, L0_attn_conv_b, L0_attn_x_proj_w, L0_attn_dt_proj_w, L0_attn_dt_proj_b, L0_attn_A_log, L0_attn_D_skip, L0_attn_out_proj_w, L0_attn_ln_g, L0_attn_ln_b, L0_cond2_W1, L0_cond2_b1, L0_cond2_W2, L0_cond2_b2, L0_cond2_We, L0_cond2_be, L0_ffn_gate_kernel, L0_ffn_w0, L0_ffn_w1, L0_ffn_wo, L1_cond_W1, L1_cond_b1, L1_cond_v, L1_attn_w_kv_down, L1_attn_w_kv_up, L1_attn_w_q, L1_attn_w_out, L1_cond2_weight, L1_cond2_bias, L1_ffn_w1, L1_ffn_w2):
    import jax
    import jax.numpy as jnp

    def _L0_cond_ref(y, zX, zY, zR, dx, dy):
        import jax, jax.numpy as jnp
        import numpy as np
        yp_x = jnp.pad(y, ((0, 0), (0, 0), (1, 1)), mode='reflect')
        lap_x = (yp_x[:, :, :-2] - 2.0 * y + yp_x[:, :, 2:]) / (dx * dx)
        yp_y = jnp.pad(y, ((0, 0), (1, 1), (0, 0)), mode='reflect')
        lap_y = (yp_y[:, :-2, :] - 2.0 * y + yp_y[:, 2:, :]) / (dy * dy)
        du_dt = zX[:, :, None] * lap_x + zY[:, :, None] * lap_y + zR[:, :, None] * y * (1.0 - y)
        return du_dt

    def _L0_attn_ref(x, in_proj_w, conv_w, conv_b, x_proj_w, dt_proj_w, dt_proj_b, A_log, D_skip, out_proj_w, ln_g, ln_b):
        import jax, jax.numpy as jnp
        import numpy as np
        D_MODEL = 128
        D_STATE = 16
        D_CONV = 4
        EXPAND = 2
        N_LAYERS = 4
        D_INNER = EXPAND * D_MODEL
        DT_RANK = (D_MODEL + 15) // 16
        BATCH, SEQ = (2, 128)
        LN_EPS = 1e-05

        def _layer_norm(x, g, b):
            mu = jnp.mean(x, axis=-1, keepdims=True)
            var = jnp.mean(jnp.square(x - mu), axis=-1, keepdims=True)
            return (x - mu) * jax.lax.rsqrt(var + LN_EPS) * g + b

        def _scan_combine(e1, e2):
            a1, b1 = e1
            a2, b2 = e2
            return (a1 * a2, a2 * b1 + b2)

        def _mamba_block(x, in_w, cw, cb, xp_w, dt_w, dt_b, A_log, D_skip, out_w):
            xz = jnp.einsum('bld,ed->ble', x, in_w)
            xm, z = jnp.split(xz, 2, axis=-1)
            xc = jnp.transpose(xm, (0, 2, 1))
            xc = jax.lax.conv_general_dilated(xc, cw[:, None, :], window_strides=(1,), padding=[(D_CONV - 1, 0)], feature_group_count=D_INNER, dimension_numbers=('NCH', 'OIH', 'NCH'))
            xm = jax.nn.silu(jnp.transpose(xc, (0, 2, 1)) + cb[None, None, :])
            xdbl = jnp.einsum('bld,ed->ble', xm, xp_w)
            dt, Bm, Cm = jnp.split(xdbl, [DT_RANK, DT_RANK + D_STATE], axis=-1)
            dt = jax.nn.softplus(jnp.einsum('blr,dr->bld', dt, dt_w) + dt_b)
            A = -jnp.exp(A_log)
            dA = jnp.exp(dt[..., None] * A)
            dBu = dt[..., None] * Bm[:, :, None, :] * xm[..., None]
            _, h = jax.lax.associative_scan(_scan_combine, (dA, dBu), axis=1)
            y = jnp.einsum('blds,bls->bld', h, Cm) + xm * D_skip
            y = y * jax.nn.silu(z)
            return jnp.einsum('bld,od->blo', y, out_w)
        for i in range(N_LAYERS):
            x = x + _mamba_block(_layer_norm(x, ln_g, ln_b), in_proj_w[i], conv_w[i], conv_b[i], x_proj_w[i], dt_proj_w[i], dt_proj_b[i], A_log[i], D_skip[i], out_proj_w[i])
        return _layer_norm(x, ln_g, ln_b)

    def _L0_cond2_ref(x, indices, W1, b1, W2, b2, We, be):
        import jax, jax.numpy as jnp
        import numpy as np
        IN, HID, OUT, PART, E = (128, 512, 128, 32, 8)
        B, N = (16, 256)
        h = jax.nn.gelu(jnp.einsum('bni,ih->bnh', x, W1) + b1, approximate=False)
        shared_x = jnp.einsum('bnh,ho->bno', h, W2) + b2
        We_sel = We[indices]
        be_sel = be[indices]
        expert_x = jnp.einsum('bnh,bhp->bnp', h, We_sel) + be_sel[:, None, :]
        return jnp.concatenate([shared_x, expert_x], axis=-1)

    def _L0_ffn_ref(inputs, gate_kernel, w0, w1, wo):
        import jax, jax.numpy as jnp
        import numpy as np
        E = 8
        TOPK = 2
        D = 128
        F = 512
        B, S = (2, 64)

        def _gmm(x, W, expert_onehot):
            return jnp.einsum('te,td,edf->tf', expert_onehot, x, W)
        dtype = inputs.dtype
        gate_logits = jnp.einsum('bsd,de->bse', inputs, gate_kernel)
        weights, selected_experts = jax.lax.top_k(gate_logits, TOPK)
        weights = jax.nn.softmax(weights.astype(jnp.float32), axis=-1).astype(dtype)
        inputs_2d = jnp.reshape(inputs, (-1, D))
        flat_sel = jnp.ravel(selected_experts)
        sort_idx = jnp.argsort(flat_sel)
        rep = jnp.repeat(inputs_2d, TOPK, axis=0)
        sorted_hidden = jnp.take(rep, sort_idx, axis=0)
        T = flat_sel.shape[0]
        group_sizes = jnp.zeros((E,), jnp.int32).at[flat_sel].add(1)
        expert_ids = jnp.repeat(jnp.arange(E), group_sizes, total_repeat_length=T)
        onehot = jax.nn.one_hot(expert_ids, E, dtype=dtype)
        layer_1 = _gmm(sorted_hidden, w0, onehot)
        layer_2 = _gmm(sorted_hidden, w1, onehot)
        intermediate = jax.nn.silu(layer_1) * layer_2
        layer_3 = _gmm(intermediate, wo, onehot)
        unsort = jnp.take(layer_3, jnp.argsort(sort_idx), axis=0)
        combined = unsort * jnp.ravel(weights)[:, None]
        out = jnp.sum(combined.reshape(-1, TOPK, D), axis=1)
        return out.reshape(inputs.shape).astype(dtype)

    def _L1_cond_ref(hidden, W1, b1, v, prompt_type_ids):
        import jax, jax.numpy as jnp
        import numpy as np
        NEG_INF = -1e+30
        B, S, D = hidden.shape
        attn_in = jnp.tanh(jnp.einsum('bsd,da->bsa', hidden, W1) + b1)
        scores = jnp.einsum('bsa,a->bs', attn_in, v)
        idx = jnp.arange(S)
        j = idx[:, None]
        l = idx[None, :]
        prefix_m = l <= j
        postfix_m = l >= j
        cloze_m = l != j
        pt = prompt_type_ids[:, None, None]
        mask = jnp.where(pt == 0, prefix_m[None], jnp.where(pt == 1, postfix_m[None], cloze_m[None]))
        masked_scores = jnp.where(mask, scores[:, None, :], NEG_INF)
        p = jax.nn.softmax(masked_scores, axis=-1)
        cnt = jnp.sum(mask, axis=-1).astype(hidden.dtype)
        pooled = jnp.einsum('bjl,bld->bjd', p, hidden) / cnt[..., None]
        return pooled

    def _L1_attn_ref(x, w_kv_down, w_kv_up, w_q, w_out):
        import jax, jax.numpy as jnp
        import numpy as np
        B, T, C = (64, 32, 128)
        N_HEAD, HEAD_SIZE, KV_RANK = (16, 64, 128)
        BLOCK_SIZE = 32
        Bx, Tx, Cx = x.shape
        HD = N_HEAD * HEAD_SIZE
        latent_kv = x @ w_kv_down
        kv = latent_kv @ w_kv_up
        k, v = (kv[..., :HD], kv[..., HD:])
        k = k.reshape(Bx, Tx, N_HEAD, HEAD_SIZE)
        v = v.reshape(Bx, Tx, N_HEAD, HEAD_SIZE)
        q = (x @ w_q).reshape(Bx, Tx, N_HEAD, HEAD_SIZE)
        scale = HEAD_SIZE ** (-0.5)
        att = jnp.einsum('bqhd,bkhd->bhqk', q, k) * scale
        causal = jnp.tril(jnp.ones((Tx, Tx), dtype=bool))
        att = jnp.where(causal, att, -jnp.inf)
        att = jax.nn.softmax(att, axis=-1)
        y = jnp.einsum('bhqk,bkhd->bqhd', att, v)
        y = y.reshape(Bx, Tx, HD)
        return y @ w_out

    def _L1_cond2_ref(x, subject_id, weight, bias):
        import jax, jax.numpy as jnp
        import numpy as np
        S, O, H = (8, 128, 128)
        B, N = (32, 64)
        W = weight[subject_id]
        b = bias[subject_id]
        y = jnp.einsum('bnh,boh->bno', x, W) + b[:, None, :]
        return y

    def _L1_ffn_ref(x, w1, w2):
        import jax, jax.numpy as jnp
        import numpy as np
        EMBED_DIM = 128
        HIDDEN = 4 * EMBED_DIM
        BATCH, SEQ = (4, 512)
        EPS = 1e-05

        def _quant_weight(w):
            s = jnp.clip(jnp.mean(jnp.abs(w)), EPS, None)
            wq = jnp.clip(jnp.round(w / s), -1.0, 1.0) * s
            return w + jax.lax.stop_gradient(wq - w)

        def _quant_act(x):
            scale = 127.0 / jnp.clip(jnp.max(jnp.abs(x), axis=-1, keepdims=True), EPS, None)
            xq = jnp.clip(jnp.round(x * scale), -128.0, 127.0) / scale
            return x + jax.lax.stop_gradient(xq - x)

        def _bitlinear(x, w):
            return jnp.einsum('bsi,oi->bso', _quant_act(x), _quant_weight(w))
        h = jax.nn.gelu(_bitlinear(x, w1), approximate=False)
        return _bitlinear(h, w2)
    x = x + _L0_attn_ref(_L0_cond_ref(x, condB_zX[:, None], condB_zY[:, None], condB_zR[:, None], 1, 1), L0_attn_in_proj_w, L0_attn_conv_w, L0_attn_conv_b, L0_attn_x_proj_w, L0_attn_dt_proj_w, L0_attn_dt_proj_b, L0_attn_A_log, L0_attn_D_skip, L0_attn_out_proj_w, L0_attn_ln_g, L0_attn_ln_b)
    x = x + _L0_ffn_ref(_L0_cond2_ref(x, itok_B_0_7, L0_cond2_W1, L0_cond2_b1, L0_cond2_W2, L0_cond2_b2, L0_cond2_We, L0_cond2_be), L0_ffn_gate_kernel, L0_ffn_w0, L0_ffn_w1, L0_ffn_wo)
    x = x + _L1_attn_ref(_L1_cond_ref(x, L1_cond_W1, L1_cond_b1, L1_cond_v, itok_B_0_2), L1_attn_w_kv_down, L1_attn_w_kv_up, L1_attn_w_q, L1_attn_w_out)
    x = x + _L1_ffn_ref(_L1_cond2_ref(x, itok_B_0_7, L1_cond2_weight, L1_cond2_bias), L1_ffn_w1, L1_ffn_w2)
    return x

_drawn_inputs = setup_inputs


def setup_inputs(seed=0):
    import zlib

    import numpy as np

    out = dict(_drawn_inputs(seed))
    spreads = {'L0_attn_conv_b': (0.0, 0.1),
     'L0_attn_D_skip': (1.0, 0.2),
     'L0_attn_ln_g': (1.0, 0.2),
     'L0_attn_ln_b': (0.0, 0.1)}
    factors = {}
    for name, (base, spread) in spreads.items():
        noise = np.random.default_rng([zlib.crc32(name.encode()), seed]).standard_normal(out[name].shape)
        drawn = base * np.exp(spread * noise) if base else spread * noise
        out[name] = jnp.asarray(drawn.astype(out[name].dtype))
    for name, factor in factors.items():
        out[name] = (out[name] * factor).astype(out[name].dtype)
    return out
```

```python
from contextlib import ExitStack

import concourse.bass as bass
from concourse import mybir

F32 = mybir.dt.float32
BF16 = mybir.dt.bfloat16
I32 = mybir.dt.int32
U32 = mybir.dt.uint32
ALU = mybir.AluOpType
ACT = mybir.ActivationFunctionType
AX_X = mybir.AxisListType.X

P = 128
B, S, D = 8, 256, 128
TOK = B * S
NT = TOK // P
HALVES = 2
NS = 16
RANK = 8
TAPS = 4
LAYERS = 4
PAIR = 2 * S
NPAIR = B // 2
SLOTS = LAYERS * NPAIR
LN_EPS = 1e-5
BIG = 1.0e30
FF = 512
FC = FF // P
NE = 8
MC = 96
NH, HS = 16, 64
HD = NH * HS
SCALE = HS ** -0.5
TRI = 3 * P
ROUND = 1.5 * 2 ** 23
RT, RT_DIFF = 18, 12

XPN = 3 * 2 * NS + RANK
BC3 = 3 * 2 * NS
FC_TAP = 0
FC_Z = TAPS * 2 * P
FC_XP = FC_Z + 2 * P
FC_DTB = FC_XP + HALVES * XPN
FC_CB = FC_DTB + HALVES
FC_END = FC_CB + HALVES
SC_D = 0
SC_OUT = HALVES * P
SC_END = SC_OUT + HALVES * P


def wait(eng, sem, value):
    if isinstance(value, int) and value <= 0:
        return
    eng.wait_ge(sem, value)


def program(nc, io, stop_after=None):
    with ExitStack() as ctx:
        def sb(name, shape, dt=F32):
            return ctx.enter_context(nc.sbuf_tensor(name, shape, dt))

        def pb(name, shape, dt=F32):
            return ctx.enter_context(nc.psum_tensor(name, shape, dt))

        sems = {}

        def sem(name):
            if name not in sems:
                sems[name] = ctx.enter_context(nc.semaphore(name))
            return sems[name]

        banks = pb("banks", [P, 8, 512])
        ps_B = [banks[:, 2 * i:2 * i + 2, :].rearrange("p a (b l) -> p (a b) l", b=2) for i in range(2)]
        ps_C = banks[:, 4, :].rearrange("p (a l) -> p a l", a=2)
        ps_Y = banks[:, 5, :].rearrange("p (a l) -> p a l", a=2)
        ps_F = [banks[:, 6 + i, :] for i in range(2)]

        ident = sb("ident", [P, P])
        mean_w = sb("mean_w", [P, P])
        ypad = sb("ypad", [P, B, S + 2])
        xs = sb("xs", [P, TOK])

        zb = sb("zb", [P, 3, B])
        lng = sb("lng", [P, 1])
        lnb = sb("lnb", [P, 1])
        eps = sb("eps", [P, 1])
        sel = sb("sel", [BC3, 2 * NS, P], BF16)
        h = [sb(f"h{i}", [P, NS, S]) for i in range(4)]
        dA = [sb(f"dA{i}", [P, NS, S]) for i in range(2)]
        Cb = [sb(f"Cb{i}", [P, NS, S]) for i in range(2)]
        wF = sb("wF", [P, FC_END])
        wS = sb("wS", [P, SC_END])
        wdt = sb("wdt", [P, HALVES * P])
        A_all = sb("A_all", [P, LAYERS, HALVES * NS])
        A_cur = [sb(f"A_cur{i}", [P, HALVES * NS]) for i in range(2)]
        xm = [sb(f"xm{i}", [P, HALVES, PAIR]) for i in range(2)]
        zs = [sb(f"zs{i}", [P, HALVES, PAIR]) for i in range(2)]
        dt = sb("dt", [P, HALVES, PAIR])
        u = sb("u", [P, HALVES, PAIR])
        bc = [sb(f"bc{i}", [BC3, PAIR], BF16) for i in range(2)]
        xc = sb("xc", [P, PAIR])
        rstd = sb("rstd", [P, PAIR])
        xn = sb("xn", [P, 2, S + TAPS - 1])
        xh = sb("xh", [P, HALVES, PAIR])
        th = sb("th", [P, HALVES, PAIR])
        yz = sb("yz", [P, HALVES, 2, S])
        ids = sb("ids", [1, B], I32)
        smx2 = sb("smx2", [P, 2, NH])
        prc_f = smx2[:, 0, 0:B]
        r1 = xc[0:BC3, :]
        r2 = th[0:BC3, 0, 0:PAIR // 2].bitcast(BF16)
        tri = Cb[0][:, 0, 0:P]
        dt8 = rstd[BC3:BC3 + RANK, :]

        flat = [t[:, :, :].rearrange("p a b -> p (a b)") for t in (*h, *dA)]
        raw_in, raw_cw = flat[0][:, 0:2 * P], flat[0][:, 2 * P:2 * P + TAPS * 2 * P]
        o = 2 * P + TAPS * 2 * P
        raw_out, raw_sm = flat[0][:, o:o + HALVES * P], flat[0][:, o + HALVES * P:o + HALVES * P + 2 * HALVES]
        bunF, bunS = flat[1][:, 0:FC_END], flat[1][:, FC_END:FC_END + SC_END]
        xtok = flat[2][:, 0:TOK].rearrange("p (a b) -> p a b", a=NT)
        lapx = flat[3][:, 0:TOK].rearrange("p (a b) -> p a b", a=B)
        lapy = flat[3][:, TOK:2 * TOK].rearrange("p (a b) -> p a b", a=B)
        grow = flat[2][:, TOK:2 * TOK].rearrange("p (a b) -> p a b", a=B)
        scrF = nc.dram_tensor("scrF", [LAYERS, P, FC_END], F32).ap()
        scrS = nc.dram_tensor("scrS", [LAYERS, P, SC_END], F32).ap()

        out_tok = io["out"].rearrange("b (c p) f -> p (b c) f", p=P)
        x_tok = io["x"].rearrange("b (c p) f -> p (b c) f", p=P)

        def layer_of(ap, L):
            return ap[bass.ds(L, 1)].rearrange("l p n -> (l p) n")


        a_h0, a_h1, a_h2, a_h3, a_dA0, a_dA1, a_Cb0, a_Cb1 = (
            t[:, :, :].rearrange("p a b -> p (a b)") for t in (*h, *dA, *Cb))

        def carve(area, *widths):
            at, got = 0, []
            for w in widths:
                got.append(area[:, at:at + w])
                at += w
            assert at <= area.shape[1], (at, area.shape)
            return got

        def fold(ap, a):
            return ap.rearrange("p (a b) -> p a b", a=a)

        xcF, rsF = a_h2[:, 0:TOK], a_h3[:, 0:TOK]
        xt_, rT = carve(a_Cb0, TOK, TOK)
        xt = fold(xt_, NT)
        mW1, mWa, mWb, mHa, mHb, mBias, mB1 = carve(a_Cb1, FF, FF, FF, FC * S, FC * S, B, FC)
        mWcat, mH = [fold(mWa, FC), fold(mWb, FC)], [fold(mHa, FC), fold(mHb, FC)]
        gw, lg_, io_, oh1_, oh2_, tmp_, m1, m2, i1, w1_, w2_, dn = carve(
            a_dA1, NE, NT * NE, NE, NT * NE, NT * NE, NT * NE, NT, NT, NT, NT, NT, NT)
        lg, oh1, oh2, tmp = (fold(t, NT) for t in (lg_, oh1_, oh2_, tmp_))
        ex = []
        for area in (a_h0, a_h1):
            a0, a1, ao = carve(area, FF, FF, FF)
            ex.append((a0, a1, fold(ao, FC)))
        sil = carve(a_h1[:, 3 * FF:], 512, 512)
        inter = [fold(t, FC) for t in carve(a_h2, FC * 512, FC * 512)]
        x2T, at_ = carve(a_h3, TOK, TOK)
        pm_, pMa, pMb, pPa, pPb, pcnt, pone, pcb, pmx, psm, prc = carve(
            a_dA0, 3 * PAIR, PAIR, PAIR, PAIR, PAIR, 3 * 2, 3 * B, 2 * B, 4, 4, 4)
        pm = pm_.rearrange("p (k j l) -> p k j l", k=3, j=2)
        pM, pPT = [fold(pMa, 2), fold(pMb, 2)], [fold(pPa, 2), fold(pPb, 2)]
        Sall = a_h2[:, 0:TOK]
        pSa, pSb, cW1, cv, cb1, cid = carve(a_dA1[:, 1024:1728], S, S, 32, P, 1, B)
        pStage = [fold(pSa, 2), fold(pSb, 2)]
        pT = a_dA1[:, 2048:4096]
        Wk, Wv, Wq, Wo_ = carve(a_h0, HD, HD, HD, 8 * P)
        Wo = fold(Wo_, 8)
        Wd, latT, V_, ssum, sinv, smx = carve(a_h1, P, S, 2 * HD, 2 * NH, 2 * NH, 2 * NH)
        V = fold(V_, 2)
        qT, kT = (fold(t, 8) for t in carve(a_h2, 8 * S, 8 * S))
        Pr = carve(a_h3, *[TRI] * 4)
        PT = carve(a_dA0, *[TRI] * 4)
        sums, inv, negm = (t.rearrange("p (a b) -> p a b", a=2) for t in (ssum, sinv, smx))
        y_, yT_ = carve(a_Cb1, 2 * HD, 8 * S)
        y, yT = fold(y_, 2), fold(yT_, 8)
        idb, cmask = (t.bitcast(BF16) for t in carve(a_dA1[:, 1728:], P // 2, P // 2))
        cmraw = a_dA1[:, 1728 + P:1728 + 2 * P]
        f1raw, f2raw, f1q_, f2q_, fcwa, fcwb, fcba, fcbb = carve(
            xs[:, :], FF, FF, FF // 2, FF // 2, P, P, P, P)
        f1q, f2q, fcw, fcb = f1q_.bitcast(BF16), fold(f2q_.bitcast(BF16), FC), [fcwa, fcwb], [fcba, fcbb]
        fsc = yz[:].rearrange("p a b c -> p (a b c)")
        (fsm,) = carve(fsc, 16)
        fst = [fold(fsc[:, 64 + k * S:64 + (k + 1) * S], 2) for k in range(2)]
        fx3T = [u[:, k, 0:S] for k in range(2)]
        fc = [fold(u[:, k, S:2 * S], 2) for k in range(2)]
        ft = [fold(dt[:, k, 0:S], 2) for k in range(2)]
        fq = [fold(dt[:, k, S:S + S // 2].bitcast(BF16), 2) for k in range(2)]
        fqT = [dt[:, k, S + S // 2:2 * S].bitcast(BF16) for k in range(2)]
        fg = [fold(t, 2) for t in carve(a_h2, 2 * FF, 2 * FF)]
        ft2 = [fold(t, 2) for t in carve(a_h3, 2 * FF, 2 * FF)]
        fq2 = [fold(t.bitcast(BF16), 2) for t in carve(a_dA0, FF, FF)]
        fq2T = [t.bitcast(BF16).rearrange("p (t c k) -> p t c k", t=2, c=FC) for t in carve(a_dA0[:, 2 * FF:], FF, FF)]
        fo = [fold(t, 2) for t in carve(a_Cb1, S, S)]
        fr = fold(fsm[:, 0:8], 4)

        def bank(k, n=512):
            return banks[:, k, 0:n]

        DONE_R = ("res", SLOTS + NPAIR)

        class Chain:
            def __init__(self, e, name, base=0):
                self.e, self.name, self.base, self.k = e, name, base, 0

            def __call__(self, ins):
                self.k += 1
                ins.then_inc(sem(self.name), 1)

            def sync(self):
                self.e.wait_ge(sem(self.name), self.base + self.k)

        def tail_sync(e):
            e.wait_ge(sem(DONE_R[0]), DONE_R[1])

            def dma(dst, src, name):
                e.dma_start(dst, src).then_inc(sem(name), 16)

            dma(ids[:], io["itok_B_0_7"].rearrange("(a b) -> a b", a=1), "ids_in")
            dma(mW1, io["L0_cond2_W1"], "mw_in")
            dma(mB1, io["b1c"], "mw_in")
            for k in range(2):
                dma(mWcat[k][:, :, 0:MC], io["L0_cond2_W2"].rearrange("(c p) o -> p c o", p=P), "mw_in")
            dma(mBias[0:MC, :], bass.AP(io["L0_cond2_b2"].tensor, 0, [[1, MC], [0, B], [1, 1]]), "mw_in")
            e.wait_ge(sem("ids_in"), 16)
            with e.Fori(0, B // 2) as j:
                for q in range(2):
                    b = j * 2 + q
                    sid = e.value_load(ids[0:1, bass.ds(b, 1)], min_val=0, max_val=NE - 1)
                    e.wait_ge(sem("rT"), b + 7)
                    dma(mWcat[q][:, :, MC:P],
                        io["L0_cond2_We"][bass.ds(sid, 1)].rearrange("a (c p) o -> p (a c) o", p=P), f"we{q}")
                    dma(mBias[MC:P, bass.ds(b, 1)],
                        io["L0_cond2_be"][bass.ds(sid, 1)].rearrange("a o -> o a"), f"we{q}")
            dma(gw, io["L0_ffn_gate_kernel"], "gw_in")
            dma(io_, bass.AP(io["iota8"].tensor, 0, [[0, P], [1, NE]]), "gw_in")

            def expert(x, k):
                a0, a1, ao = ex[k]
                dma(a0, layer_of(io["L0_ffn_w0"], x), f"ex{k}")
                dma(a1, layer_of(io["L0_ffn_w1"], x), f"ex{k}")
                dma(ao, io["L0_ffn_wo"][bass.ds(x, 1)].rearrange("a (c p) o -> p (a c) o", p=P), f"ex{k}")

            expert(0, 0)
            expert(1, 1)
            with e.Fori(1, NE // 2) as j:
                for k in range(2):
                    e.wait_ge(sem("mo_dn"), 8 * j - 4 + 4 * k)
                    expert(j * 2 + k, k)
            e.wait_ge(sem("mo_acc"), 4 * NE * 4)
            dma(pm_, io["pmask"], "pc_in")
            dma(pcnt, io["pcnt"], "pc_in")
            dma(cW1, io["L1_cond_W1"], "pc_in")
            dma(cb1[0:32, :], io["L1_cond_b1"].rearrange("(p a) -> p a", a=1), "pc_in")
            dma(cv[0:32, :], bass.AP(io["L1_cond_v"].tensor, 0, [[1, 32], [0, P], [1, 1]]), "pc_in")
            dma(cid.bitcast(I32), bass.AP(io["itok_B_0_2"].tensor, 0, [[0, P], [1, B]]), "pc_in")
            dma(cmraw, io["cmask"], "pc_in")
            dma(Wk, io["L1_attn_w_kv_up"][:, 0:HD], "aw_in")
            dma(Wv, io["L1_attn_w_kv_up"][:, HD:2 * HD], "aw_in")
            dma(Wq, io["L1_attn_w_q"], "aw_in")
            dma(Wo, io["L1_attn_w_out"].rearrange("(c p) o -> p c o", p=P), "aw_in")
            dma(Wd, io["L1_attn_w_kv_down"], "aw_in")
            e.sem_inc(sem("out"), 32)
            dma(f1raw, io["f1t"], "fw_in")
            dma(f2raw, io["f2t"], "fw_in")

            def conditioned(b, q):
                sid = e.value_load(ids[0:1, bass.ds(b, 1)], min_val=0, max_val=NE - 1)
                e.wait_ge(sem("f_c"), b + 7)
                dma(fcw[q], layer_of(io["cw"], sid), f"cw{q}")
                dma(fcb[q], bass.AP(io["L1_cond2_bias"].tensor, sid * P, [[0, P], [1, P]]), f"cw{q}")

            def result(b, q):
                e.wait_ge(sem("f_o"), 2 * b + 6)
                dma(out_tok[:, bass.ds(b * 2, 2), :], fo[q], "out")

            conditioned(0, 0)
            conditioned(1, 1)
            with e.Fori(0, B // 2 - 1) as j:
                for q in range(2):
                    result(j * 2 + q, q)
                    conditioned(j * 2 + 2 + q, q)
            result(B - 2, 0)
            result(B - 1, 1)
            e.wait_ge(sem("out"), 16 * B + 32)

        def tail_gpsimd(e):
            e.wait_ge(sem("mo_acc"), 4 * NE * 4)
            with e.Fori(0, B // 2) as j:
                for q in range(2):
                    b = j * 2 + q
                    e.wait_ge(sem("pT"), b + 7)
                    e.tensor_copy(pStage[q], xt[:, bass.ds(b * 2, 2), :]).then_inc(sem("pst"), 1)
            with e.Fori(0, B // 2) as j:
                for q in range(2):
                    b = j * 2 + q
                    e.wait_ge(sem("x3"), 2 * b + 4)
                    e.wait_ge(sem("f_o"), 2 * b + 2)
                    e.tensor_copy(fst[q], xt[:, bass.ds(b * 2, 2), :]).then_inc(sem("fst"), 1)

        def tail_tensor(e):
            e.wait_ge(sem(DONE_R[0]), DONE_R[1])
            for k in range(4):
                e.matmul(bank(k), mean_w[:], xs[:, k * 512:(k + 1) * 512], start=True, stop=True
                         ).then_inc(sem("fm"), 1)
            for k in range(4):
                e.wait_ge(sem("fsq"), k + 1)
                e.matmul(bank(4 + k), mean_w[:], rsF[:, k * 512:(k + 1) * 512], start=True, stop=True
                         ).then_inc(sem("fv"), 1)
            e.wait_ge(sem("x1"), 3)
            for k in range(4):
                for j in range(4):
                    c = (4 * k + j) * P
                    m = e.transpose(bank(k)[:, j * P:(j + 1) * P], xs[:, c:c + P], ident[:])
                m.then_inc(sem("x1t_ps"), 1)

            def up(b, q):
                wait(e, sem("gelu"), 4 * b - 4)
                for c in range(FC):
                    m = e.matmul(fold(banks[:, 2 * q + c // 2, :], 2)[:, c % 2, :], mW1[:, c * P:(c + 1) * P],
                                 xs[:, bass.ds(b * S, S)], start=True, stop=True)
                m.then_inc(sem("up"), 1)

            def down(b, j, q):
                e.wait_ge(sem("gelu"), 4 * b + 4)
                e.wait_ge(sem(f"we{q}"), 32 * j + 32)
                e.wait_ge(sem("rT"), b + 7)
                for c in range(FC):
                    m = e.matmul(bank(4 + q, S), mWcat[q][:, c, :], mH[q][:, c, :], start=(c == 0), stop=(c == 3))
                m.then_inc(sem("dn"), 1)

            e.wait_ge(sem("mw_in"), 80)
            e.wait_ge(sem("x1t"), 4)
            up(0, 0)
            with e.Fori(0, B // 2 - 1) as j:
                up(j * 2 + 1, 1)
                down(j * 2, j, 0)
                up(j * 2 + 2, 0)
                down(j * 2 + 1, j, 1)
            up(B - 1, 1)
            down(B - 2, B // 2 - 1, 0)
            down(B - 1, B // 2 - 1, 1)

            e.wait_ge(sem("rT"), 8 + B)
            e.wait_ge(sem("gw_in"), 32)
            for t in range(NT):
                m = e.matmul(bank(6)[:, t * NE:(t + 1) * NE], rT[:, t * P:(t + 1) * P], gw, start=True, stop=True)
            m.then_inc(sem("lg_ps"), 1)

            def ex_up(G, g, k):
                for c in range(FC):
                    X = G * 4 + c
                    wait(e, sem("mo_int"), X - 1)
                    for w in range(2):
                        m = e.matmul(bank(2 * (c % 2) + w), ex[k][w][:, c * P:(c + 1) * P],
                                     rT[:, g * 512:(g + 1) * 512], start=True, stop=True)
                    m.then_inc(sem("mo_up"), 1)

            def ex_down(G, g, k):
                e.wait_ge(sem("mo_int"), 4 * G + 4)
                wait(e, sem("mo_acc"), 4 * G - 4)
                for j in range(4):
                    for c in range(FC):
                        m = e.matmul(bank(6 + g % 2)[:, j * P:(j + 1) * P], inter[g % 2][:, c, j * P:(j + 1) * P],
                                     ex[k][2][:, c, :], start=(c == 0), stop=(c == 3))
                m.then_inc(sem("mo_dn"), 1)

            def ex_body(j, first):
                for k in range(2):
                    e.wait_ge(sem(f"ex{k}"), 48 * j + 48)
                    for g in range(4):
                        G = j * 8 + k * 4 + g
                        ex_up(G, g, k)
                        if not (first and k == 0 and g == 0):
                            ex_down(G - 1, (g - 1) % 4, k if g else 1 - k)

            e.wait_ge(sem("lg"), 1)
            ex_body(0, True)
            with e.Fori(1, NE // 2) as j:
                ex_body(j, False)
            ex_down(4 * NE - 1, 3, 1)

            e.wait_ge(sem("mo_acc"), 4 * NE * 4)
            for k in range(4):
                for j in range(4):
                    m = e.transpose(bank(k)[:, j * P:(j + 1) * P], xt[:, 4 * k + j, :], ident[:])
                m.then_inc(sem("x2T_ps"), 1)
            e.wait_ge(sem("pc_in"), 112)
            for k in range(4):
                e.wait_ge(sem("x2T"), k + 1)
                e.matmul(bank(4 + k)[0:32, :], cW1, x2T[:, k * 512:(k + 1) * 512], start=True, stop=True
                         ).then_inc(sem("at_ps"), 1)
            for k in range(4):
                e.wait_ge(sem("at"), k + 1)
                e.matmul(bank(k), cv[0:32, :], at_[0:32, k * 512:(k + 1) * 512], start=True, stop=True
                         ).then_inc(sem("S_ps"), 1)
            e.wait_ge(sem("Sall"), 4)
            with e.Fori(0, B // 2) as j:
                for q in range(2):
                    b = j * 2 + q
                    e.wait_ge(sem("pP"), b + 1)
                    e.wait_ge(sem("pPT"), b + 7)
                    for jc in range(2):
                        for lc in range(2):
                            m = e.transpose(bank(q)[:, lc * S + jc * P:lc * S + (jc + 1) * P],
                                            pM[q][:, jc, lc * P:(lc + 1) * P], ident[:])
                    m.then_inc(sem("pPT_ps"), 1)
                    e.wait_ge(sem("pPT"), b + 9)
                    e.wait_ge(sem("pst"), b + 1)
                    e.wait_ge(sem("pT"), b + 7)
                    for lc in range(2):
                        m = e.matmul(bank(2 + q, S), pStage[q][:, lc, :], pPT[q][:, lc, :],
                                     start=(lc == 0), stop=(lc == 1))
                    m.then_inc(sem("pT_ps"), 1)

            e.wait_ge(sem("pT"), 8 + B)
            e.wait_ge(sem("aw_in"), 80)
            e.wait_ge(sem("acon"), 2)

            def qk_bank(dst, w, rhs, c):
                for i in range(2):
                    m = e.matmul(fold(banks[:, dst, :], 2)[:, i, :], w[:, (c + i) * P:(c + i + 1) * P], rhs,
                                 start=True, stop=True)
                return m

            def scores(b, hp):
                wait(e, sem("P"), (16 * b + 2 * hp - 2) if hp >= 2 else 0)
                for hh in range(2):
                    bk, r = 2 * (hp % 2) + hh, hh * HS
                    out_, c = bank(bk), hp
                    for jc in range(2):
                        lo, n = (0, P) if jc == 0 else (P, 2 * P)
                        e.matmul(out_[:, lo:lo + n], qT[r:r + HS, c, jc * P:(jc + 1) * P], kT[r:r + HS, c, 0:n],
                                 start=(jc == 0), stop=False, skip_group_check=True)
                        m = e.matmul(out_[:, 2 * jc * P:(2 * jc + 1) * P], idb, cmask,
                                     start=False, stop=(jc == 1), skip_group_check=True)
                m.then_inc(sem("S2_ps"), 1)

            def turn(b, hd):
                e.wait_ge(sem("P"), 16 * b + hd + 1)
                if hd >= 2:
                    e.wait_ge(sem("PT"), 16 * b + hd - 1)
                for k in range(3):
                    m = e.transpose(bank(4 + hd % 2)[:, k * P:(k + 1) * P], Pr[hd % 4][:, k * P:(k + 1) * P], ident[:])
                m.then_inc(sem("PT_ps"), 1)

            def values(b, hp):
                if hp == 4:
                    e.wait_ge(sem("att_y"), 4 * b + 2)
                for hd in (2 * hp, 2 * hp + 1):
                    e.wait_ge(sem("PT"), 16 * b + hd + 1)
                    c = (hd % 8) * HS
                    pt, v = PT[hd % 4], hd * HS
                    e.matmul(bank(6)[:, c:c + HS], pt[:, 0:P], V[:, 0, v:v + HS], start=True, stop=True)
                    e.matmul(bank(7)[:, c:c + HS], pt[:, P:2 * P], V[:, 0, v:v + HS], start=True, stop=False)
                    m = e.matmul(bank(7)[:, c:c + HS], pt[:, 2 * P:3 * P], V[:, 1, v:v + HS], start=False, stop=True)
                m.then_inc(sem("av"), 1)

            with e.Fori(0, B) as b:
                x_b = pT[:, bass.ds(b * S, S)]
                e.matmul(bank(0, S), Wd, x_b, start=True, stop=True).then_inc(sem("lat_ps"), 1)
                for c in range(4):
                    qk_bank(1 + c, Wq, x_b, 2 * c).then_inc(sem("q_ps"), 1)
                e.wait_ge(sem("lat"), b + 1)
                for c in range(4):
                    if c == 1:
                        e.wait_ge(sem("x3"), 2 * b + 2)
                    qk_bank((5, 6, 7, 0)[c], Wk, latT, 2 * c).then_inc(sem("k_ps"), 1)
                for c in range(4):
                    e.wait_ge(sem("q_sb"), 4 * b + c + 1)
                    e.matmul(bank(1 + c), latT[:, (c // 2) * P:(c // 2 + 1) * P], Wv[:, (c % 2) * 512:(c % 2 + 1) * 512],
                             start=True, stop=True).then_inc(sem("v_ps"), 1)
                e.wait_ge(sem("k_sb"), 4 * b + 4)
                e.wait_ge(sem("v_sb"), 4 * b + 4)
                for hp in range(8):
                    scores(b, hp)
                    if hp >= 1:
                        turn(b, 2 * hp - 2)
                        turn(b, 2 * hp - 1)
                    if hp >= 2:
                        values(b, hp - 2)
                turn(b, 14)
                turn(b, 15)
                values(b, 6)
                values(b, 7)
                e.wait_ge(sem("att_y"), 4 * b + 4)
                for c in range(4):
                    if c >= 2:
                        e.wait_ge(sem("yT"), 4 * b + c - 1)
                    for i in range(2):
                        for jc in range(2):
                            at = 2 * c + i
                            m = e.transpose(bank(4 + c % 2)[:, i * S + jc * P:i * S + (jc + 1) * P],
                                            y[:, jc, at * P:(at + 1) * P], ident[:])
                    m.then_inc(sem("yT_ps"), 1)
                e.wait_ge(sem("yT"), 4 * b + 4)
                for jc in range(2):
                    for c in range(8):
                        m = e.matmul(bank(6 + jc, P), yT[:, c, jc * P:(jc + 1) * P], Wo[:, c, :],
                                     start=(c == 0), stop=(c == 7))
                m.then_inc(sem("o2"), 1)

            e.wait_ge(sem("x3"), 2 * B + 2)
            e.wait_ge(sem("fwa"), 2)
            e.matmul(bank(6, 2), mean_w[:], fsm[:, 8:10], start=True, stop=True).then_inc(sem("fws_ps"), 1)
            e.wait_ge(sem("fwq"), 9)
            with e.Fori(0, B // 2) as j:
                for q in range(2):
                    b = j * 2 + q
                    e.wait_ge(sem("fst"), b + 1)
                    for t in range(2):
                        m = e.transpose(bank(0)[:, t * P:(t + 1) * P], fst[q][:, t, :], ident[:])
                    m.then_inc(sem("fx_ps"), 1)
                    e.wait_ge(sem("fx"), b + 1)
                    e.wait_ge(sem(f"cw{q}"), 32 * j + 32)
                    for t in range(2):
                        m = e.matmul(bank(1)[:, t * P:(t + 1) * P], fx3T[q][:, t * P:(t + 1) * P], fcw[q],
                                     start=True, stop=True)
                    m.then_inc(sem("fc_ps"), 1)
                    e.wait_ge(sem("f_q"), b + 1)
                    for t in range(2):
                        m = e.transpose(bank(2).bitcast(BF16)[:, t * P:(t + 1) * P], fq[q][:, t, :], idb)
                    m.then_inc(sem("fqT_ps"), 1)
                    e.wait_ge(sem("fqT"), b + 1)
                    for t in range(2):
                        m = e.matmul(bank(3 + t), fqT[q][:, t * P:(t + 1) * P], f1q, start=True, stop=True)
                    m.then_inc(sem("fu_ps"), 1)
                    e.wait_ge(sem("f_q2"), b + 1)
                    for t in range(2):
                        for c in range(FC):
                            k = t * FC + c
                            m = e.transpose(bank(5).bitcast(BF16)[:, k * P:(k + 1) * P],
                                            fq2[q][:, t, c * P:(c + 1) * P], idb)
                    m.then_inc(sem("fq2T_ps"), 1)
                    e.wait_ge(sem("fq2T"), b + 1)
                    for t in range(2):
                        for c in range(FC):
                            m = e.matmul(bank(6)[:, t * P:(t + 1) * P], fq2T[q][:, t, c, :], f2q[:, c, :],
                                         start=(c == 0), stop=(c == 3))
                    m.then_inc(sem("fd_ps"), 1)
                    e.wait_ge(sem("f_o"), 2 * b + 6)

        def tail_scalar(e):
            for k in range(4):
                e.wait_ge(sem("fxc"), k + 1)
                e.activation(rsF[:, k * 512:(k + 1) * 512], xcF[:, k * 512:(k + 1) * 512], ACT.Square
                             ).then_inc(sem("fsq"), 1)
            e.wait_ge(sem("fv"), 4)
            e.activation(fold(rsF, 4), banks[:, 4:8, :], ACT.Ln, bias=eps[:, 0:1]).then_inc(sem("frs"), 1)
            e.wait_ge(sem("frs"), 1)
            e.activation(rsF, rsF, ACT.Exp, scale=-0.5).then_inc(sem("frs"), 1)
            for k in range(4):
                e.wait_ge(sem("x1t_ps"), k + 1)
                e.activation(xt_[:, k * 512:(k + 1) * 512], bank(k), ACT.Copy).then_inc(sem("x1t"), 1)

            def gelu(b, q):
                e.wait_ge(sem("up"), b + 1)
                wait(e, sem("dn"), b - 1)
                for c in range(FC):
                    e.activation(mH[q][:, c, :], fold(banks[:, 2 * q + c // 2, :], 2)[:, c % 2, :], ACT.Gelu,
                                 bias=mB1[:, c:c + 1]).then_inc(sem("gelu"), 1)

            e.wait_ge(sem("mw_in"), 80)
            gelu(0, 0)
            gelu(1, 1)
            with e.Fori(1, B // 2) as j:
                gelu(j * 2, 0)
                gelu(j * 2 + 1, 1)
            e.wait_ge(sem("rt"), RT_DIFF)
            e.activation(w2_, dn, ACT.Exp).then_inc(sem("rexp"), 1)

            def silu(G, first):
                for c in range(FC):
                    X = G * 4 + c
                    e.wait_ge(sem("mo_up"), X + 1)
                    if not (first and c < 2):
                        e.wait_ge(sem("mo_int"), X - 1)
                    e.activation(sil[c % 2], bank(2 * (c % 2)), ACT.Silu).then_inc(sem("mo_sil"), 1)

            silu(0, True)
            with e.Fori(1, 4 * NE) as G:
                silu(G, False)

            for k in range(4):
                e.wait_ge(sem("x2T_ps"), k + 1)
                e.activation(x2T[:, k * 512:(k + 1) * 512], bank(k), ACT.Copy).then_inc(sem("x2T"), 1)
            for k in range(4):
                e.wait_ge(sem("at_ps"), k + 1)
                e.activation(at_[0:32, k * 512:(k + 1) * 512], bank(4 + k)[0:32, :], ACT.Tanh, bias=cb1[0:32, :]
                             ).then_inc(sem("at"), 1)
            for k in range(4):
                e.wait_ge(sem("S_ps"), k + 1)
                e.activation(Sall[:, k * 512:(k + 1) * 512], bank(k), ACT.Copy).then_inc(sem("Sall"), 1)
            e.sem_inc(sem("pPT"), 8)
            with e.Fori(0, B // 2) as j:
                for q in range(2):
                    b = j * 2 + q
                    e.wait_ge(sem("pmx"), b + 1)
                    for jc in range(2):
                        e.activation(pM[q][:, jc, :], pM[q][:, jc, :], ACT.Exp, bias=pmx[:, 2 * q + jc:2 * q + jc + 1],
                                     accum_out=psm[:, 2 * q + jc:2 * q + jc + 1]).then_inc(sem("pexp"), 1)
                    e.wait_ge(sem("pPT_ps"), b + 1)
                    e.wait_ge(sem("pT"), b + 7)
                    e.activation(pPT[q], fold(bank(q), 2), ACT.Copy).then_inc(sem("pPT"), 1)

            with e.Fori(0, B) as b:
                e.wait_ge(sem("lat_ps"), b + 1)
                e.activation(latT, bank(0, S), ACT.Copy).then_inc(sem("lat"), 1)
                for c in range(4):
                    e.wait_ge(sem("q_ps"), 4 * b + c + 1)
                    e.activation(qT[:, 2 * c:2 * c + 2, :], fold(bank(1 + c), 2), ACT.Copy).then_inc(sem("q_sb"), 1)
                for c in range(4):
                    e.wait_ge(sem("v_ps"), 4 * b + c + 1)
                    e.activation(V[:, c // 2, (c % 2) * 512:(c % 2 + 1) * 512], bank(1 + c), ACT.Copy
                                 ).then_inc(sem("v_sb"), 1)
                for hp in range(8):
                    e.wait_ge(sem("negm"), 8 * b + hp + 1)
                    for hh in range(2):
                        hd = 2 * hp + hh
                        if hd >= 4:
                            e.wait_ge(sem("PT_ps"), 16 * b + hd - 3)
                        for jc in range(2):
                            lo, n = (0, P) if jc == 0 else (P, 2 * P)
                            m = e.activation(Pr[hd % 4][:, lo:lo + n], bank(2 * (hp % 2) + hh)[:, lo:lo + n], ACT.Exp,
                                             bias=negm[:, jc, hd:hd + 1], scale=SCALE,
                                             accum_out=sums[:, jc, hd:hd + 1])
                        m.then_inc(sem("P"), 1)

            with e.Fori(0, B // 2) as j:
                for q in range(2):
                    b = j * 2 + q
                    e.wait_ge(sem("fx_ps"), b + 1)
                    e.activation(fx3T[q], bank(0, S), ACT.Copy).then_inc(sem("fx"), 1)
                    e.wait_ge(sem("fqT_ps"), b + 1)
                    e.activation(fqT[q], bank(2).bitcast(BF16)[:, 0:S], ACT.Copy).then_inc(sem("fqT"), 1)
                    e.wait_ge(sem("fu_ps"), b + 1)
                    for t in range(2):
                        e.activation(fg[q][:, t, :], bank(3 + t), ACT.Gelu, scale=fr[:, 1, t:t + 1]
                                     ).then_inc(sem("f_g"), 1)

        def tail_vector(e):
            for k in range(4):
                e.wait_ge(sem("fm"), k + 1)
                if k == 0:
                    e.wait_ge(sem(DONE_R[0]), DONE_R[1])
                e.tensor_tensor(xcF[:, k * 512:(k + 1) * 512], xs[:, k * 512:(k + 1) * 512], bank(k), ALU.subtract
                                ).then_inc(sem("fxc"), 1)
            e.wait_ge(sem("frs"), 2)
            e.wait_ge(sem("fxc"), 4)
            e.scalar_tensor_tensor(out=xcF, in0=xcF, scalar=lng[:, 0:1], in1=rsF, op0=ALU.mult, op1=ALU.mult
                                   ).then_inc(sem("x1"), 1)
            e.wait_ge(sem("x1"), 1)
            e.tensor_scalar(xcF, xcF, lnb[:, 0:1], None, ALU.add).then_inc(sem("x1"), 1)
            e.wait_ge(sem("x1"), 2)
            e.tensor_tensor(fold(xs[:, :], B), fold(xcF, B), ypad[:, :, 1:S + 1], ALU.add).then_inc(sem("x1"), 1)
            e.sem_inc(sem("rT"), 8)
            e.wait_ge(sem("mw_in"), 80)
            with e.Fori(0, B // 2) as j:
                for q in range(2):
                    b = j * 2 + q
                    e.wait_ge(sem("dn"), b + 1)
                    e.wait_ge(sem(f"we{q}"), 32 * j + 32)
                    e.tensor_scalar(rT[:, bass.ds(b * S, S)], bank(4 + q, S), mBias[:, bass.ds(b, 1)], None, ALU.add
                                    ).then_inc(sem("rT"), 1)

            r = Chain(e, "rt")

            def each(ap):
                return ap.unsqueeze(2).to_broadcast([P, NT, NE])

            iota = io_.unsqueeze(1).to_broadcast([P, NT, NE])

            def top(m, oh):
                r(e.tensor_reduce(m, lg, AX_X, ALU.max)); r.sync()
                r(e.tensor_tensor(tmp, lg, each(m), ALU.is_equal)); r.sync()
                r(e.scalar_tensor_tensor(out=tmp, in0=tmp, scalar=-100.0, in1=iota, op0=ALU.mult, op1=ALU.add)); r.sync()
                r(e.tensor_reduce(i1, tmp, AX_X, ALU.min)); r.sync()
                r(e.tensor_tensor(oh, tmp, each(i1), ALU.is_equal)); r.sync()

            e.wait_ge(sem("lg_ps"), 1)
            e.tensor_copy(lg, fold(bank(6, NT * NE), NT)).then_inc(sem("lg"), 1)
            e.wait_ge(sem("lg"), 1)
            e.wait_ge(sem("gw_in"), 32)
            top(m1, oh1)
            r(e.scalar_tensor_tensor(out=lg, in0=oh1, scalar=-BIG, in1=lg, op0=ALU.mult, op1=ALU.add)); r.sync()
            top(m2, oh2)
            r(e.tensor_tensor(dn, m2, m1, ALU.subtract)); r.sync()
            e.wait_ge(sem("rexp"), 1)
            r(e.tensor_scalar(dn, w2_, 1.0, None, ALU.add)); r.sync()
            r(e.reciprocal(w1_, dn)); r.sync()
            r(e.tensor_tensor(w2_, w2_, w1_, ALU.mult)); r.sync()
            r(e.tensor_tensor(oh1, oh1, each(w1_), ALU.mult))
            r(e.tensor_tensor(oh2, oh2, each(w2_), ALU.mult)); r.sync()
            r(e.tensor_tensor(oh1, oh1, oh2, ALU.add)); r.sync()
            assert r.k == RT

            def ex_mul(G, g):
                for c in range(FC):
                    e.wait_ge(sem("mo_sil"), G * 4 + c + 1)
                    e.tensor_tensor(inter[g % 2][:, c, :], sil[c % 2], bank(2 * (c % 2) + 1), ALU.mult
                                    ).then_inc(sem("mo_int"), 1)

            def ex_acc(G, g, x):
                e.wait_ge(sem("mo_dn"), G + 1)
                for j in range(4):
                    t = 4 * g + j
                    e.scalar_tensor_tensor(out=xt[:, t, :], in0=bank(6 + g % 2)[:, j * P:(j + 1) * P],
                                           scalar=oh1[:, t, bass.ds(x, 1)], in1=xt[:, t, :], op0=ALU.mult, op1=ALU.add
                                           ).then_inc(sem("mo_acc"), 1)

            def ex_body(j, first):
                for k in range(2):
                    for g in range(4):
                        G = j * 8 + k * 4 + g
                        ex_mul(G, g)
                        if not (first and k == 0 and g == 0):
                            ex_acc(G - 1, (g - 1) % 4, j * 2 + k - (0 if g else 1))

            ex_body(0, True)
            with e.Fori(1, NE // 2) as j:
                ex_body(j, False)
            ex_acc(4 * NE - 1, 3, NE - 1)

            c_ = Chain(e, "pcst")
            e.wait_ge(sem("pc_in"), 112)
            one = fold(pone, 3)
            c_(e.tensor_copy(prc_f, cid.bitcast(I32))); c_.sync()
            c_(e.tensor_scalar(one[:, 0, :], prc_f, 0.0, None, ALU.is_equal))
            c_(e.tensor_scalar(one[:, 1, :], prc_f, 1.0, None, ALU.is_equal)); c_.sync()
            c_(e.tensor_tensor(one[:, 2, :], one[:, 0, :], one[:, 1, :], ALU.add)); c_.sync()
            c_(e.tensor_scalar(one[:, 2, :], one[:, 2, :], -1.0, 1.0, ALU.mult, ALU.add)); c_.sync()
            cnt_b = fold(pcb, B)
            for jc in range(2):
                c_(e.tensor_scalar(cnt_b[:, :, jc], one[:, 0, :], pcnt[:, jc:jc + 1], None, ALU.mult)); c_.sync()
                for k in (1, 2):
                    c_(e.scalar_tensor_tensor(out=cnt_b[:, :, jc], in0=one[:, k, :], scalar=pcnt[:, 2 * k + jc:2 * k + jc + 1],
                                              in1=cnt_b[:, :, jc], op0=ALU.mult, op1=ALU.add)); c_.sync()
            c_(e.tensor_copy(idb, ident[:]))
            c_(e.tensor_copy(cmask, cmraw)); c_.sync()
            e.sem_inc(sem("acon"), 2)
            e.wait_ge(sem("Sall"), 4)
            e.sem_inc(sem("pT"), 8)
            with e.Fori(0, B // 2) as j:
                for q in range(2):
                    b = j * 2 + q
                    m = Chain(e, "pch", b * 7)
                    e.wait_ge(sem("pPT"), b + 7)
                    flat_ = pM[q].rearrange("p a b -> p (a b)")
                    kk = [pm_[:, k * PAIR:(k + 1) * PAIR] for k in range(3)]
                    m(e.tensor_scalar(flat_, kk[0], one[:, 0, bass.ds(b, 1)], None, ALU.mult)); m.sync()
                    for k in (1, 2):
                        m(e.scalar_tensor_tensor(out=flat_, in0=kk[k], scalar=one[:, k, bass.ds(b, 1)], in1=flat_,
                                                 op0=ALU.mult, op1=ALU.add)); m.sync()
                    m(e.tensor_tensor(pM[q], pM[q], Sall[:, bass.ds(b * S, S)].unsqueeze(1).to_broadcast([P, 2, S]),
                                      ALU.add)); m.sync()
                    e.tensor_reduce(pmx[:, 2 * q:2 * q + 2], pM[q], AX_X, ALU.max, negate=True).then_inc(sem("pmx"), 1)
                    e.wait_ge(sem("pexp"), 2 * b + 2)
                    m(e.tensor_tensor(prc[:, 0:2], psm[:, 2 * q:2 * q + 2], cnt_b[:, bass.ds(b, 1), :].rearrange("p a b -> p (a b)"),
                                      ALU.mult)); m.sync()
                    m(e.reciprocal(prc[:, 2:4], prc[:, 0:2])); m.sync()
                    m(e.tensor_tensor(pM[q], pM[q], prc[:, 2:4].unsqueeze(2).to_broadcast([P, 2, S]), ALU.mult)); m.sync()
                    assert m.k == 7
                    e.sem_inc(sem("pP"), 1)
                    e.wait_ge(sem("pT_ps"), b + 1)
                    e.tensor_copy(pT[:, bass.ds(b * S, S)], bank(2 + q, S)).then_inc(sem("pT"), 1)

            e.sem_inc(sem("x3"), 2)
            with e.Fori(0, B) as b:
                for c in range(4):
                    e.wait_ge(sem("k_ps"), 4 * b + c + 1)
                    e.tensor_copy(kT[:, 2 * c:2 * c + 2, :], fold(bank((5, 6, 7, 0)[c]), 2)).then_inc(sem("k_sb"), 1)

                def maxima(hp):
                    e.wait_ge(sem("S2_ps"), 8 * b + hp + 1)
                    lo = 2 * (hp % 2)
                    for jc in range(2):
                        c0, n = (0, P) if jc == 0 else (P, 2 * P)
                        m = e.tensor_reduce(smx2[:, jc, 2 * hp:2 * hp + 2], banks[:, lo:lo + 2, c0:c0 + n], AX_X, ALU.max)
                        m.then_inc(sem("smax"), 1)
                    e.wait_ge(sem("smax"), 16 * b + 2 * hp + 2)
                    e.tensor_scalar(negm[:, :, 2 * hp:2 * hp + 2], smx2[:, :, 2 * hp:2 * hp + 2], -SCALE, None, ALU.mult
                                    ).then_inc(sem("negm"), 1)

                def turned(hd):
                    e.wait_ge(sem("PT_ps"), 16 * b + hd + 1)
                    if hd >= 4:
                        e.wait_ge(sem("av"), 8 * b + hd // 2 - 1)
                    e.tensor_copy(PT[hd % 4], bank(4 + hd % 2, TRI)).then_inc(sem("PT"), 1)

                def finish(half):
                    e.wait_ge(sem("av"), 8 * b + 4 * half + 4)
                    hs = slice(8 * half, 8 * half + 8)
                    e.reciprocal(inv[:, :, hs], sums[:, :, hs]).then_inc(sem("inv"), 1)
                    e.wait_ge(sem("inv"), 2 * b + half + 1)
                    for jc in range(2):
                        e.tensor_tensor(y[:, jc, half * 512:(half + 1) * 512].rearrange("p (h d) -> p h d", h=8),
                                        bank(6 + jc).rearrange("p (h d) -> p h d", h=8),
                                        inv[:, jc, hs].unsqueeze(2).to_broadcast([P, 8, HS]), ALU.mult
                                        ).then_inc(sem("att_y"), 1)

                maxima(0)
                for hp in range(1, 8):
                    maxima(hp)
                    turned(2 * hp - 2)
                    turned(2 * hp - 1)
                    if hp == 6:
                        finish(0)
                turned(14)
                turned(15)
                finish(1)
                for c in range(4):
                    e.wait_ge(sem("yT_ps"), 4 * b + c + 1)
                    e.tensor_copy(yT[:, 2 * c:2 * c + 2, :], fold(bank(4 + c % 2), 2)).then_inc(sem("yT"), 1)
                e.wait_ge(sem("o2"), b + 1)
                for jc in range(2):
                    t = xt[:, bass.ds(b * 2 + jc, 1), :].rearrange("p a b -> p (a b)")
                    e.tensor_tensor(t, t, bank(6 + jc, P), ALU.add).then_inc(sem("x3"), 1)

            w = Chain(e, "fwq")
            e.wait_ge(sem("fw_in"), 32)
            e.tensor_reduce(fsm[:, 8:9], f1raw, AX_X, ALU.add, apply_absolute_value=True).then_inc(sem("fwa"), 1)
            e.tensor_reduce(fsm[:, 9:10], f2raw, AX_X, ALU.add, apply_absolute_value=True).then_inc(sem("fwa"), 1)
            e.wait_ge(sem("fws_ps"), 1)
            w(e.tensor_scalar(fsm[:, 10:12], bank(6, 2), 1.0 / FF, LN_EPS, ALU.mult, ALU.max)); w.sync()
            w(e.reciprocal(fsm[:, 12:14], fsm[:, 10:12])); w.sync()
            for k, (raw, dst) in enumerate(((f1raw, f1q_), (f2raw, f2q_))):
                w(e.tensor_scalar(raw, raw, fsm[:, 12 + k:13 + k], ROUND, ALU.mult, ALU.add)); w.sync()
                w(e.tensor_scalar(raw, raw, -ROUND, -1.0, ALU.add, ALU.max)); w.sync()
                w(e.tensor_scalar(dst.bitcast(BF16), raw, 1.0, None, ALU.min)); w.sync()
            w(e.tensor_scalar(fsm[:, 14:16], fsm[:, 10:12], 1.0 / 127.0, None, ALU.mult)); w.sync()
            e.sem_inc(sem("f_c"), 8)
            e.sem_inc(sem("f_o"), 4)

            def quantise(m, src, tmp_t, dst, row):
                m(e.tensor_reduce(fr[:, 2, :], src, AX_X, ALU.max, apply_absolute_value=True)); m.sync()
                m(e.tensor_scalar(fr[:, 2, :], fr[:, 2, :], LN_EPS, None, ALU.max)); m.sync()
                m(e.reciprocal(fr[:, 3, :], fr[:, 2, :]))
                m(e.tensor_scalar(fr[:, row, :], fr[:, 2, :], fsm[:, 14 + (row != 1):15 + (row != 1)], None, ALU.mult)); m.sync()
                m(e.tensor_scalar(fr[:, 3, :], fr[:, 3, :], 127.0, None, ALU.mult)); m.sync()
                for t in range(2):
                    m(e.tensor_scalar(tmp_t[:, t, :], src[:, t, :], fr[:, 3, t:t + 1], ROUND, ALU.mult, ALU.add))
                m.sync()
                m(e.tensor_scalar(tmp_t, tmp_t, -ROUND, 127.0, ALU.add, ALU.min)); m.sync()
                e.tensor_scalar(dst, tmp_t, -128.0, None, ALU.max).then_inc(sem("f_q" if row == 1 else "f_q2"), 1)

            with e.Fori(0, B // 2) as j:
                for q in range(2):
                    b = j * 2 + q
                    m = Chain(e, "fch", b * 16)
                    e.wait_ge(sem("fc_ps"), b + 1)
                    e.wait_ge(sem(f"cw{q}"), 32 * j + 32)
                    e.tensor_tensor(fc[q], fold(bank(1, S), 2), fcb[q].unsqueeze(1).to_broadcast([P, 2, P]), ALU.add
                                    ).then_inc(sem("f_c"), 1)
                    e.wait_ge(sem("f_c"), b + 9)
                    quantise(m, fc[q], ft[q], fq[q], 1)
                    e.wait_ge(sem("f_g"), 2 * b + 2)
                    quantise(m, fg[q], ft2[q], fq2[q], 0)
                    assert m.k == 16
                    e.wait_ge(sem("fq2T_ps"), b + 1)
                    e.tensor_copy(fq2T[q].rearrange("p t c k -> p (t c k)"), bank(5).bitcast(BF16)).then_inc(sem("fq2T"), 1)
                    e.wait_ge(sem("fd_ps"), b + 1)
                    e.wait_ge(sem("out"), 16 * b + 16)
                    for t in range(2):
                        e.scalar_tensor_tensor(out=fo[q][:, t, :], in0=bank(6)[:, t * P:(t + 1) * P],
                                               scalar=fr[:, 0, t:t + 1], in1=fst[q][:, t, :], op0=ALU.mult, op1=ALU.add
                                               ).then_inc(sem("f_o"), 1)

        block = ctx.enter_context(nc.Block())

        @block.sync
        def _(e):
            e.dma_start(xtok, x_tok).then_inc(sem("x_in"), 16)
            for j, n in enumerate(("condB_zX", "condB_zY", "condB_zR")):
                e.dma_start(zb[:, j, :], bass.AP(io[n].tensor, 0, [[0, P], [1, B]])).then_inc(sem("z_in"), 16)
            e.dma_start(lng[:], io["L0_attn_ln_g"].rearrange("(p a) -> p a", a=1)).then_inc(sem("ln_in"), 16)
            e.dma_start(lnb[:], io["L0_attn_ln_b"].rearrange("(p a) -> p a", a=1)).then_inc(sem("ln_in"), 16)
            e.dma_start(A_all[:].rearrange("p l s -> p (l s)"), io["A_log"]).then_inc(sem("alog_in"), 16)

            def prepare(L):
                e.wait_ge(sem("scr"), 32 * L + 32)
                e.dma_start(raw_in, layer_of(io["in_w"], L)).then_inc(sem("raw"), 16)
                e.dma_start(raw_cw, bass.AP(io["conv_w"].tensor, L * (TAPS * 2 * P), [[0, P], [1, TAPS * 2 * P]])
                            ).then_inc(sem("raw"), 16)
                e.dma_start(bunF[:, FC_Z:FC_CB], layer_of(io["zxp_w"], L)).then_inc(sem("raw"), 16)
                e.dma_start(raw_out, layer_of(io["out_w"], L)).then_inc(sem("raw"), 16)
                e.dma_start(raw_sm, layer_of(io["small"], L)).then_inc(sem("raw"), 16)
                e.wait_ge(sem("bun"), 5 * L + 5)
                e.dma_start(layer_of(scrF, L), bunF).then_inc(sem("scr"), 16)
                e.dma_start(layer_of(scrS, L), bunS).then_inc(sem("scr"), 16)

            def load(L):
                wait(e, sem("dt"), L * (2 * NPAIR))
                wait(e, sem("dt_ps"), L * (2 * NPAIR))
                e.dma_start(wF[:], layer_of(scrF, L)).then_inc(sem("wF"), 16)
                e.dma_start(wdt[BC3:BC3 + RANK, :], layer_of(io["dt_w"], L)).then_inc(sem("wF"), 16)
                wait(e, sem("o_ps"), L * NPAIR)
                e.dma_start(wS[:], layer_of(scrS, L)).then_inc(sem("wS"), 16)

            e.sem_inc(sem("scr"), 32)
            with e.Fori(0, LAYERS) as L:
                prepare(L)
            e.wait_ge(sem("scr"), 32 * LAYERS + 32)
            load(0)
            with e.Fori(1, LAYERS) as L:
                load(L)
            tail_sync(e)

        @block.gpsimd
        def _(e):
            count = [0]

            def const(ins):
                count[0] += 1
                ins.then_inc(sem("const"), 1)
                e.wait_ge(sem("const"), count[0])

            def diagonal(t, value, base, cols):
                const(e.affine_select(out=t, in_=t, compare_op=ALU.not_equal, fill=value, base=base,
                                      pattern=cols, channel_multiplier=1))

            const(e.memset(ident[:], 0.0))
            diagonal(ident[:], 1.0, 0, [[-1, P]])
            const(e.memset(tri, 0.0))
            diagonal(tri, -2.0, 0, [[-1, P]])
            diagonal(tri, 1.0, 1, [[-1, P]])
            diagonal(tri, 1.0, -1, [[-1, P]])
            diagonal(tri[:, 0:1], 2.0, -1, [[0, 1]])
            diagonal(tri[:, P - 1:P], 2.0, 2 - P, [[0, 1]])
            const(e.memset(mean_w[:], 1.0 / P))
            const(e.memset(eps[:], LN_EPS))
            const(e.memset(xn[:, :, 0:TAPS - 1], 0.0))
            for part in range(3):
                if part == 0:
                    const(e.memset(sel[:], 0.0))
                diagonal(sel[:], 1.0, -2 * NS * part, [[-1, 2 * NS], [0, P]])
            assert count[0] == CONSTS
            for half in range(HALVES):
                e.memset(dA[half][:, :, 0:1], 0.0).then_inc(sem("dA0"), 1)

            def slot(p, q):
                for i in range(2):
                    n = 2 * p + i
                    for half in range(HALVES):
                        hb = h[2 * i + half]
                        e.wait_ge(sem("scan"), 2 * n + half + 1)
                        e.wait_ge(sem("C"), 8 * n + 8)
                        e.tensor_tensor(hb[:], hb[:], Cb[i][:], ALU.mult).then_inc(sem("hC"), 1)

            with e.Fori(0, SLOTS) as p:
                slot(p, 0)
            tail_gpsimd(e)

        def cols(t):
            c = (t % NPAIR) * PAIR
            return bass.ds(c, PAIR)

        def pe_mean(e, t, q):
            e.wait_ge(sem("res"), t + 1)
            wait(e, sem("dt"), 2 * t)
            e.matmul(ps_F[0][:], mean_w[:], xs[:, cols(t)], start=True, stop=True).then_inc(sem("mean"), 1)

        def dve_center(e, t, q):
            e.wait_ge(sem("mean"), t + 1)
            e.tensor_tensor(xc[:], xs[:, cols(t)], ps_F[0][:], ALU.subtract).then_inc(sem("xc"), 1)

        def act_square(e, t, q):
            e.wait_ge(sem("xc"), t + 1)
            e.activation(rstd[:], xc[:], ACT.Square).then_inc(sem("sq"), 1)

        def pe_var(e, t, q):
            e.wait_ge(sem("sq"), t + 1)
            e.matmul(ps_F[1][:], mean_w[:], rstd[:], start=True, stop=True).then_inc(sem("var"), 1)

        def act_rstd(e, t, q):
            e.wait_ge(sem("var"), t + 1)
            e.activation(rstd[:], ps_F[1][:], ACT.Ln, bias=eps[:, 0:1]).then_inc(sem("lnv"), 1)
            e.wait_ge(sem("lnv"), t + 1)
            e.activation(rstd[:], rstd[:], ACT.Exp, scale=-0.5).then_inc(sem("rstd"), 1)

        def dve_norm(e, t, q):
            e.wait_ge(sem("rstd"), t + 1)
            e.scalar_tensor_tensor(out=xc[:], in0=xc[:], scalar=lng[:, 0:1], in1=rstd[:],
                                   op0=ALU.mult, op1=ALU.mult).then_inc(sem("xg"), 1)
            e.wait_ge(sem("xg"), t + 1)
            e.tensor_scalar(xn[:, :, TAPS - 1:], xc[:].rearrange("p (b l) -> p b l", b=2), lnb[:, 0:1], None,
                            ALU.add).then_inc(sem("xn"), 1)

        def pe_conv(e, t, q):
            e.wait_ge(sem("xn"), t + 1)
            e.wait_ge(sem("wF"), 32 * (t // NPAIR) + 32)
            for half in range(HALVES):
                for k in range(TAPS):
                    m = e.matmul(ps_F[half][:].rearrange("p (b l) -> p b l", b=2),
                                 wF[:, FC_TAP + k * 2 * P + half * P:FC_TAP + k * 2 * P + (half + 1) * P],
                                 xn[:, :, k:k + S], start=(k == 0), stop=(k == TAPS - 1))
                m.then_inc(sem("conv"), 1)

        def dve_xh(e, t, q):
            for half in range(HALVES):
                e.wait_ge(sem("conv"), 2 * t + half + 1)
                e.tensor_scalar(xh[:, half, :], ps_F[half][:], wF[:, FC_CB + half:FC_CB + half + 1], None,
                                ALU.add).then_inc(sem("xh"), 1)

        def act_th(e, t, q):
            e.wait_ge(sem("xh"), 2 * t + 2)
            e.activation(th[:], xh[:], ACT.Tanh).then_inc(sem("th"), 1)

        def dve_xm(e, t, q):
            e.wait_ge(sem("th"), t + 1)
            e.scalar_tensor_tensor(out=xm[q][:], in0=th[:], scalar=1.0, in1=xh[:],
                                   op0=ALU.add, op1=ALU.mult).then_inc(sem("xm"), 1)

        def pe_z(e, t, q):
            for half in range(HALVES):
                e.wait_ge(sem("xh"), 2 * t + half + 1)
                c = FC_Z + half * P
                e.matmul(ps_F[half][:].rearrange("p (b l) -> p b l", b=2), wF[:, c:c + P],
                         xn[:, :, TAPS - 1:], start=True, stop=True).then_inc(sem("z_ps"), 1)

        def act_zt(e, t, q):
            e.wait_ge(sem("xm"), t + 1)
            for half in range(HALVES):
                e.wait_ge(sem("z_ps"), 2 * t + half + 1)
                e.activation(th[:, half, :], ps_F[half][:], ACT.Tanh, scale=0.5).then_inc(sem("zt"), 1)

        def dve_zs(e, t, q):
            for half in range(HALVES):
                e.wait_ge(sem("zt"), 2 * t + half + 1)
                e.scalar_tensor_tensor(out=zs[q][:, half, :], in0=th[:, half, :], scalar=1.0,
                                       in1=ps_F[half][:], op0=ALU.add, op1=ALU.mult).then_inc(sem("zs"), 1)

        def pe_xproj(e, t, q):
            e.wait_ge(sem("zs"), 2 * t + 1)
            e.wait_ge(sem("xm"), t + 1)
            for half in range(HALVES):
                c = FC_XP + half * XPN
                m = e.matmul(ps_F[0][0:XPN, :], wF[:, c:c + XPN], xm[q][:, half, :],
                             start=(half == 0), stop=(half == 1))
            m.then_inc(sem("xd"), 1)

        def dve_split(e, t, q):
            e.wait_ge(sem("xd"), t + 1)
            m = 2 * NS
            e.tensor_copy(bc[q][:, :], ps_F[0][0:BC3, :]).then_inc(sem("split"), 1)
            e.tensor_copy(dt8, ps_F[0][BC3:XPN, :]).then_inc(sem("split"), 1)
            e.wait_ge(sem("split"), 5 * t + 1)
            e.tensor_tensor(r1, ps_F[0][0:BC3, :], bc[q][:, :], ALU.subtract).then_inc(sem("split"), 1)
            e.wait_ge(sem("split"), 5 * t + 3)
            e.tensor_copy(r2[2 * m:BC3, :], r1[2 * m:BC3, :]).then_inc(sem("split"), 1)
            e.tensor_copy(bc[q][m:2 * m, :], r1[m:2 * m, :]).then_inc(sem("split"), 1)
            e.wait_ge(sem("split"), 5 * t + 4)
            e.tensor_tensor(bc[q][2 * m:BC3, :], r1[2 * m:BC3, :], r2[2 * m:BC3, :],
                            ALU.subtract).then_inc(sem("bc"), 1)

        def pe_dt(e, t, q):
            for half in range(HALVES):
                if half == 0:
                    e.wait_ge(sem("split"), 5 * t + 2)
                    e.wait_ge(sem("zs"), 2 * t + 2)
                    e.wait_ge(sem("res"), t - 1 + NPAIR)
                else:
                    e.wait_ge(sem("bc"), t + 1)
                e.matmul(ps_F[1 - half][:], wdt[BC3:BC3 + RANK, half * P:(half + 1) * P], dt8,
                         start=True, stop=True).then_inc(sem("dt_ps"), 1)

        def dve_amin(e, t, q):
            for half in range(HALVES):
                e.wait_ge(sem("dt_ps"), 2 * t + half + 1)
                e.tensor_scalar(xh[:, half, :], ps_F[1 - half][:], wF[:, FC_DTB + half:FC_DTB + half + 1], 40.0,
                                ALU.add, ALU.min).then_inc(sem("amin"), 1)

        def act_softplus(e, t, q):
            e.wait_ge(sem("amin"), 2 * t + 2)
            e.activation(xh[:], xh[:], ACT.Exp).then_inc(sem("sp"), 1)
            e.wait_ge(sem("sp"), 2 * t + 1)
            e.activation(xh[:], xh[:], ACT.Ln, bias=1.0).then_inc(sem("sp"), 1)

        def dve_dt(e, t, q):
            e.wait_ge(sem("sp"), 2 * t + 2)
            for half in range(HALVES):
                e.scalar_tensor_tensor(out=dt[:, half, :], in0=ps_F[1 - half][:],
                                       scalar=wF[:, FC_DTB + half:FC_DTB + half + 1], in1=xh[:, half, :],
                                       op0=ALU.add, op1=ALU.max).then_inc(sem("dt"), 1)
            e.wait_ge(sem("dt"), 2 * t + 2)
            e.tensor_tensor(u[:], dt[:], xm[q][:], ALU.mult).then_inc(sem("u"), 1)

        def pe_B(e, p, q, i):
            n = 2 * p + i
            if i == 0:
                e.wait_ge(sem("bc"), p + 1)
            for g in range(4):
                wait(e, sem("mul"), 8 * n + 2 * g - 2)
                for j in range(4):
                    m = e.matmul(ps_B[g % 2][:, j, :], sel[:, 4 * g + j, :], bc[q][:, i * S:(i + 1) * S],
                                 start=True, stop=True)
                m.then_inc(sem("B"), 1)

        def pe_C(e, p, q, i, lo, hi):
            n = 2 * p + i
            for c in range(lo, hi):
                wait(e, sem("C"), 8 * n + c)
                for j in range(2):
                    m = e.matmul(ps_C[:, j, :], sel[:, NS + 2 * c + j, :], bc[q][:, i * S:(i + 1) * S],
                                 start=True, stop=True)
                m.then_inc(sem("C_ps"), 1)

        def act_C(e, p, q, i, lo, hi):
            n = 2 * p + i
            wait(e, sem("hC"), 2 * n - 2)
            for c in range(lo, hi):
                e.wait_ge(sem("C_ps"), 8 * n + c + 1)
                e.activation(Cb[i][:, 2 * c:2 * c + 2, :], ps_C, ACT.Copy).then_inc(sem("C"), 1)

        def act_dA(e, p, q, i, half):
            n = 2 * p + i
            if i == 0 and half == 0:
                wait(e, sem("dA"), 4 * p)
                e.activation(A_cur[q][:], A_all[:, bass.ds(p // NPAIR, 1), :].rearrange("p l s -> p (l s)"),
                             ACT.Copy).then_inc(sem("A_cur"), 1)
                e.wait_ge(sem("A_cur"), p + 1)
                e.wait_ge(sem("dt"), 2 * p + 2)
            wait(e, sem("scan"), 2 * n + half - 1)
            if isinstance(p, int) and p == 0:
                e.wait_ge(sem("dA0"), 2)
            for s in range(NS):
                m = e.activation(dA[half][:, s, 1:S], dt[:, half, i * S + 1:(i + 1) * S], ACT.Exp,
                                 scale=A_cur[q][:, half * NS + s:half * NS + s + 1])
            m.then_inc(sem("dA"), 1)

        def dve_mul(e, p, q, i, g):
            n = 2 * p + i
            e.wait_ge(sem("B"), 4 * n + g + 1)
            if g == 0:
                e.wait_ge(sem("u"), p + 1)
                if isinstance(p, int) and p == 0:
                    e.wait_ge(sem("scr"), 32 * LAYERS + 32)
            for half in range(HALVES):
                e.tensor_tensor(h[2 * i + half][:, 4 * g:4 * g + 4, :], ps_B[g % 2],
                                u[:, half, i * S:(i + 1) * S].unsqueeze(1).to_broadcast([P, 4, S]),
                                ALU.mult).then_inc(sem("mul"), 1)

        def dve_scan(e, p, q, i, half):
            n = 2 * p + i
            e.wait_ge(sem("dA"), 2 * n + half + 1)
            e.wait_ge(sem("mul"), 8 * n + 8)
            hb = h[2 * i + half][:, :, :].rearrange("p s l -> p (s l)")
            e.tensor_tensor_scan(hb, dA[half][:, :, :].rearrange("p s l -> p (s l)"), hb, 0.0,
                                 ALU.mult, ALU.add).then_inc(sem("scan"), 1)

        def pe_sum(e, p, q, i, half):
            n = 2 * p + i
            e.wait_ge(sem("hC"), 2 * n + half + 1)
            if half == 0:
                wait(e, sem("gate"), n)
            if i == 0 and half == 0:
                e.wait_ge(sem("wS"), 16 * (p // NPAIR) + 16)
            for s in range(NS):
                e.matmul(ps_Y[:, half, :], ident[:], h[2 * i + half][:, s, :], start=(s == 0), stop=False)
            e.matmul(ps_Y[:, half, :], wS[:, SC_D + half * P:SC_D + (half + 1) * P],
                     xm[q][:, half, i * S:(i + 1) * S], start=False, stop=True).then_inc(sem("y"), 1)

        def dve_gate(e, p, q, i):
            n = 2 * p + i
            e.wait_ge(sem("y"), 2 * n + 2)
            e.tensor_tensor(yz[:, :, i, :], ps_Y, zs[q][:, :, i * S:(i + 1) * S],
                            ALU.mult).then_inc(sem("gate"), 1)

        def pe_out(e, p, q):
            e.wait_ge(sem("gate"), 2 * p + 2)
            if isinstance(p, int) and p >= SLOTS - 2:
                e.wait_ge(sem("dt"), 2 * SLOTS)
                wait(e, sem("res"), p + NPAIR)
            else:
                e.wait_ge(sem("zs"), 2 * p + 6)
            for half in range(HALVES):
                m = e.matmul(ps_F[1][:], wS[:, SC_OUT + half * P:SC_OUT + (half + 1) * P],
                             yz[:, half, :, :].rearrange("p i l -> p (i l)"), start=(half == 0), stop=(half == 1))
            m.then_inc(sem("o_ps"), 1)

        def dve_res(e, p, q):
            e.wait_ge(sem("o_ps"), p + 1)
            e.tensor_tensor(xs[:, cols(p)], xs[:, cols(p)], ps_F[1][:], ALU.add).then_inc(sem("res"), 1)
            e.wait_ge(sem("res"), p + 1 + NPAIR)

        def pe_slot(e, p, q, prev, nxt):
            r = 1 - q
            for i in range(2):
                if nxt and i == 0:
                    pe_mean(e, p + 1, r)
                pe_B(e, p, q, i)
                if i == 0:
                    if nxt:
                        pe_var(e, p + 1, r)
                    pe_C(e, p, q, i, 0, 8)
                    if nxt:
                        pe_conv(e, p + 1, r)
                    if prev:
                        pe_sum(e, p - 1, r, 1, 0)
                    if nxt:
                        pe_z(e, p + 1, r)
                    if prev:
                        pe_sum(e, p - 1, r, 1, 1)
                else:
                    if prev:
                        pe_out(e, p - 1, r)
                    if nxt:
                        pe_xproj(e, p + 1, r)
                    pe_C(e, p, q, i, 0, 8)
                    if nxt:
                        pe_dt(e, p + 1, r)
                    pe_sum(e, p, q, 0, 0)
                    pe_sum(e, p, q, 0, 1)

        def act_slot(e, p, q, prev, nxt):
            r = 1 - q
            for i in range(2):
                if nxt and i == 1:
                    act_zt(e, p + 1, r)
                act_dA(e, p, q, i, 0)
                if nxt and i == 0:
                    act_square(e, p + 1, r)
                act_C(e, p, q, i, 0, 4)
                if nxt and i == 0:
                    act_rstd(e, p + 1, r)
                act_dA(e, p, q, i, 1)
                act_C(e, p, q, i, 4, 8)
                if nxt and i == 0:
                    act_th(e, p + 1, r)
                if nxt and i == 1:
                    act_softplus(e, p + 1, r)

        def dve_slot(e, p, q, prev, nxt):
            r = 1 - q
            for i in range(2):
                dve_mul(e, p, q, i, 0)
                if nxt:
                    (dve_center, dve_zs)[i](e, p + 1, r)
                dve_mul(e, p, q, i, 1)
                dve_mul(e, p, q, i, 2)
                if i == 1 and nxt:
                    dve_split(e, p + 1, r)
                dve_mul(e, p, q, i, 3)
                if i == 0 and nxt:
                    dve_norm(e, p + 1, r)
                if i == 1 and prev:
                    dve_res(e, p - 1, r)
                dve_scan(e, p, q, i, 0)
                if nxt:
                    (dve_xh, dve_amin)[i](e, p + 1, r)
                dve_scan(e, p, q, i, 1)
                if i == 0:
                    if prev:
                        dve_gate(e, p - 1, r, 1)
                    if nxt:
                        dve_xm(e, p + 1, r)
                else:
                    dve_gate(e, p, q, 0)
                    if nxt:
                        dve_dt(e, p + 1, r)

        def slots(e, slot):
            slot(e, 0, 0, False, True)
            with e.Fori(0, (SLOTS - 2) // 2) as j:
                slot(e, j * 2 + 1, 1, True, True)
                slot(e, j * 2 + 2, 0, True, True)
            slot(e, SLOTS - 1, 1, True, False)

        LAST, LQ = SLOTS - 1, 1

        @block.tensor
        def _(e):
            e.wait_ge(sem("x_in"), 16)
            e.wait_ge(sem("const"), CONSTS)
            for k in range(4):
                wait(e, sem("xT"), k - 1)
                for j in range(4):
                    m = e.transpose(ps_F[k % 2][:, j * P:(j + 1) * P], xtok[:, 4 * k + j, :], ident[:])
                m.then_inc(sem("xT_ps"), 1)
            for k in range(4):
                e.wait_ge(sem("xT"), 4 if k < 2 else 4)
                wait(e, sem("lapx"), k - 1)
                e.matmul(ps_F[k % 2][:].rearrange("p (b l) -> p b l", b=2), tri,
                         ypad[:, 2 * k:2 * k + 2, 1:S + 1], start=True, stop=True).then_inc(sem("lapx_ps"), 1)
            pe_mean(e, 0, 0)
            pe_var(e, 0, 0)
            pe_conv(e, 0, 0)
            pe_z(e, 0, 0)
            pe_xproj(e, 0, 0)
            pe_dt(e, 0, 0)
            slots(e, pe_slot)
            pe_sum(e, LAST, LQ, 1, 0)
            pe_sum(e, LAST, LQ, 1, 1)
            pe_out(e, LAST, LQ)
            tail_tensor(e)

        @block.scalar
        def _(e):
            for k in range(4):
                e.wait_ge(sem("xT_ps"), k + 1)
                e.activation(ypad[:, 2 * k:2 * k + 2, 1:S + 1], ps_F[k % 2][:].rearrange("p (b l) -> p b l", b=2),
                             ACT.Copy).then_inc(sem("xT"), 1)
            for k in range(4):
                e.wait_ge(sem("lapx_ps"), k + 1)
                e.activation(lapx[:, 2 * k:2 * k + 2, :], ps_F[k % 2][:].rearrange("p (b l) -> p b l", b=2),
                             ACT.Copy).then_inc(sem("lapx"), 1)
            e.wait_ge(sem("alog_in"), 16)
            e.activation(A_all[:], A_all[:], ACT.Exp).then_inc(sem("A"), 1)
            e.wait_ge(sem("A"), 1)
            e.activation(A_all[:], A_all[:], ACT.Copy, scale=-1.0).then_inc(sem("A"), 1)
            e.wait_ge(sem("A"), 2)
            act_square(e, 0, 0)
            act_rstd(e, 0, 0)
            act_th(e, 0, 0)
            act_zt(e, 0, 0)
            act_softplus(e, 0, 0)
            slots(e, act_slot)
            tail_scalar(e)

        @block.vector
        def _(e):
            y = ypad[:, :, 1:S + 1]
            count = [0]

            def du(ins):
                count[0] += 1
                ins.then_inc(sem("du"), 1)
                e.wait_ge(sem("du"), count[0])

            def per_batch(j):
                return zb[:, j, :].unsqueeze(2).to_broadcast([P, B, S])

            xs3 = xs[:].rearrange("p (b l) -> p b l", b=B)
            e.wait_ge(sem("xT"), 4)
            du(e.tensor_copy(ypad[:, :, 0:1], ypad[:, :, 2:3]))
            du(e.tensor_copy(ypad[:, :, S + 1:S + 2], ypad[:, :, S - 1:S]))
            du(e.tensor_tensor(lapy, ypad[:, :, 0:S], ypad[:, :, 2:S + 2], ALU.add))
            du(e.scalar_tensor_tensor(out=lapy, in0=y, scalar=-2.0, in1=lapy, op0=ALU.mult, op1=ALU.add))
            e.wait_ge(sem("z_in"), 48)
            du(e.tensor_tensor(lapy, lapy, per_batch(1), ALU.mult))
            du(e.tensor_scalar(grow, y, -1.0, 1.0, ALU.mult, ALU.add))
            du(e.tensor_tensor(grow, grow, y, ALU.mult))
            du(e.tensor_tensor(grow, grow, per_batch(2), ALU.mult))
            du(e.tensor_tensor(grow, grow, lapy, ALU.add))
            e.wait_ge(sem("lapx"), 4)
            du(e.tensor_tensor(lapx, lapx, per_batch(0), ALU.mult))
            du(e.tensor_tensor(xs3, lapx, grow, ALU.add))
            e.sem_inc(sem("res"), NPAIR)
            e.wait_ge(sem("const"), CONSTS)
            with e.Fori(0, LAYERS) as L:
                e.wait_ge(sem("raw"), 80 * L + 80)
                e.scalar_tensor_tensor(out=bunF[:, 0:FC_Z].rearrange("p (k e) -> p k e", k=TAPS),
                                       in0=raw_in.unsqueeze(1).to_broadcast([P, TAPS, 2 * P]), scalar=0.5,
                                       in1=raw_cw.rearrange("p (k e) -> p k e", k=TAPS),
                                       op0=ALU.mult, op1=ALU.mult).then_inc(sem("bun"), 1)
                e.tensor_scalar(bunF[:, FC_CB:FC_END], raw_sm[:, 0:HALVES], 0.5, None, ALU.mult
                                ).then_inc(sem("bun"), 1)
                for half in range(HALVES):
                    e.tensor_scalar(bunS[:, SC_D + half * P:SC_D + (half + 1) * P], ident[:],
                                    raw_sm[:, HALVES + half:HALVES + half + 1], None, ALU.mult
                                    ).then_inc(sem("bun"), 1)
                e.tensor_scalar(bunS[:, SC_OUT:SC_END], raw_out, 0.5, None, ALU.mult).then_inc(sem("bun"), 1)
            e.wait_ge(sem("ln_in"), 32)
            dve_center(e, 0, 0)
            dve_norm(e, 0, 0)
            dve_xh(e, 0, 0)
            dve_xm(e, 0, 0)
            dve_zs(e, 0, 0)
            dve_split(e, 0, 0)
            dve_amin(e, 0, 0)
            dve_dt(e, 0, 0)
            slots(e, dve_slot)
            dve_gate(e, LAST, LQ, 1)
            dve_res(e, LAST, LQ)
            tail_vector(e)


CONSTS = 15

def laid_out(a):
    import numpy as np

    def halves_first(w):
        n = w.shape[2]
        return w.reshape(LAYERS, HALVES, P, n).transpose(0, 2, 1, 3).reshape(LAYERS, P, HALVES * n)

    in_t = a["L0_attn_in_proj_w"].transpose(0, 2, 1)
    xp = a["L0_attn_x_proj_w"].transpose(0, 2, 1)
    xp = np.concatenate([xp[:, :, RANK:]] * 3 + [xp[:, :, :RANK]], axis=2)
    col = lambda n: a[n].reshape(LAYERS, HALVES, P).transpose(0, 2, 1)
    return {
        "in_w": in_t[:, :, :2 * P],
        "conv_w": a["L0_attn_conv_w"].transpose(0, 2, 1),
        "zxp_w": np.concatenate([in_t[:, :, 2 * P:], halves_first(xp), col("L0_attn_dt_proj_b")], axis=2),
        "out_w": halves_first(a["L0_attn_out_proj_w"].transpose(0, 2, 1)),
        "small": np.concatenate([col("L0_attn_conv_b"), col("L0_attn_D_skip")], axis=2),
        "dt_w": a["L0_attn_dt_proj_w"].transpose(0, 2, 1),
        "b1c": a["L0_cond2_b1"].reshape(FC, P).T,
        "cw": a["L1_cond2_weight"].transpose(0, 2, 1),
        "f1t": a["L1_ffn_w1"].T,
        "f2t": a["L1_ffn_w2"].T.reshape(FC, P, P).transpose(1, 0, 2).reshape(P, FF),
        "A_log": a["L0_attn_A_log"].reshape(LAYERS, HALVES, P, NS).transpose(2, 0, 1, 3).reshape(P, -1),
    }


def constants():
    import numpy as np
    j, l = np.arange(S)[:, None], np.arange(S)[None, :]
    keep = np.stack([l <= j, l >= j, l != j])
    by_part = keep.reshape(3, 2, P, S).transpose(2, 0, 1, 3)
    return {
        "iota8": (100 + np.arange(NE)).astype(np.float32),
        "pmask": np.where(by_part, 0, -BIG).astype(np.float32).reshape(P, -1),
        "pcnt": by_part.sum(-1).astype(np.float32).reshape(P, -1),
        "cmask": np.where(np.arange(P)[None, :] <= np.arange(P)[:, None], 0, -BIG).astype(np.float32),
    }


SAME = ["x", "condB_zX", "condB_zY", "condB_zR", "itok_B_0_7", "itok_B_0_2", "L0_attn_ln_g", "L0_attn_ln_b",
        "L0_cond2_W1", "L0_cond2_W2", "L0_cond2_b2", "L0_cond2_We", "L0_cond2_be", "L0_ffn_gate_kernel",
        "L0_ffn_w0", "L0_ffn_w1", "L0_ffn_wo", "L1_cond_W1", "L1_cond_b1", "L1_cond_v", "L1_attn_w_kv_down",
        "L1_attn_w_kv_up", "L1_attn_w_q", "L1_attn_w_out", "L1_cond2_bias"]


def kernel(**inputs):
    import numpy as np
    import concourse.bacc as bacc
    from concourse.bass_utils import run_bass_kernel_spmd

    nc = bacc.Bacc("TRN2", target_bir_lowering=False, num_devices=1)
    given = {n: np.asarray(v) for n, v in inputs.items()}
    arrays = {n: np.ascontiguousarray(v) for n, v in {**{n: given[n] for n in SAME}, **laid_out(given), **constants()}.items()}
    io = {n: nc.dram_tensor(f"in_{n}", v.shape, mybir.dt.from_np(v.dtype), kind="ExternalInput").ap()
          for n, v in arrays.items()}
    io["out"] = nc.dram_tensor("out_x", (B, S, D), F32, kind="ExternalOutput").ap()
    program(nc, io)
    r = run_bass_kernel_spmd(nc, [{f"in_{n}": v for n, v in arrays.items()}], core_ids=[0])
    return r.results[0]["out_x"]
```

```python
from contextlib import ExitStack

import concourse.bass as bass
from concourse import mybir

F32 = mybir.dt.float32
BF16 = mybir.dt.bfloat16
I32 = mybir.dt.int32
U32 = mybir.dt.uint32
ALU = mybir.AluOpType
ACT = mybir.ActivationFunctionType
AX_X = mybir.AxisListType.X

P = 128
B, S, D = 8, 256, 128
TOK = B * S
NT = TOK // P
HALVES = 2
NS = 16
RANK = 8
TAPS = 4
LAYERS = 4
PAIR = 2 * S
NPAIR = B // 2
SLOTS = LAYERS * NPAIR
LN_EPS = 1e-5
BIG = 1.0e30
FF = 512
FC = FF // P
NE = 8
MC = 96
NH, HS = 16, 64
HD = NH * HS
SCALE = HS ** -0.5
TRI = 3 * P
ROUND = 1.5 * 2 ** 23
RT, RT_DIFF = 18, 12

XPN = 3 * 2 * NS + RANK
BC3 = 3 * 2 * NS
FC_TAP = 0
FC_Z = TAPS * 2 * P
FC_XP = FC_Z + 2 * P
FC_DTB = FC_XP + HALVES * XPN
FC_CB = FC_DTB + HALVES
FC_END = FC_CB + HALVES
SC_D = 0
SC_OUT = HALVES * P
SC_END = SC_OUT + HALVES * P


def wait(eng, sem, value):
    if isinstance(value, int) and value <= 0:
        return
    eng.wait_ge(sem, value)


def program(nc, io, stop_after=None):
    with ExitStack() as ctx:
        def sb(name, shape, dt=F32):
            return ctx.enter_context(nc.sbuf_tensor(name, shape, dt))

        def pb(name, shape, dt=F32):
            return ctx.enter_context(nc.psum_tensor(name, shape, dt))

        sems = {}

        def sem(name):
            if name not in sems:
                sems[name] = ctx.enter_context(nc.semaphore(name))
            return sems[name]

        banks = pb("banks", [P, 8, 512])
        ps_B = [banks[:, 2 * i:2 * i + 2, :].rearrange("p a (b l) -> p (a b) l", b=2) for i in range(2)]
        ps_C = banks[:, 4, :].rearrange("p (a l) -> p a l", a=2)
        ps_Y = banks[:, 5, :].rearrange("p (a l) -> p a l", a=2)
        ps_F = [banks[:, 6 + i, :] for i in range(2)]

        ident = sb("ident", [P, P])
        mean_w = sb("mean_w", [P, P])
        center_w = sb("center_w", [P, P])
        ypad = sb("ypad", [P, B, S + 2])
        xs = sb("xs", [P, TOK])

        zb = sb("zb", [P, 3, B])
        lng = sb("lng", [P, 1])
        lnb = sb("lnb", [P, 1])
        eps = sb("eps", [P, 1])
        sel = sb("sel", [BC3, 2 * NS, P], BF16)
        h = [sb(f"h{i}", [P, NS, S]) for i in range(4)]
        dA = [sb(f"dA{i}", [P, NS, S]) for i in range(2)]
        Cb = [sb(f"Cb{i}", [P, NS, S]) for i in range(2)]
        wF = sb("wF", [P, FC_END])
        wS = sb("wS", [P, SC_END])
        wdt = sb("wdt", [P, HALVES * P])
        A_all = sb("A_all", [P, LAYERS, HALVES * NS])
        A_cur = [sb(f"A_cur{i}", [P, HALVES * NS]) for i in range(2)]
        xm = [sb(f"xm{i}", [P, HALVES, PAIR]) for i in range(2)]
        zs = [sb(f"zs{i}", [P, HALVES, PAIR]) for i in range(2)]
        dt = sb("dt", [P, HALVES, PAIR])
        u = sb("u", [P, HALVES, PAIR])
        bc = [sb(f"bc{i}", [BC3, PAIR], BF16) for i in range(2)]
        xc = sb("xc", [P, PAIR])
        rstd = sb("rstd", [P, PAIR])
        xn = sb("xn", [P, 2, S + TAPS - 1])
        xh = sb("xh", [P, HALVES, PAIR])
        th = sb("th", [P, HALVES, PAIR])
        yz = sb("yz", [P, HALVES, 2, S])
        ids = sb("ids", [1, B], I32)
        smx2 = sb("smx2", [P, 2, NH])
        prc_f = smx2[:, 0, 0:B]
        r1 = xc[0:BC3, :]
        r2 = th[0:BC3, 0, 0:PAIR // 2].bitcast(BF16)
        tri = Cb[0][:, 0, 0:P]
        dt8 = rstd[BC3:BC3 + RANK, :]

        flat = [t[:, :, :].rearrange("p a b -> p (a b)") for t in (*h, *dA)]
        raw_in, raw_cw = flat[0][:, 0:2 * P], flat[0][:, 2 * P:2 * P + TAPS * 2 * P]
        o = 2 * P + TAPS * 2 * P
        raw_out, raw_sm = flat[0][:, o:o + HALVES * P], flat[0][:, o + HALVES * P:o + HALVES * P + 2 * HALVES]
        bunF, bunS = flat[1][:, 0:FC_END], flat[1][:, FC_END:FC_END + SC_END]
        xtok = flat[2][:, 0:TOK].rearrange("p (a b) -> p a b", a=NT)
        lapx = flat[3][:, 0:TOK].rearrange("p (a b) -> p a b", a=B)
        lapy = flat[3][:, TOK:2 * TOK].rearrange("p (a b) -> p a b", a=B)
        grow = flat[2][:, TOK:2 * TOK].rearrange("p (a b) -> p a b", a=B)
        scrF = nc.dram_tensor("scrF", [LAYERS, P, FC_END], F32).ap()
        scrS = nc.dram_tensor("scrS", [LAYERS, P, SC_END], F32).ap()

        out_tok = io["out"].rearrange("b (c p) f -> p (b c) f", p=P)
        x_tok = io["x"].rearrange("b (c p) f -> p (b c) f", p=P)

        def layer_of(ap, L):
            return ap[bass.ds(L, 1)].rearrange("l p n -> (l p) n")


        a_h0, a_h1, a_h2, a_h3, a_dA0, a_dA1, a_Cb0, a_Cb1 = (
            t[:, :, :].rearrange("p a b -> p (a b)") for t in (*h, *dA, *Cb))

        def carve(area, *widths):
            at, got = 0, []
            for w in widths:
                got.append(area[:, at:at + w])
                at += w
            assert at <= area.shape[1], (at, area.shape)
            return got

        def fold(ap, a):
            return ap.rearrange("p (a b) -> p a b", a=a)

        xcF, rsF = a_h2[:, 0:TOK], a_h3[:, 0:TOK]
        xt_, rT = carve(a_Cb0, TOK, TOK)
        xt = fold(xt_, NT)
        mW1, mWa, mWb, mHa, mHb, mBias, mB1 = carve(a_Cb1, FF, FF, FF, FC * S, FC * S, B, FC)
        mWcat, mH = [fold(mWa, FC), fold(mWb, FC)], [fold(mHa, FC), fold(mHb, FC)]
        gw, lg_, io_, oh1_, oh2_, tmp_, m1, m2, i1, w1_, w2_, dn = carve(
            a_dA1, NE, NT * NE, NE, NT * NE, NT * NE, NT * NE, NT, NT, NT, NT, NT, NT)
        lg, oh1, oh2, tmp = (fold(t, NT) for t in (lg_, oh1_, oh2_, tmp_))
        ex = []
        for area in (a_h0, a_h1):
            a0, a1, ao = carve(area, FF, FF, FF)
            ex.append((a0, a1, fold(ao, FC)))
        sil = carve(a_h1[:, 3 * FF:], 512, 512)
        inter = [fold(t, FC) for t in carve(a_h2, FC * 512, FC * 512)]
        x2T, at_ = carve(a_h3, TOK, TOK)
        pm_, pMa, pMb, pPa, pPb, pcnt, pone, pcb, pmx, psm, prc = carve(
            a_dA0, 3 * PAIR, PAIR, PAIR, PAIR, PAIR, 3 * 2, 3 * B, 2 * B, 4, 4, 4)
        pm = pm_.rearrange("p (k j l) -> p k j l", k=3, j=2)
        pM, pPT = [fold(pMa, 2), fold(pMb, 2)], [fold(pPa, 2), fold(pPb, 2)]
        Sall = a_h2[:, 0:TOK]
        pSa, pSb, cW1, cv, cb1, cid = carve(a_dA1[:, 1024:1728], S, S, 32, P, 1, B)
        pStage = [fold(pSa, 2), fold(pSb, 2)]
        pT = a_dA1[:, 2048:4096]
        Wk, Wv, Wq, Wo_ = carve(a_h0, HD, HD, HD, 8 * P)
        Wo = fold(Wo_, 8)
        Wd, latT, V_, ssum, sinv, smx = carve(a_h1, P, S, 2 * HD, 2 * NH, 2 * NH, 2 * NH)
        V = fold(V_, 2)
        qT, kT = (fold(t, 8) for t in carve(a_h2, 8 * S, 8 * S))
        Pr = carve(a_h3, *[TRI] * 4)
        PT = carve(a_dA0, *[TRI] * 4)
        sums, inv, negm = (t.rearrange("p (a b) -> p a b", a=2) for t in (ssum, sinv, smx))
        y_, yT_ = carve(a_Cb1, 2 * HD, 8 * S)
        y, yT = fold(y_, 2), fold(yT_, 8)
        idb, cmask = (t.bitcast(BF16) for t in carve(a_dA1[:, 1728:], P // 2, P // 2))
        cmraw = a_dA1[:, 1728 + P:1728 + 2 * P]
        f1raw, f2raw, f1q_, f2q_, fcwa, fcwb, fcba, fcbb = carve(
            xs[:, :], FF, FF, FF // 2, FF // 2, P, P, P, P)
        f1q, f2q, fcw, fcb = f1q_.bitcast(BF16), fold(f2q_.bitcast(BF16), FC), [fcwa, fcwb], [fcba, fcbb]
        fsc = yz[:].rearrange("p a b c -> p (a b c)")
        (fsm,) = carve(fsc, 16)
        fst = [fold(fsc[:, 64 + k * S:64 + (k + 1) * S], 2) for k in range(2)]
        fx3T = [u[:, k, 0:S] for k in range(2)]
        fc = [fold(u[:, k, S:2 * S], 2) for k in range(2)]
        ft = [fold(dt[:, k, 0:S], 2) for k in range(2)]
        fq = [fold(dt[:, k, S:S + S // 2].bitcast(BF16), 2) for k in range(2)]
        fqT = [dt[:, k, S + S // 2:2 * S].bitcast(BF16) for k in range(2)]
        fg = [fold(t, 2) for t in carve(a_h2, 2 * FF, 2 * FF)]
        ft2 = [fold(t, 2) for t in carve(a_h3, 2 * FF, 2 * FF)]
        fq2 = [fold(t.bitcast(BF16), 2) for t in carve(a_dA0, FF, FF)]
        fq2T = [t.bitcast(BF16).rearrange("p (t c k) -> p t c k", t=2, c=FC) for t in carve(a_dA0[:, 2 * FF:], FF, FF)]
        fo = [fold(t, 2) for t in carve(a_Cb1, S, S)]
        fr = fold(fsm[:, 0:8], 4)

        def bank(k, n=512):
            return banks[:, k, 0:n]

        DONE_R = ("res", SLOTS + NPAIR)

        class Chain:
            def __init__(self, e, name, base=0):
                self.e, self.name, self.base, self.k = e, name, base, 0

            def __call__(self, ins):
                self.k += 1
                ins.then_inc(sem(self.name), 1)

            def sync(self):
                self.e.wait_ge(sem(self.name), self.base + self.k)

        def tail_sync(e):
            e.wait_ge(sem(DONE_R[0]), DONE_R[1])

            def dma(dst, src, name):
                e.dma_start(dst, src).then_inc(sem(name), 16)

            dma(ids[:], io["itok_B_0_7"].rearrange("(a b) -> a b", a=1), "ids_in")
            dma(mW1, io["L0_cond2_W1"], "mw_in")
            dma(mB1, io["b1c"], "mw_in")
            for k in range(2):
                dma(mWcat[k][:, :, 0:MC], io["L0_cond2_W2"].rearrange("(c p) o -> p c o", p=P), "mw_in")
            dma(mBias[0:MC, :], bass.AP(io["L0_cond2_b2"].tensor, 0, [[1, MC], [0, B], [1, 1]]), "mw_in")
            e.wait_ge(sem("ids_in"), 16)
            with e.Fori(0, B // 2) as j:
                for q in range(2):
                    b = j * 2 + q
                    sid = e.value_load(ids[0:1, bass.ds(b, 1)], min_val=0, max_val=NE - 1)
                    e.wait_ge(sem("rT"), b + 7)
                    dma(mWcat[q][:, :, MC:P],
                        io["L0_cond2_We"][bass.ds(sid, 1)].rearrange("a (c p) o -> p (a c) o", p=P), f"we{q}")
                    dma(mBias[MC:P, bass.ds(b, 1)],
                        io["L0_cond2_be"][bass.ds(sid, 1)].rearrange("a o -> o a"), f"we{q}")
            dma(gw, io["L0_ffn_gate_kernel"], "gw_in")
            dma(io_, bass.AP(io["iota8"].tensor, 0, [[0, P], [1, NE]]), "gw_in")

            def expert(x, k):
                a0, a1, ao = ex[k]
                dma(a0, layer_of(io["L0_ffn_w0"], x), f"ex{k}")
                dma(a1, layer_of(io["L0_ffn_w1"], x), f"ex{k}")
                dma(ao, io["L0_ffn_wo"][bass.ds(x, 1)].rearrange("a (c p) o -> p (a c) o", p=P), f"ex{k}")

            expert(0, 0)
            expert(1, 1)
            with e.Fori(1, NE // 2) as j:
                for k in range(2):
                    e.wait_ge(sem("mo_dn"), 8 * j - 4 + 4 * k)
                    expert(j * 2 + k, k)
            e.wait_ge(sem("mo_acc"), 4 * NE * 4)
            dma(pm_, io["pmask"], "pc_in")
            dma(pcnt, io["pcnt"], "pc_in")
            dma(cW1, io["L1_cond_W1"], "pc_in")
            dma(cb1[0:32, :], io["L1_cond_b1"].rearrange("(p a) -> p a", a=1), "pc_in")
            dma(cv[0:32, :], bass.AP(io["L1_cond_v"].tensor, 0, [[1, 32], [0, P], [1, 1]]), "pc_in")
            dma(cid.bitcast(I32), bass.AP(io["itok_B_0_2"].tensor, 0, [[0, P], [1, B]]), "pc_in")
            dma(cmraw, io["cmask"], "pc_in")
            dma(Wk, io["L1_attn_w_kv_up"][:, 0:HD], "aw_in")
            dma(Wv, io["L1_attn_w_kv_up"][:, HD:2 * HD], "aw_in")
            dma(Wq, io["L1_attn_w_q"], "aw_in")
            dma(Wo, io["L1_attn_w_out"].rearrange("(c p) o -> p c o", p=P), "aw_in")
            dma(Wd, io["L1_attn_w_kv_down"], "aw_in")
            e.sem_inc(sem("out"), 32)
            dma(f1raw, io["f1t"], "fw_in")
            dma(f2raw, io["f2t"], "fw_in")

            def conditioned(b, q):
                sid = e.value_load(ids[0:1, bass.ds(b, 1)], min_val=0, max_val=NE - 1)
                e.wait_ge(sem("f_c"), b + 7)
                dma(fcw[q], layer_of(io["cw"], sid), f"cw{q}")
                dma(fcb[q], bass.AP(io["L1_cond2_bias"].tensor, sid * P, [[0, P], [1, P]]), f"cw{q}")

            def result(b, q):
                e.wait_ge(sem("f_o"), 2 * b + 6)
                dma(out_tok[:, bass.ds(b * 2, 2), :], fo[q], "out")

            conditioned(0, 0)
            conditioned(1, 1)
            with e.Fori(0, B // 2 - 1) as j:
                for q in range(2):
                    result(j * 2 + q, q)
                    conditioned(j * 2 + 2 + q, q)
            result(B - 2, 0)
            result(B - 1, 1)
            e.wait_ge(sem("out"), 16 * B + 32)

        def tail_gpsimd(e):
            e.wait_ge(sem("mo_acc"), 4 * NE * 4)
            with e.Fori(0, B // 2) as j:
                for q in range(2):
                    b = j * 2 + q
                    e.wait_ge(sem("pT"), b + 7)
                    e.tensor_copy(pStage[q], xt[:, bass.ds(b * 2, 2), :]).then_inc(sem("pst"), 1)
            with e.Fori(0, B // 2) as j:
                for q in range(2):
                    b = j * 2 + q
                    e.wait_ge(sem("x3"), 2 * b + 4)
                    e.wait_ge(sem("f_o"), 2 * b + 2)
                    e.tensor_copy(fst[q], xt[:, bass.ds(b * 2, 2), :]).then_inc(sem("fst"), 1)

        def tail_tensor(e):
            e.wait_ge(sem(DONE_R[0]), DONE_R[1])
            for k in range(4):
                e.matmul(bank(k), mean_w[:], xs[:, k * 512:(k + 1) * 512], start=True, stop=True
                         ).then_inc(sem("fm"), 1)
            for k in range(4):
                e.wait_ge(sem("fsq"), k + 1)
                e.matmul(bank(4 + k), mean_w[:], rsF[:, k * 512:(k + 1) * 512], start=True, stop=True
                         ).then_inc(sem("fv"), 1)
            e.wait_ge(sem("x1"), 3)
            for k in range(4):
                for j in range(4):
                    c = (4 * k + j) * P
                    m = e.transpose(bank(k)[:, j * P:(j + 1) * P], xs[:, c:c + P], ident[:])
                m.then_inc(sem("x1t_ps"), 1)

            def up(b, q):
                wait(e, sem("gelu"), 4 * b - 4)
                for c in range(FC):
                    m = e.matmul(fold(banks[:, 2 * q + c // 2, :], 2)[:, c % 2, :], mW1[:, c * P:(c + 1) * P],
                                 xs[:, bass.ds(b * S, S)], start=True, stop=True)
                m.then_inc(sem("up"), 1)

            def down(b, j, q):
                e.wait_ge(sem("gelu"), 4 * b + 4)
                e.wait_ge(sem(f"we{q}"), 32 * j + 32)
                e.wait_ge(sem("rT"), b + 7)
                for c in range(FC):
                    m = e.matmul(bank(4 + q, S), mWcat[q][:, c, :], mH[q][:, c, :], start=(c == 0), stop=(c == 3))
                m.then_inc(sem("dn"), 1)

            e.wait_ge(sem("mw_in"), 80)
            e.wait_ge(sem("x1t"), 4)
            up(0, 0)
            with e.Fori(0, B // 2 - 1) as j:
                up(j * 2 + 1, 1)
                down(j * 2, j, 0)
                up(j * 2 + 2, 0)
                down(j * 2 + 1, j, 1)
            up(B - 1, 1)
            down(B - 2, B // 2 - 1, 0)
            down(B - 1, B // 2 - 1, 1)

            e.wait_ge(sem("rT"), 8 + B)
            e.wait_ge(sem("gw_in"), 32)
            for t in range(NT):
                m = e.matmul(bank(6)[:, t * NE:(t + 1) * NE], rT[:, t * P:(t + 1) * P], gw, start=True, stop=True)
            m.then_inc(sem("lg_ps"), 1)

            def ex_up(G, g, k):
                for c in range(FC):
                    X = G * 4 + c
                    wait(e, sem("mo_int"), X - 1)
                    for w in range(2):
                        m = e.matmul(bank(2 * (c % 2) + w), ex[k][w][:, c * P:(c + 1) * P],
                                     rT[:, g * 512:(g + 1) * 512], start=True, stop=True)
                    m.then_inc(sem("mo_up"), 1)

            def ex_down(G, g, k):
                e.wait_ge(sem("mo_int"), 4 * G + 4)
                wait(e, sem("mo_acc"), 4 * G - 4)
                for j in range(4):
                    for c in range(FC):
                        m = e.matmul(bank(6 + g % 2)[:, j * P:(j + 1) * P], inter[g % 2][:, c, j * P:(j + 1) * P],
                                     ex[k][2][:, c, :], start=(c == 0), stop=(c == 3))
                m.then_inc(sem("mo_dn"), 1)

            def ex_body(j, first):
                for k in range(2):
                    e.wait_ge(sem(f"ex{k}"), 48 * j + 48)
                    for g in range(4):
                        G = j * 8 + k * 4 + g
                        ex_up(G, g, k)
                        if not (first and k == 0 and g == 0):
                            ex_down(G - 1, (g - 1) % 4, k if g else 1 - k)

            e.wait_ge(sem("lg"), 1)
            ex_body(0, True)
            with e.Fori(1, NE // 2) as j:
                ex_body(j, False)
            ex_down(4 * NE - 1, 3, 1)

            e.wait_ge(sem("mo_acc"), 4 * NE * 4)
            for k in range(4):
                for j in range(4):
                    m = e.transpose(bank(k)[:, j * P:(j + 1) * P], xt[:, 4 * k + j, :], ident[:])
                m.then_inc(sem("x2T_ps"), 1)
            e.wait_ge(sem("pc_in"), 112)
            for k in range(4):
                e.wait_ge(sem("x2T"), k + 1)
                e.matmul(bank(4 + k)[0:32, :], cW1, x2T[:, k * 512:(k + 1) * 512], start=True, stop=True
                         ).then_inc(sem("at_ps"), 1)
            for k in range(4):
                e.wait_ge(sem("at"), k + 1)
                e.matmul(bank(k), cv[0:32, :], at_[0:32, k * 512:(k + 1) * 512], start=True, stop=True
                         ).then_inc(sem("S_ps"), 1)
            e.wait_ge(sem("Sall"), 4)
            with e.Fori(0, B // 2) as j:
                for q in range(2):
                    b = j * 2 + q
                    e.wait_ge(sem("pP"), b + 1)
                    e.wait_ge(sem("pPT"), b + 7)
                    for jc in range(2):
                        for lc in range(2):
                            m = e.transpose(bank(q)[:, lc * S + jc * P:lc * S + (jc + 1) * P],
                                            pM[q][:, jc, lc * P:(lc + 1) * P], ident[:])
                    m.then_inc(sem("pPT_ps"), 1)
                    e.wait_ge(sem("pPT"), b + 9)
                    e.wait_ge(sem("pst"), b + 1)
                    e.wait_ge(sem("pT"), b + 7)
                    for lc in range(2):
                        m = e.matmul(bank(2 + q, S), pStage[q][:, lc, :], pPT[q][:, lc, :],
                                     start=(lc == 0), stop=(lc == 1))
                    m.then_inc(sem("pT_ps"), 1)

            e.wait_ge(sem("pT"), 8 + B)
            e.wait_ge(sem("aw_in"), 80)
            e.wait_ge(sem("acon"), 2)

            def qk_bank(dst, w, rhs, c):
                for i in range(2):
                    m = e.matmul(fold(banks[:, dst, :], 2)[:, i, :], w[:, (c + i) * P:(c + i + 1) * P], rhs,
                                 start=True, stop=True)
                return m

            def scores(b, hp):
                wait(e, sem("P"), (16 * b + 2 * hp - 2) if hp >= 2 else 0)
                for hh in range(2):
                    bk, r = 2 * (hp % 2) + hh, hh * HS
                    out_, c = bank(bk), hp
                    for jc in range(2):
                        lo, n = (0, P) if jc == 0 else (P, 2 * P)
                        e.matmul(out_[:, lo:lo + n], qT[r:r + HS, c, jc * P:(jc + 1) * P], kT[r:r + HS, c, 0:n],
                                 start=(jc == 0), stop=False, skip_group_check=True)
                        m = e.matmul(out_[:, 2 * jc * P:(2 * jc + 1) * P], idb, cmask,
                                     start=False, stop=(jc == 1), skip_group_check=True)
                m.then_inc(sem("S2_ps"), 1)

            def turn(b, hd):
                e.wait_ge(sem("P"), 16 * b + hd + 1)
                if hd >= 2:
                    e.wait_ge(sem("PT"), 16 * b + hd - 1)
                for k in range(3):
                    m = e.transpose(bank(4 + hd % 2)[:, k * P:(k + 1) * P], Pr[hd % 4][:, k * P:(k + 1) * P], ident[:])
                m.then_inc(sem("PT_ps"), 1)

            def values(b, hp):
                if hp == 4:
                    e.wait_ge(sem("att_y"), 4 * b + 2)
                for hd in (2 * hp, 2 * hp + 1):
                    e.wait_ge(sem("PT"), 16 * b + hd + 1)
                    c = (hd % 8) * HS
                    pt, v = PT[hd % 4], hd * HS
                    e.matmul(bank(6)[:, c:c + HS], pt[:, 0:P], V[:, 0, v:v + HS], start=True, stop=True)
                    e.matmul(bank(7)[:, c:c + HS], pt[:, P:2 * P], V[:, 0, v:v + HS], start=True, stop=False)
                    m = e.matmul(bank(7)[:, c:c + HS], pt[:, 2 * P:3 * P], V[:, 1, v:v + HS], start=False, stop=True)
                m.then_inc(sem("av"), 1)

            with e.Fori(0, B) as b:
                x_b = pT[:, bass.ds(b * S, S)]
                e.matmul(bank(0, S), Wd, x_b, start=True, stop=True).then_inc(sem("lat_ps"), 1)
                for c in range(4):
                    qk_bank(1 + c, Wq, x_b, 2 * c).then_inc(sem("q_ps"), 1)
                e.wait_ge(sem("lat"), b + 1)
                for c in range(4):
                    if c == 1:
                        e.wait_ge(sem("x3"), 2 * b + 2)
                    qk_bank((5, 6, 7, 0)[c], Wk, latT, 2 * c).then_inc(sem("k_ps"), 1)
                for c in range(4):
                    e.wait_ge(sem("q_sb"), 4 * b + c + 1)
                    e.matmul(bank(1 + c), latT[:, (c // 2) * P:(c // 2 + 1) * P], Wv[:, (c % 2) * 512:(c % 2 + 1) * 512],
                             start=True, stop=True).then_inc(sem("v_ps"), 1)
                e.wait_ge(sem("k_sb"), 4 * b + 4)
                e.wait_ge(sem("v_sb"), 4 * b + 4)
                for hp in range(8):
                    scores(b, hp)
                    if hp >= 1:
                        turn(b, 2 * hp - 2)
                        turn(b, 2 * hp - 1)
                    if hp >= 2:
                        values(b, hp - 2)
                turn(b, 14)
                turn(b, 15)
                values(b, 6)
                values(b, 7)
                e.wait_ge(sem("att_y"), 4 * b + 4)
                for c in range(4):
                    if c >= 2:
                        e.wait_ge(sem("yT"), 4 * b + c - 1)
                    for i in range(2):
                        for jc in range(2):
                            at = 2 * c + i
                            m = e.transpose(bank(4 + c % 2)[:, i * S + jc * P:i * S + (jc + 1) * P],
                                            y[:, jc, at * P:(at + 1) * P], ident[:])
                    m.then_inc(sem("yT_ps"), 1)
                e.wait_ge(sem("yT"), 4 * b + 4)
                for jc in range(2):
                    for c in range(8):
                        m = e.matmul(bank(6 + jc, P), yT[:, c, jc * P:(jc + 1) * P], Wo[:, c, :],
                                     start=(c == 0), stop=(c == 7))
                m.then_inc(sem("o2"), 1)

            e.wait_ge(sem("x3"), 2 * B + 2)
            e.wait_ge(sem("fwa"), 2)
            e.matmul(bank(6, 2), mean_w[:], fsm[:, 8:10], start=True, stop=True).then_inc(sem("fws_ps"), 1)
            e.wait_ge(sem("fwq"), 9)
            with e.Fori(0, B // 2) as j:
                for q in range(2):
                    b = j * 2 + q
                    e.wait_ge(sem("fst"), b + 1)
                    for t in range(2):
                        m = e.transpose(bank(0)[:, t * P:(t + 1) * P], fst[q][:, t, :], ident[:])
                    m.then_inc(sem("fx_ps"), 1)
                    e.wait_ge(sem("fx"), b + 1)
                    e.wait_ge(sem(f"cw{q}"), 32 * j + 32)
                    for t in range(2):
                        m = e.matmul(bank(1)[:, t * P:(t + 1) * P], fx3T[q][:, t * P:(t + 1) * P], fcw[q],
                                     start=True, stop=True)
                    m.then_inc(sem("fc_ps"), 1)
                    e.wait_ge(sem("f_q"), b + 1)
                    for t in range(2):
                        m = e.transpose(bank(2).bitcast(BF16)[:, t * P:(t + 1) * P], fq[q][:, t, :], idb)
                    m.then_inc(sem("fqT_ps"), 1)
                    e.wait_ge(sem("fqT"), b + 1)
                    for t in range(2):
                        m = e.matmul(bank(3 + t), fqT[q][:, t * P:(t + 1) * P], f1q, start=True, stop=True)
                    m.then_inc(sem("fu_ps"), 1)
                    e.wait_ge(sem("f_q2"), b + 1)
                    for t in range(2):
                        for c in range(FC):
                            k = t * FC + c
                            m = e.transpose(bank(5).bitcast(BF16)[:, k * P:(k + 1) * P],
                                            fq2[q][:, t, c * P:(c + 1) * P], idb)
                    m.then_inc(sem("fq2T_ps"), 1)
                    e.wait_ge(sem("fq2T"), b + 1)
                    for t in range(2):
                        for c in range(FC):
                            m = e.matmul(bank(6)[:, t * P:(t + 1) * P], fq2T[q][:, t, c, :], f2q[:, c, :],
                                         start=(c == 0), stop=(c == 3))
                    m.then_inc(sem("fd_ps"), 1)
                    e.wait_ge(sem("f_o"), 2 * b + 6)

        def tail_scalar(e):
            for k in range(4):
                e.wait_ge(sem("fxc"), k + 1)
                e.activation(rsF[:, k * 512:(k + 1) * 512], xcF[:, k * 512:(k + 1) * 512], ACT.Square
                             ).then_inc(sem("fsq"), 1)
            e.wait_ge(sem("fv"), 4)
            e.activation(fold(rsF, 4), banks[:, 4:8, :], ACT.Ln, bias=eps[:, 0:1]).then_inc(sem("frs"), 1)
            e.wait_ge(sem("frs"), 1)
            e.activation(rsF, rsF, ACT.Exp, scale=-0.5).then_inc(sem("frs"), 1)
            for k in range(4):
                e.wait_ge(sem("x1t_ps"), k + 1)
                e.activation(xt_[:, k * 512:(k + 1) * 512], bank(k), ACT.Copy).then_inc(sem("x1t"), 1)

            def gelu(b, q):
                e.wait_ge(sem("up"), b + 1)
                wait(e, sem("dn"), b - 1)
                for c in range(FC):
                    e.activation(mH[q][:, c, :], fold(banks[:, 2 * q + c // 2, :], 2)[:, c % 2, :], ACT.Gelu,
                                 bias=mB1[:, c:c + 1]).then_inc(sem("gelu"), 1)

            e.wait_ge(sem("mw_in"), 80)
            gelu(0, 0)
            gelu(1, 1)
            with e.Fori(1, B // 2) as j:
                gelu(j * 2, 0)
                gelu(j * 2 + 1, 1)
            e.wait_ge(sem("rt"), RT_DIFF)
            e.activation(w2_, dn, ACT.Exp).then_inc(sem("rexp"), 1)

            def silu(G, first):
                for c in range(FC):
                    X = G * 4 + c
                    e.wait_ge(sem("mo_up"), X + 1)
                    if not (first and c < 2):
                        e.wait_ge(sem("mo_int"), X - 1)
                    e.activation(sil[c % 2], bank(2 * (c % 2)), ACT.Silu).then_inc(sem("mo_sil"), 1)

            silu(0, True)
            with e.Fori(1, 4 * NE) as G:
                silu(G, False)

            for k in range(4):
                e.wait_ge(sem("x2T_ps"), k + 1)
                e.activation(x2T[:, k * 512:(k + 1) * 512], bank(k), ACT.Copy).then_inc(sem("x2T"), 1)
            for k in range(4):
                e.wait_ge(sem("at_ps"), k + 1)
                e.activation(at_[0:32, k * 512:(k + 1) * 512], bank(4 + k)[0:32, :], ACT.Tanh, bias=cb1[0:32, :]
                             ).then_inc(sem("at"), 1)
            for k in range(4):
                e.wait_ge(sem("S_ps"), k + 1)
                e.activation(Sall[:, k * 512:(k + 1) * 512], bank(k), ACT.Copy).then_inc(sem("Sall"), 1)
            e.sem_inc(sem("pPT"), 8)
            with e.Fori(0, B // 2) as j:
                for q in range(2):
                    b = j * 2 + q
                    e.wait_ge(sem("pmx"), b + 1)
                    for jc in range(2):
                        e.activation(pM[q][:, jc, :], pM[q][:, jc, :], ACT.Exp, bias=pmx[:, 2 * q + jc:2 * q + jc + 1],
                                     accum_out=psm[:, 2 * q + jc:2 * q + jc + 1]).then_inc(sem("pexp"), 1)
                    e.wait_ge(sem("pPT_ps"), b + 1)
                    e.wait_ge(sem("pT"), b + 7)
                    e.activation(pPT[q], fold(bank(q), 2), ACT.Copy).then_inc(sem("pPT"), 1)

            with e.Fori(0, B) as b:
                e.wait_ge(sem("lat_ps"), b + 1)
                e.activation(latT, bank(0, S), ACT.Copy).then_inc(sem("lat"), 1)
                for c in range(4):
                    e.wait_ge(sem("q_ps"), 4 * b + c + 1)
                    e.activation(qT[:, 2 * c:2 * c + 2, :], fold(bank(1 + c), 2), ACT.Copy).then_inc(sem("q_sb"), 1)
                for c in range(4):
                    e.wait_ge(sem("v_ps"), 4 * b + c + 1)
                    e.activation(V[:, c // 2, (c % 2) * 512:(c % 2 + 1) * 512], bank(1 + c), ACT.Copy
                                 ).then_inc(sem("v_sb"), 1)
                for hp in range(8):
                    e.wait_ge(sem("negm"), 8 * b + hp + 1)
                    for hh in range(2):
                        hd = 2 * hp + hh
                        if hd >= 4:
                            e.wait_ge(sem("PT_ps"), 16 * b + hd - 3)
                        for jc in range(2):
                            lo, n = (0, P) if jc == 0 else (P, 2 * P)
                            m = e.activation(Pr[hd % 4][:, lo:lo + n], bank(2 * (hp % 2) + hh)[:, lo:lo + n], ACT.Exp,
                                             bias=negm[:, jc, hd:hd + 1], scale=SCALE,
                                             accum_out=sums[:, jc, hd:hd + 1])
                        m.then_inc(sem("P"), 1)

            with e.Fori(0, B // 2) as j:
                for q in range(2):
                    b = j * 2 + q
                    e.wait_ge(sem("fx_ps"), b + 1)
                    e.activation(fx3T[q], bank(0, S), ACT.Copy).then_inc(sem("fx"), 1)
                    e.wait_ge(sem("fqT_ps"), b + 1)
                    e.activation(fqT[q], bank(2).bitcast(BF16)[:, 0:S], ACT.Copy).then_inc(sem("fqT"), 1)
                    e.wait_ge(sem("fu_ps"), b + 1)
                    for t in range(2):
                        e.activation(fg[q][:, t, :], bank(3 + t), ACT.Gelu, scale=fr[:, 1, t:t + 1]
                                     ).then_inc(sem("f_g"), 1)

        def tail_vector(e):
            for k in range(4):
                e.wait_ge(sem("fm"), k + 1)
                if k == 0:
                    e.wait_ge(sem(DONE_R[0]), DONE_R[1])
                e.tensor_tensor(xcF[:, k * 512:(k + 1) * 512], xs[:, k * 512:(k + 1) * 512], bank(k), ALU.subtract
                                ).then_inc(sem("fxc"), 1)
            e.wait_ge(sem("frs"), 2)
            e.wait_ge(sem("fxc"), 4)
            e.scalar_tensor_tensor(out=xcF, in0=xcF, scalar=lng[:, 0:1], in1=rsF, op0=ALU.mult, op1=ALU.mult
                                   ).then_inc(sem("x1"), 1)
            e.wait_ge(sem("x1"), 1)
            e.tensor_scalar(xcF, xcF, lnb[:, 0:1], None, ALU.add).then_inc(sem("x1"), 1)
            e.wait_ge(sem("x1"), 2)
            e.tensor_tensor(fold(xs[:, :], B), fold(xcF, B), ypad[:, :, 1:S + 1], ALU.add).then_inc(sem("x1"), 1)
            e.sem_inc(sem("rT"), 8)
            e.wait_ge(sem("mw_in"), 80)
            with e.Fori(0, B // 2) as j:
                for q in range(2):
                    b = j * 2 + q
                    e.wait_ge(sem("dn"), b + 1)
                    e.wait_ge(sem(f"we{q}"), 32 * j + 32)
                    e.tensor_scalar(rT[:, bass.ds(b * S, S)], bank(4 + q, S), mBias[:, bass.ds(b, 1)], None, ALU.add
                                    ).then_inc(sem("rT"), 1)

            r = Chain(e, "rt")

            def each(ap):
                return ap.unsqueeze(2).to_broadcast([P, NT, NE])

            iota = io_.unsqueeze(1).to_broadcast([P, NT, NE])

            def top(m, oh):
                r(e.tensor_reduce(m, lg, AX_X, ALU.max)); r.sync()
                r(e.tensor_tensor(tmp, lg, each(m), ALU.is_equal)); r.sync()
                r(e.scalar_tensor_tensor(out=tmp, in0=tmp, scalar=-100.0, in1=iota, op0=ALU.mult, op1=ALU.add)); r.sync()
                r(e.tensor_reduce(i1, tmp, AX_X, ALU.min)); r.sync()
                r(e.tensor_tensor(oh, tmp, each(i1), ALU.is_equal)); r.sync()

            e.wait_ge(sem("lg_ps"), 1)
            e.tensor_copy(lg, fold(bank(6, NT * NE), NT)).then_inc(sem("lg"), 1)
            e.wait_ge(sem("lg"), 1)
            e.wait_ge(sem("gw_in"), 32)
            top(m1, oh1)
            r(e.scalar_tensor_tensor(out=lg, in0=oh1, scalar=-BIG, in1=lg, op0=ALU.mult, op1=ALU.add)); r.sync()
            top(m2, oh2)
            r(e.tensor_tensor(dn, m2, m1, ALU.subtract)); r.sync()
            e.wait_ge(sem("rexp"), 1)
            r(e.tensor_scalar(dn, w2_, 1.0, None, ALU.add)); r.sync()
            r(e.reciprocal(w1_, dn)); r.sync()
            r(e.tensor_tensor(w2_, w2_, w1_, ALU.mult)); r.sync()
            r(e.tensor_tensor(oh1, oh1, each(w1_), ALU.mult))
            r(e.tensor_tensor(oh2, oh2, each(w2_), ALU.mult)); r.sync()
            r(e.tensor_tensor(oh1, oh1, oh2, ALU.add)); r.sync()
            assert r.k == RT

            def ex_mul(G, g):
                for c in range(FC):
                    e.wait_ge(sem("mo_sil"), G * 4 + c + 1)
                    e.tensor_tensor(inter[g % 2][:, c, :], sil[c % 2], bank(2 * (c % 2) + 1), ALU.mult
                                    ).then_inc(sem("mo_int"), 1)

            def ex_acc(G, g, x):
                e.wait_ge(sem("mo_dn"), G + 1)
                for j in range(4):
                    t = 4 * g + j
                    e.scalar_tensor_tensor(out=xt[:, t, :], in0=bank(6 + g % 2)[:, j * P:(j + 1) * P],
                                           scalar=oh1[:, t, bass.ds(x, 1)], in1=xt[:, t, :], op0=ALU.mult, op1=ALU.add
                                           ).then_inc(sem("mo_acc"), 1)

            def ex_body(j, first):
                for k in range(2):
                    for g in range(4):
                        G = j * 8 + k * 4 + g
                        ex_mul(G, g)
                        if not (first and k == 0 and g == 0):
                            ex_acc(G - 1, (g - 1) % 4, j * 2 + k - (0 if g else 1))

            ex_body(0, True)
            with e.Fori(1, NE // 2) as j:
                ex_body(j, False)
            ex_acc(4 * NE - 1, 3, NE - 1)

            c_ = Chain(e, "pcst")
            e.wait_ge(sem("pc_in"), 112)
            one = fold(pone, 3)
            c_(e.tensor_copy(prc_f, cid.bitcast(I32))); c_.sync()
            c_(e.tensor_scalar(one[:, 0, :], prc_f, 0.0, None, ALU.is_equal))
            c_(e.tensor_scalar(one[:, 1, :], prc_f, 1.0, None, ALU.is_equal)); c_.sync()
            c_(e.tensor_tensor(one[:, 2, :], one[:, 0, :], one[:, 1, :], ALU.add)); c_.sync()
            c_(e.tensor_scalar(one[:, 2, :], one[:, 2, :], -1.0, 1.0, ALU.mult, ALU.add)); c_.sync()
            cnt_b = fold(pcb, B)
            for jc in range(2):
                c_(e.tensor_scalar(cnt_b[:, :, jc], one[:, 0, :], pcnt[:, jc:jc + 1], None, ALU.mult)); c_.sync()
                for k in (1, 2):
                    c_(e.scalar_tensor_tensor(out=cnt_b[:, :, jc], in0=one[:, k, :], scalar=pcnt[:, 2 * k + jc:2 * k + jc + 1],
                                              in1=cnt_b[:, :, jc], op0=ALU.mult, op1=ALU.add)); c_.sync()
            c_(e.tensor_copy(idb, ident[:]))
            c_(e.tensor_copy(cmask, cmraw)); c_.sync()
            e.sem_inc(sem("acon"), 2)
            e.wait_ge(sem("Sall"), 4)
            e.sem_inc(sem("pT"), 8)
            with e.Fori(0, B // 2) as j:
                for q in range(2):
                    b = j * 2 + q
                    m = Chain(e, "pch", b * 7)
                    e.wait_ge(sem("pPT"), b + 7)
                    flat_ = pM[q].rearrange("p a b -> p (a b)")
                    kk = [pm_[:, k * PAIR:(k + 1) * PAIR] for k in range(3)]
                    m(e.tensor_scalar(flat_, kk[0], one[:, 0, bass.ds(b, 1)], None, ALU.mult)); m.sync()
                    for k in (1, 2):
                        m(e.scalar_tensor_tensor(out=flat_, in0=kk[k], scalar=one[:, k, bass.ds(b, 1)], in1=flat_,
                                                 op0=ALU.mult, op1=ALU.add)); m.sync()
                    m(e.tensor_tensor(pM[q], pM[q], Sall[:, bass.ds(b * S, S)].unsqueeze(1).to_broadcast([P, 2, S]),
                                      ALU.add)); m.sync()
                    e.tensor_reduce(pmx[:, 2 * q:2 * q + 2], pM[q], AX_X, ALU.max, negate=True).then_inc(sem("pmx"), 1)
                    e.wait_ge(sem("pexp"), 2 * b + 2)
                    m(e.tensor_tensor(prc[:, 0:2], psm[:, 2 * q:2 * q + 2], cnt_b[:, bass.ds(b, 1), :].rearrange("p a b -> p (a b)"),
                                      ALU.mult)); m.sync()
                    m(e.reciprocal(prc[:, 2:4], prc[:, 0:2])); m.sync()
                    m(e.tensor_tensor(pM[q], pM[q], prc[:, 2:4].unsqueeze(2).to_broadcast([P, 2, S]), ALU.mult)); m.sync()
                    assert m.k == 7
                    e.sem_inc(sem("pP"), 1)
                    e.wait_ge(sem("pT_ps"), b + 1)
                    e.tensor_copy(pT[:, bass.ds(b * S, S)], bank(2 + q, S)).then_inc(sem("pT"), 1)

            e.sem_inc(sem("x3"), 2)
            with e.Fori(0, B) as b:
                for c in range(4):
                    e.wait_ge(sem("k_ps"), 4 * b + c + 1)
                    e.tensor_copy(kT[:, 2 * c:2 * c + 2, :], fold(bank((5, 6, 7, 0)[c]), 2)).then_inc(sem("k_sb"), 1)

                def maxima(hp):
                    e.wait_ge(sem("S2_ps"), 8 * b + hp + 1)
                    lo = 2 * (hp % 2)
                    for jc in range(2):
                        c0, n = (0, P) if jc == 0 else (P, 2 * P)
                        m = e.tensor_reduce(smx2[:, jc, 2 * hp:2 * hp + 2], banks[:, lo:lo + 2, c0:c0 + n], AX_X, ALU.max)
                        m.then_inc(sem("smax"), 1)
                    e.wait_ge(sem("smax"), 16 * b + 2 * hp + 2)
                    e.tensor_scalar(negm[:, :, 2 * hp:2 * hp + 2], smx2[:, :, 2 * hp:2 * hp + 2], -SCALE, None, ALU.mult
                                    ).then_inc(sem("negm"), 1)

                def turned(hd):
                    e.wait_ge(sem("PT_ps"), 16 * b + hd + 1)
                    if hd >= 4:
                        e.wait_ge(sem("av"), 8 * b + hd // 2 - 1)
                    e.tensor_copy(PT[hd % 4], bank(4 + hd % 2, TRI)).then_inc(sem("PT"), 1)

                def finish(half):
                    e.wait_ge(sem("av"), 8 * b + 4 * half + 4)
                    hs = slice(8 * half, 8 * half + 8)
                    e.reciprocal(inv[:, :, hs], sums[:, :, hs]).then_inc(sem("inv"), 1)
                    e.wait_ge(sem("inv"), 2 * b + half + 1)
                    for jc in range(2):
                        e.tensor_tensor(y[:, jc, half * 512:(half + 1) * 512].rearrange("p (h d) -> p h d", h=8),
                                        bank(6 + jc).rearrange("p (h d) -> p h d", h=8),
                                        inv[:, jc, hs].unsqueeze(2).to_broadcast([P, 8, HS]), ALU.mult
                                        ).then_inc(sem("att_y"), 1)

                maxima(0)
                for hp in range(1, 8):
                    maxima(hp)
                    turned(2 * hp - 2)
                    turned(2 * hp - 1)
                    if hp == 6:
                        finish(0)
                turned(14)
                turned(15)
                finish(1)
                for c in range(4):
                    e.wait_ge(sem("yT_ps"), 4 * b + c + 1)
                    e.tensor_copy(yT[:, 2 * c:2 * c + 2, :], fold(bank(4 + c % 2), 2)).then_inc(sem("yT"), 1)
                e.wait_ge(sem("o2"), b + 1)
                for jc in range(2):
                    t = xt[:, bass.ds(b * 2 + jc, 1), :].rearrange("p a b -> p (a b)")
                    e.tensor_tensor(t, t, bank(6 + jc, P), ALU.add).then_inc(sem("x3"), 1)

            w = Chain(e, "fwq")
            e.wait_ge(sem("fw_in"), 32)
            e.tensor_reduce(fsm[:, 8:9], f1raw, AX_X, ALU.add, apply_absolute_value=True).then_inc(sem("fwa"), 1)
            e.tensor_reduce(fsm[:, 9:10], f2raw, AX_X, ALU.add, apply_absolute_value=True).then_inc(sem("fwa"), 1)
            e.wait_ge(sem("fws_ps"), 1)
            w(e.tensor_scalar(fsm[:, 10:12], bank(6, 2), 1.0 / FF, LN_EPS, ALU.mult, ALU.max)); w.sync()
            w(e.reciprocal(fsm[:, 12:14], fsm[:, 10:12])); w.sync()
            for k, (raw, dst) in enumerate(((f1raw, f1q_), (f2raw, f2q_))):
                w(e.tensor_scalar(raw, raw, fsm[:, 12 + k:13 + k], ROUND, ALU.mult, ALU.add)); w.sync()
                w(e.tensor_scalar(raw, raw, -ROUND, -1.0, ALU.add, ALU.max)); w.sync()
                w(e.tensor_scalar(dst.bitcast(BF16), raw, 1.0, None, ALU.min)); w.sync()
            w(e.tensor_scalar(fsm[:, 14:16], fsm[:, 10:12], 1.0 / 127.0, None, ALU.mult)); w.sync()
            e.sem_inc(sem("f_c"), 8)
            e.sem_inc(sem("f_o"), 4)

            def quantise(m, src, tmp_t, dst, row):
                m(e.tensor_reduce(fr[:, 2, :], src, AX_X, ALU.max, apply_absolute_value=True)); m.sync()
                m(e.tensor_scalar(fr[:, 2, :], fr[:, 2, :], LN_EPS, None, ALU.max)); m.sync()
                m(e.reciprocal(fr[:, 3, :], fr[:, 2, :]))
                m(e.tensor_scalar(fr[:, row, :], fr[:, 2, :], fsm[:, 14 + (row != 1):15 + (row != 1)], None, ALU.mult)); m.sync()
                m(e.tensor_scalar(fr[:, 3, :], fr[:, 3, :], 127.0, None, ALU.mult)); m.sync()
                for t in range(2):
                    m(e.tensor_scalar(tmp_t[:, t, :], src[:, t, :], fr[:, 3, t:t + 1], ROUND, ALU.mult, ALU.add))
                m.sync()
                m(e.tensor_scalar(tmp_t, tmp_t, -ROUND, 127.0, ALU.add, ALU.min)); m.sync()
                e.tensor_scalar(dst, tmp_t, -128.0, None, ALU.max).then_inc(sem("f_q" if row == 1 else "f_q2"), 1)

            with e.Fori(0, B // 2) as j:
                for q in range(2):
                    b = j * 2 + q
                    m = Chain(e, "fch", b * 16)
                    e.wait_ge(sem("fc_ps"), b + 1)
                    e.wait_ge(sem(f"cw{q}"), 32 * j + 32)
                    e.tensor_tensor(fc[q], fold(bank(1, S), 2), fcb[q].unsqueeze(1).to_broadcast([P, 2, P]), ALU.add
                                    ).then_inc(sem("f_c"), 1)
                    e.wait_ge(sem("f_c"), b + 9)
                    quantise(m, fc[q], ft[q], fq[q], 1)
                    e.wait_ge(sem("f_g"), 2 * b + 2)
                    quantise(m, fg[q], ft2[q], fq2[q], 0)
                    assert m.k == 16
                    e.wait_ge(sem("fq2T_ps"), b + 1)
                    e.tensor_copy(fq2T[q].rearrange("p t c k -> p (t c k)"), bank(5).bitcast(BF16)).then_inc(sem("fq2T"), 1)
                    e.wait_ge(sem("fd_ps"), b + 1)
                    e.wait_ge(sem("out"), 16 * b + 16)
                    for t in range(2):
                        e.scalar_tensor_tensor(out=fo[q][:, t, :], in0=bank(6)[:, t * P:(t + 1) * P],
                                               scalar=fr[:, 0, t:t + 1], in1=fst[q][:, t, :], op0=ALU.mult, op1=ALU.add
                                               ).then_inc(sem("f_o"), 1)

        block = ctx.enter_context(nc.Block())

        @block.sync
        def _(e):
            e.dma_start(xtok, x_tok).then_inc(sem("x_in"), 16)
            for j, n in enumerate(("condB_zX", "condB_zY", "condB_zR")):
                e.dma_start(zb[:, j, :], bass.AP(io[n].tensor, 0, [[0, P], [1, B]])).then_inc(sem("z_in"), 16)
            e.dma_start(lng[:], io["L0_attn_ln_g"].rearrange("(p a) -> p a", a=1)).then_inc(sem("ln_in"), 16)
            e.dma_start(lnb[:], io["L0_attn_ln_b"].rearrange("(p a) -> p a", a=1)).then_inc(sem("ln_in"), 16)
            e.dma_start(A_all[:].rearrange("p l s -> p (l s)"), io["A_log"]).then_inc(sem("alog_in"), 16)

            def prepare(L):
                e.wait_ge(sem("scr"), 32 * L + 32)
                e.dma_start(raw_in, layer_of(io["in_w"], L)).then_inc(sem("raw"), 16)
                e.dma_start(raw_cw, bass.AP(io["conv_w"].tensor, L * (TAPS * 2 * P), [[0, P], [1, TAPS * 2 * P]])
                            ).then_inc(sem("raw"), 16)
                e.dma_start(bunF[:, FC_Z:FC_CB], layer_of(io["zxp_w"], L)).then_inc(sem("raw"), 16)
                e.dma_start(raw_out, layer_of(io["out_w"], L)).then_inc(sem("raw"), 16)
                e.dma_start(raw_sm, layer_of(io["small"], L)).then_inc(sem("raw"), 16)
                e.wait_ge(sem("bun"), 5 * L + 5)
                e.dma_start(layer_of(scrF, L), bunF).then_inc(sem("scr"), 16)
                e.dma_start(layer_of(scrS, L), bunS).then_inc(sem("scr"), 16)

            def load(L):
                wait(e, sem("dt"), L * (2 * NPAIR))
                wait(e, sem("dt_ps"), L * (2 * NPAIR))
                e.dma_start(wF[:], layer_of(scrF, L)).then_inc(sem("wF"), 16)
                e.dma_start(wdt[BC3:BC3 + RANK, :], layer_of(io["dt_w"], L)).then_inc(sem("wF"), 16)
                wait(e, sem("o_ps"), L * NPAIR)
                e.dma_start(wS[:], layer_of(scrS, L)).then_inc(sem("wS"), 16)

            e.sem_inc(sem("scr"), 32)
            with e.Fori(0, LAYERS) as L:
                prepare(L)
            e.wait_ge(sem("scr"), 32 * LAYERS + 32)
            load(0)
            with e.Fori(1, LAYERS) as L:
                load(L)
            tail_sync(e)

        @block.gpsimd
        def _(e):
            count = [0]

            def const(ins):
                count[0] += 1
                ins.then_inc(sem("const"), 1)
                e.wait_ge(sem("const"), count[0])

            def diagonal(t, value, base, cols):
                const(e.affine_select(out=t, in_=t, compare_op=ALU.not_equal, fill=value, base=base,
                                      pattern=cols, channel_multiplier=1))

            const(e.memset(ident[:], 0.0))
            diagonal(ident[:], 1.0, 0, [[-1, P]])
            const(e.memset(tri, 0.0))
            diagonal(tri, -2.0, 0, [[-1, P]])
            diagonal(tri, 1.0, 1, [[-1, P]])
            diagonal(tri, 1.0, -1, [[-1, P]])
            diagonal(tri[:, 0:1], 2.0, -1, [[0, 1]])
            diagonal(tri[:, P - 1:P], 2.0, 2 - P, [[0, 1]])
            const(e.memset(mean_w[:], 1.0 / P))
            const(e.tensor_tensor(center_w[:], ident[:], mean_w[:], ALU.subtract))
            const(e.memset(eps[:], LN_EPS))
            const(e.memset(xn[:, :, 0:TAPS - 1], 0.0))
            for part in range(3):
                if part == 0:
                    const(e.memset(sel[:], 0.0))
                diagonal(sel[:], 1.0, -2 * NS * part, [[-1, 2 * NS], [0, P]])
            assert count[0] == CONSTS
            for half in range(HALVES):
                e.memset(dA[half][:, :, 0:1], 0.0).then_inc(sem("dA0"), 1)

            def slot(p, q):
                for i in range(2):
                    n = 2 * p + i
                    for half in range(HALVES):
                        hb = h[2 * i + half]
                        e.wait_ge(sem("scan"), 2 * n + half + 1)
                        e.wait_ge(sem("C"), 8 * n + 8)
                        e.tensor_tensor(hb[:], hb[:], Cb[i][:], ALU.mult).then_inc(sem("hC"), 1)
                        e.wait_ge(sem("hC"), 4 * p + 2 * i + half + 1)
                        e.tensor_tensor(hb[:, PRE:2 * PRE, :], hb[:, 0:PRE, :], hb[:, PRE:2 * PRE, :], ALU.add
                                        ).then_inc(sem("pre"), 1)

            with e.Fori(0, SLOTS) as p:
                slot(p, 0)
            tail_gpsimd(e)

        def cols(t):
            c = (t % NPAIR) * PAIR
            return bass.ds(c, PAIR)

        def pe_center(e, t, q):
            e.wait_ge(sem("res"), t + 1)
            wait(e, sem("dt"), 2 * t)
            e.matmul(ps_F[0][:], center_w[:], xs[:, cols(t)], start=True, stop=True).then_inc(sem("cen"), 1)

        def act_square(e, t, q):
            e.wait_ge(sem("cen"), t + 1)
            e.activation(rstd[:], ps_F[0][:], ACT.Square).then_inc(sem("sq"), 1)

        def pe_var(e, t, q):
            e.wait_ge(sem("sq"), t + 1)
            e.matmul(ps_F[1][:], mean_w[:], rstd[:], start=True, stop=True).then_inc(sem("var"), 1)

        def act_lnv(e, t, q):
            e.wait_ge(sem("var"), t + 1)
            e.activation(rstd[:], ps_F[1][:], ACT.Ln, bias=eps[:, 0:1]).then_inc(sem("lnv"), 1)

        def act_rstd(e, t, q):
            e.wait_ge(sem("lnv"), t + 1)
            e.activation(rstd[:], rstd[:], ACT.Exp, scale=-0.5).then_inc(sem("rstd"), 1)

        def dve_norm(e, t, q):
            e.wait_ge(sem("rstd"), t + 1)
            e.scalar_tensor_tensor(out=xc[:], in0=ps_F[0][:], scalar=lng[:, 0:1], in1=rstd[:],
                                   op0=ALU.mult, op1=ALU.mult).then_inc(sem("xg"), 1)
            e.wait_ge(sem("xg"), t + 1)
            e.tensor_scalar(xn[:, :, TAPS - 1:], xc[:].rearrange("p (b l) -> p b l", b=2), lnb[:, 0:1], None,
                            ALU.add).then_inc(sem("xn"), 1)

        def pe_conv(e, t, q, half):
            if half == 0:
                e.wait_ge(sem("xn"), t + 1)
                e.wait_ge(sem("wF"), 32 * (t // NPAIR) + 32)
            for k in range(TAPS):
                m = e.matmul(ps_F[half][:].rearrange("p (b l) -> p b l", b=2),
                             wF[:, FC_TAP + k * 2 * P + half * P:FC_TAP + k * 2 * P + (half + 1) * P],
                             xn[:, :, k:k + S], start=(k == 0), stop=(k == TAPS - 1))
            m.then_inc(sem("conv"), 1)

        def act_xh(e, t, q, half):
            e.wait_ge(sem("conv"), 2 * t + half + 1)
            e.activation(xh[:, half, :], ps_F[half][:], ACT.Identity, bias=wF[:, FC_CB + half:FC_CB + half + 1]
                         ).then_inc(sem("xh"), 1)

        def act_th(e, t, q):
            e.wait_ge(sem("xh"), 2 * t + 2)
            e.activation(th[:], xh[:], ACT.Tanh).then_inc(sem("th"), 1)

        def dve_xm(e, t, q):
            e.wait_ge(sem("th"), t + 1)
            e.scalar_tensor_tensor(out=xm[q][:], in0=th[:], scalar=1.0, in1=xh[:],
                                   op0=ALU.add, op1=ALU.mult).then_inc(sem("xm"), 1)

        def pe_z(e, t, q, half):
            e.wait_ge(sem("xh"), 2 * t + half + 1)
            c = FC_Z + half * P
            e.matmul(ps_F[half][:].rearrange("p (b l) -> p b l", b=2), wF[:, c:c + P],
                     xn[:, :, TAPS - 1:], start=True, stop=True).then_inc(sem("z_ps"), 1)

        def act_zt(e, t, q, half):
            if half == 0:
                e.wait_ge(sem("xm"), t + 1)
            e.wait_ge(sem("z_ps"), 2 * t + half + 1)
            e.activation(th[:, half, :], ps_F[half][:], ACT.Tanh, scale=0.5).then_inc(sem("zt"), 1)

        def dve_zs(e, t, q, half):
            e.wait_ge(sem("zt"), 2 * t + half + 1)
            e.scalar_tensor_tensor(out=zs[q][:, half, :], in0=th[:, half, :], scalar=1.0,
                                   in1=ps_F[half][:], op0=ALU.add, op1=ALU.mult).then_inc(sem("zs"), 1)

        def pe_xproj(e, t, q):
            e.wait_ge(sem("zs"), 2 * t + 1)
            e.wait_ge(sem("xm"), t + 1)
            for half in range(HALVES):
                c = FC_XP + half * XPN
                m = e.matmul(ps_F[0][0:XPN, :], wF[:, c:c + XPN], xm[q][:, half, :],
                             start=(half == 0), stop=(half == 1))
            m.then_inc(sem("xd"), 1)

        def act_high(e, t, q):
            e.wait_ge(sem("xd"), t + 1)
            e.activation(bc[q][:, :], ps_F[0][0:BC3, :], ACT.Copy).then_inc(sem("hi"), 1)

        def act_rank8(e, t, q):
            e.wait_ge(sem("xd"), t + 1)
            e.activation(dt8, ps_F[0][BC3:XPN, :], ACT.Copy).then_inc(sem("hi"), 1)

        def dve_split(e, t, q):
            e.wait_ge(sem("hi"), 2 * t + 1)
            m = 2 * NS
            e.tensor_tensor(r1, ps_F[0][0:BC3, :], bc[q][:, :], ALU.subtract).then_inc(sem("split"), 1)
            e.wait_ge(sem("split"), 3 * t + 1)
            e.tensor_copy(r2[2 * m:BC3, :], r1[2 * m:BC3, :]).then_inc(sem("split"), 1)
            e.tensor_copy(bc[q][m:2 * m, :], r1[m:2 * m, :]).then_inc(sem("split"), 1)
            e.wait_ge(sem("split"), 3 * t + 2)
            e.tensor_tensor(bc[q][2 * m:BC3, :], r1[2 * m:BC3, :], r2[2 * m:BC3, :],
                            ALU.subtract).then_inc(sem("bc"), 1)

        def pe_dt(e, t, q, half):
            if half == 0:
                e.wait_ge(sem("hi"), 2 * t + 2)
                e.wait_ge(sem("zs"), 2 * t + 2)
                e.wait_ge(sem("res"), t - 1 + NPAIR)
            else:
                e.wait_ge(sem("bc"), t + 1)
            e.matmul(ps_F[1 - half][:], wdt[BC3:BC3 + RANK, half * P:(half + 1) * P], dt8,
                     start=True, stop=True).then_inc(sem("dt_ps"), 1)

        def dve_amin(e, t, q, half):
            e.wait_ge(sem("dt_ps"), 2 * t + half + 1)
            e.tensor_scalar(xh[:, half, :], ps_F[1 - half][:], wF[:, FC_DTB + half:FC_DTB + half + 1], 40.0,
                            ALU.add, ALU.min).then_inc(sem("amin"), 1)

        def act_sp_exp(e, t, q):
            e.wait_ge(sem("amin"), 2 * t + 2)
            e.activation(xh[:], xh[:], ACT.Exp).then_inc(sem("sp"), 1)

        def act_sp_ln(e, t, q):
            e.wait_ge(sem("sp"), 2 * t + 1)
            e.activation(xh[:], xh[:], ACT.Ln, bias=1.0).then_inc(sem("sp"), 1)

        def dve_dt(e, t, q):
            e.wait_ge(sem("sp"), 2 * t + 2)
            wait(e, sem("dA"), 4 * t)
            for half in range(HALVES):
                e.scalar_tensor_tensor(out=dt[:, half, :], in0=ps_F[1 - half][:],
                                       scalar=wF[:, FC_DTB + half:FC_DTB + half + 1], in1=xh[:, half, :],
                                       op0=ALU.add, op1=ALU.max).then_inc(sem("dt"), 1)

        def dve_u(e, t, q):
            e.wait_ge(sem("dt"), 2 * t + 2)
            e.tensor_tensor(u[:], dt[:], xm[q][:], ALU.mult).then_inc(sem("u"), 1)

        def pe_B(e, p, q, i, g):
            n = 2 * p + i
            if i == 0 and g == 0:
                e.wait_ge(sem("bc"), p + 1)
            wait(e, sem("mul"), 8 * n + 2 * g - 2)
            for j in range(4):
                m = e.matmul(ps_B[g % 2][:, j, :], sel[:, 4 * g + j, :], bc[q][:, i * S:(i + 1) * S],
                             start=True, stop=True)
            m.then_inc(sem("B"), 1)

        def pe_C(e, p, q, i, c):
            n = 2 * p + i
            if i == 0 and c == 0:
                e.wait_ge(sem("bc"), p + 1)
            wait(e, sem("C"), 8 * n + c)
            for j in range(2):
                m = e.matmul(ps_C[:, j, :], sel[:, NS + 2 * c + j, :], bc[q][:, i * S:(i + 1) * S],
                             start=True, stop=True)
            m.then_inc(sem("C_ps"), 1)

        def act_C(e, p, q, i, c):
            n = 2 * p + i
            if c == 0:
                wait(e, sem("hC"), 2 * n - 2)
            e.wait_ge(sem("C_ps"), 8 * n + c + 1)
            e.activation(Cb[i][:, 2 * c:2 * c + 2, :], ps_C, ACT.Copy).then_inc(sem("C"), 1)

        def act_dA(e, p, q, i, half, part):
            n = 2 * p + i
            if i == 0 and half == 0 and part == 0:
                wait(e, sem("dA"), 4 * p)
                e.activation(A_cur[q][:], A_all[:, bass.ds(p // NPAIR, 1), :].rearrange("p l s -> p (l s)"),
                             ACT.Copy).then_inc(sem("A_cur"), 1)
                e.wait_ge(sem("A_cur"), p + 1)
                e.wait_ge(sem("dt"), 2 * p + 2)
            if part == 0:
                wait(e, sem("scan"), 2 * n + half - 1)
                if isinstance(p, int) and p == 0:
                    e.wait_ge(sem("dA0"), 2)
            for s in range(4 * part, 4 * part + 4):
                m = e.activation(dA[half][:, s, 1:S], dt[:, half, i * S + 1:(i + 1) * S], ACT.Exp,
                                 scale=A_cur[q][:, half * NS + s:half * NS + s + 1])
            if part == 3:
                m.then_inc(sem("dA"), 1)

        def dve_mul(e, p, q, i, g, half):
            n = 2 * p + i
            e.wait_ge(sem("B"), 4 * n + g + 1)
            if g == 0 and half == 0:
                e.wait_ge(sem("u"), p + 1)
                if isinstance(p, int) and p == 0:
                    e.wait_ge(sem("scr"), 32 * LAYERS + 32)
            e.tensor_tensor(h[2 * i + half][:, 4 * g:4 * g + 4, :], ps_B[g % 2],
                            u[:, half, i * S:(i + 1) * S].unsqueeze(1).to_broadcast([P, 4, S]),
                            ALU.mult).then_inc(sem("mul"), 1)

        def dve_scan(e, p, q, i, half):
            n = 2 * p + i
            e.wait_ge(sem("dA"), 2 * n + half + 1)
            e.wait_ge(sem("mul"), 8 * n + 8)
            hb = h[2 * i + half][:, :, :].rearrange("p s l -> p (s l)")
            e.tensor_tensor_scan(hb, dA[half][:, :, :].rearrange("p s l -> p (s l)"), hb, 0.0,
                                 ALU.mult, ALU.add).then_inc(sem("scan"), 1)

        def pe_sum(e, p, q, i, half, part):
            n = 2 * p + i
            if part == 0:
                e.wait_ge(sem("pre"), 2 * n + half + 1)
                if half == 0:
                    wait(e, sem("gate"), n)
            for s in SUM_PARTS[part]:
                e.matmul(ps_Y[:, half, :], ident[:], h[2 * i + half][:, s, :], start=(s == PRE), stop=False)
            if part == 3:
                if i == 0 and half == 0:
                    e.wait_ge(sem("wS"), 16 * (p // NPAIR) + 16)
                e.matmul(ps_Y[:, half, :], wS[:, SC_D + half * P:SC_D + (half + 1) * P],
                         xm[q][:, half, i * S:(i + 1) * S], start=False, stop=True).then_inc(sem("y"), 1)

        def dve_gate(e, p, q, i):
            n = 2 * p + i
            e.wait_ge(sem("y"), 2 * n + 2)
            e.tensor_tensor(yz[:, :, i, :], ps_Y, zs[q][:, :, i * S:(i + 1) * S],
                            ALU.mult).then_inc(sem("gate"), 1)

        def pe_out(e, p, q):
            e.wait_ge(sem("gate"), 2 * p + 2)
            if isinstance(p, int) and p >= SLOTS - 2:
                e.wait_ge(sem("dt"), 2 * SLOTS)
                wait(e, sem("res"), p + NPAIR)
            else:
                e.wait_ge(sem("zs"), 2 * p + 6)
            for half in range(HALVES):
                m = e.matmul(ps_F[1][:], wS[:, SC_OUT + half * P:SC_OUT + (half + 1) * P],
                             yz[:, half, :, :].rearrange("p i l -> p (i l)"), start=(half == 0), stop=(half == 1))
            m.then_inc(sem("o_ps"), 1)

        def dve_res(e, p, q):
            e.wait_ge(sem("o_ps"), p + 1)
            e.tensor_tensor(xs[:, cols(p)], xs[:, cols(p)], ps_F[1][:], ALU.add).then_inc(sem("res"), 1)
            e.wait_ge(sem("res"), p + 1 + NPAIR)

        def piece(e, table, token, p, q):
            name, _, arg = token.partition(":")
            front, fn = table[name]
            if front:
                return fn(e, p + 1, 1 - q, *map(int, arg))
            if name in ("out", "res"):
                return fn(e, p - 1, 1 - q)
            at, args = arg[0], map(int, arg[1:])
            pair, par, i = {"l": (p - 1, 1 - q, 1), "a": (p, q, 0), "b": (p, q, 1), "n": (p + 1, 1 - q, 0)}[at]
            fn(e, pair, par, i, *args)

        PE = dict(center=(1, pe_center), var=(1, pe_var), conv=(1, pe_conv), z=(1, pe_z), xproj=(1, pe_xproj),
                  dt=(1, pe_dt), B=(0, pe_B), C=(0, pe_C), sum=(0, pe_sum), out=(0, pe_out))
        ACTE = dict(square=(1, act_square), lnv=(1, act_lnv), rstd=(1, act_rstd), xh=(1, act_xh), th=(1, act_th),
                    zt=(1, act_zt), high=(1, act_high), rank8=(1, act_rank8), sp_exp=(1, act_sp_exp),
                    sp_ln=(1, act_sp_ln), dA=(0, act_dA), C=(0, act_C))
        DVE = dict(norm=(1, dve_norm), xm=(1, dve_xm), zs=(1, dve_zs), split=(1, dve_split), amin=(1, dve_amin),
                   dt=(1, dve_dt), u=(1, dve_u), mul=(0, dve_mul), scan=(0, dve_scan), gate=(0, dve_gate),
                   res=(0, dve_res))

        def in_order(table, order):
            def slot(e, p, q, prev, nxt):
                for token in order.split():
                    name, _, arg = token.partition(":")
                    ahead = table[name][0] or arg[:1] == "n"
                    behind = name in ("out", "res") or arg[:1] == "l"
                    if (ahead and not nxt) or (behind and not prev):
                        continue
                    piece(e, table, token, p, q)
            return slot

        def first(e, table, order):
            for token in order.split():
                piece(e, table, token, -1, 1)

        def slots(e, slot):
            slot(e, 0, 0, False, True)
            with e.Fori(0, (SLOTS - 2) // 2) as j:
                slot(e, j * 2 + 1, 1, True, True)
                slot(e, j * 2 + 2, 0, True, True)
            slot(e, SLOTS - 1, 1, True, False)

        LAST, LQ = SLOTS - 1, 1

        @block.tensor
        def _(e):
            e.wait_ge(sem("x_in"), 16)
            e.wait_ge(sem("const"), CONSTS)
            for k in range(4):
                wait(e, sem("xT"), k - 1)
                for j in range(4):
                    m = e.transpose(ps_F[k % 2][:, j * P:(j + 1) * P], xtok[:, 4 * k + j, :], ident[:])
                m.then_inc(sem("xT_ps"), 1)
            for k in range(4):
                e.wait_ge(sem("xT"), 4 if k < 2 else 4)
                wait(e, sem("lapx"), k - 1)
                e.matmul(ps_F[k % 2][:].rearrange("p (b l) -> p b l", b=2), tri,
                         ypad[:, 2 * k:2 * k + 2, 1:S + 1], start=True, stop=True).then_inc(sem("lapx_ps"), 1)
            first(e, PE, "center var conv:0 conv:1 z:0 z:1 xproj dt:0 dt:1 "
                         "C:n0 C:n1 C:n2 C:n3 C:n4 C:n5 C:n6 C:n7 B:n0 B:n1")
            slots(e, in_order(PE, PE_ORDER))
            for part in range(4):
                pe_sum(e, LAST, LQ, 1, 1, part)
            pe_out(e, LAST, LQ)
            tail_tensor(e)

        @block.scalar
        def _(e):
            for k in range(4):
                e.wait_ge(sem("xT_ps"), k + 1)
                e.activation(ypad[:, 2 * k:2 * k + 2, 1:S + 1], ps_F[k % 2][:].rearrange("p (b l) -> p b l", b=2),
                             ACT.Copy).then_inc(sem("xT"), 1)
            for k in range(4):
                e.wait_ge(sem("lapx_ps"), k + 1)
                e.activation(lapx[:, 2 * k:2 * k + 2, :], ps_F[k % 2][:].rearrange("p (b l) -> p b l", b=2),
                             ACT.Copy).then_inc(sem("lapx"), 1)
            e.wait_ge(sem("alog_in"), 16)
            e.activation(A_all[:], A_all[:], ACT.Exp).then_inc(sem("A"), 1)
            e.wait_ge(sem("A"), 1)
            e.activation(A_all[:], A_all[:], ACT.Copy, scale=-1.0).then_inc(sem("A"), 1)
            e.wait_ge(sem("A"), 2)
            first(e, ACTE, "square lnv rstd xh:0 xh:1 th zt:0 zt:1 high rank8 "
                           "C:n0 C:n1 C:n2 C:n3 C:n4 C:n5 C:n6 C:n7 sp_exp sp_ln dA:n00 dA:n01 dA:n02 dA:n03")
            slots(e, in_order(ACTE, ACT_ORDER))
            tail_scalar(e)

        @block.vector
        def _(e):
            y = ypad[:, :, 1:S + 1]
            count = [0]

            def du(ins):
                count[0] += 1
                ins.then_inc(sem("du"), 1)
                e.wait_ge(sem("du"), count[0])

            def per_batch(j):
                return zb[:, j, :].unsqueeze(2).to_broadcast([P, B, S])

            xs3 = xs[:].rearrange("p (b l) -> p b l", b=B)
            e.wait_ge(sem("xT"), 4)
            du(e.tensor_copy(ypad[:, :, 0:1], ypad[:, :, 2:3]))
            du(e.tensor_copy(ypad[:, :, S + 1:S + 2], ypad[:, :, S - 1:S]))
            du(e.tensor_tensor(lapy, ypad[:, :, 0:S], ypad[:, :, 2:S + 2], ALU.add))
            du(e.scalar_tensor_tensor(out=lapy, in0=y, scalar=-2.0, in1=lapy, op0=ALU.mult, op1=ALU.add))
            e.wait_ge(sem("z_in"), 48)
            du(e.tensor_tensor(lapy, lapy, per_batch(1), ALU.mult))
            du(e.tensor_scalar(grow, y, -1.0, 1.0, ALU.mult, ALU.add))
            du(e.tensor_tensor(grow, grow, y, ALU.mult))
            du(e.tensor_tensor(grow, grow, per_batch(2), ALU.mult))
            du(e.tensor_tensor(grow, grow, lapy, ALU.add))
            e.wait_ge(sem("lapx"), 4)
            du(e.tensor_tensor(lapx, lapx, per_batch(0), ALU.mult))
            du(e.tensor_tensor(xs3, lapx, grow, ALU.add))
            e.sem_inc(sem("res"), NPAIR)
            e.wait_ge(sem("const"), CONSTS)
            with e.Fori(0, LAYERS) as L:
                e.wait_ge(sem("raw"), 80 * L + 80)
                e.scalar_tensor_tensor(out=bunF[:, 0:FC_Z].rearrange("p (k e) -> p k e", k=TAPS),
                                       in0=raw_in.unsqueeze(1).to_broadcast([P, TAPS, 2 * P]), scalar=0.5,
                                       in1=raw_cw.rearrange("p (k e) -> p k e", k=TAPS),
                                       op0=ALU.mult, op1=ALU.mult).then_inc(sem("bun"), 1)
                e.tensor_scalar(bunF[:, FC_CB:FC_END], raw_sm[:, 0:HALVES], 0.5, None, ALU.mult
                                ).then_inc(sem("bun"), 1)
                for half in range(HALVES):
                    e.tensor_scalar(bunS[:, SC_D + half * P:SC_D + (half + 1) * P], ident[:],
                                    raw_sm[:, HALVES + half:HALVES + half + 1], None, ALU.mult
                                    ).then_inc(sem("bun"), 1)
                e.tensor_scalar(bunS[:, SC_OUT:SC_END], raw_out, 0.5, None, ALU.mult).then_inc(sem("bun"), 1)
            e.wait_ge(sem("ln_in"), 32)
            first(e, DVE, "norm xm zs:0 zs:1 split amin:0 amin:1 dt u")
            slots(e, in_order(DVE, DVE_ORDER))
            dve_gate(e, LAST, LQ, 1)
            dve_res(e, LAST, LQ)
            tail_vector(e)


PE_ORDER = """
B:a2 B:a3 C:b0 center var sum:l10 sum:l11 sum:l12 sum:l13 C:b1 B:b0 B:b1 C:b2 conv:0 C:b3 conv:1
B:b2 C:b4 B:b3 C:b5 z:0 sum:a00 C:b6 z:1 sum:a01 C:b7 sum:a02 xproj out sum:a03 dt:0 sum:a10 C:n0
dt:1 C:n1 sum:a11 C:n2 sum:a12 C:n3 sum:a13 C:n4 B:n0 B:n1 C:n5 sum:b00 sum:b01 C:n6 sum:b02 sum:b03
C:n7"""
ACT_ORDER = """
square dA:a10 lnv C:b0 rstd dA:a11 C:b1 dA:a12 C:b2 dA:a13 dA:b00 xh:0 C:b3 dA:b01 C:b4 xh:1 th C:b5
dA:b02 C:b6 zt:0 zt:1 dA:b03 dA:b10 high C:b7 rank8 dA:b11 dA:b12 dA:b13 C:n0 C:n1 sp_exp C:n2 sp_ln
C:n3 C:n4 C:n5 dA:n00 dA:n01 C:n6 dA:n02 C:n7 dA:n03"""
DVE_ORDER = """
mul:a00 mul:a01 mul:a10 mul:a11 mul:a20 mul:a21 mul:a30 mul:a31 scan:a0 norm gate:l mul:b00 mul:b01
mul:b10 mul:b11 scan:a1 mul:b20 mul:b21 xm mul:b30 mul:b31 zs:0 zs:1 scan:b0 res split amin:0 amin:1
scan:b1 gate:a dt u"""
PRE = 3
SUM_PARTS = [range(PRE + 3 * part, PRE + 3 * part + 3 + (part == 3)) for part in range(4)]
CONSTS = 16

def laid_out(a):
    import numpy as np

    def halves_first(w):
        n = w.shape[2]
        return w.reshape(LAYERS, HALVES, P, n).transpose(0, 2, 1, 3).reshape(LAYERS, P, HALVES * n)

    in_t = a["L0_attn_in_proj_w"].transpose(0, 2, 1)
    xp = a["L0_attn_x_proj_w"].transpose(0, 2, 1)
    xp = np.concatenate([xp[:, :, RANK:]] * 3 + [xp[:, :, :RANK]], axis=2)
    col = lambda n: a[n].reshape(LAYERS, HALVES, P).transpose(0, 2, 1)
    return {
        "in_w": in_t[:, :, :2 * P],
        "conv_w": a["L0_attn_conv_w"].transpose(0, 2, 1),
        "zxp_w": np.concatenate([in_t[:, :, 2 * P:], halves_first(xp), col("L0_attn_dt_proj_b")], axis=2),
        "out_w": halves_first(a["L0_attn_out_proj_w"].transpose(0, 2, 1)),
        "small": np.concatenate([col("L0_attn_conv_b"), col("L0_attn_D_skip")], axis=2),
        "dt_w": a["L0_attn_dt_proj_w"].transpose(0, 2, 1),
        "b1c": a["L0_cond2_b1"].reshape(FC, P).T,
        "cw": a["L1_cond2_weight"].transpose(0, 2, 1),
        "f1t": a["L1_ffn_w1"].T,
        "f2t": a["L1_ffn_w2"].T.reshape(FC, P, P).transpose(1, 0, 2).reshape(P, FF),
        "A_log": a["L0_attn_A_log"].reshape(LAYERS, HALVES, P, NS).transpose(2, 0, 1, 3).reshape(P, -1),
    }


def constants():
    import numpy as np
    j, l = np.arange(S)[:, None], np.arange(S)[None, :]
    keep = np.stack([l <= j, l >= j, l != j])
    by_part = keep.reshape(3, 2, P, S).transpose(2, 0, 1, 3)
    return {
        "iota8": (100 + np.arange(NE)).astype(np.float32),
        "pmask": np.where(by_part, 0, -BIG).astype(np.float32).reshape(P, -1),
        "pcnt": by_part.sum(-1).astype(np.float32).reshape(P, -1),
        "cmask": np.where(np.arange(P)[None, :] <= np.arange(P)[:, None], 0, -BIG).astype(np.float32),
    }


SAME = ["x", "condB_zX", "condB_zY", "condB_zR", "itok_B_0_7", "itok_B_0_2", "L0_attn_ln_g", "L0_attn_ln_b",
        "L0_cond2_W1", "L0_cond2_W2", "L0_cond2_b2", "L0_cond2_We", "L0_cond2_be", "L0_ffn_gate_kernel",
        "L0_ffn_w0", "L0_ffn_w1", "L0_ffn_wo", "L1_cond_W1", "L1_cond_b1", "L1_cond_v", "L1_attn_w_kv_down",
        "L1_attn_w_kv_up", "L1_attn_w_q", "L1_attn_w_out", "L1_cond2_bias"]


def kernel(**inputs):
    import numpy as np
    import concourse.bacc as bacc
    from concourse.bass_utils import run_bass_kernel_spmd

    nc = bacc.Bacc("TRN2", target_bir_lowering=False, num_devices=1)
    given = {n: np.asarray(v) for n, v in inputs.items()}
    arrays = {n: np.ascontiguousarray(v) for n, v in {**{n: given[n] for n in SAME}, **laid_out(given), **constants()}.items()}
    io = {n: nc.dram_tensor(f"in_{n}", v.shape, mybir.dt.from_np(v.dtype), kind="ExternalInput").ap()
          for n, v in arrays.items()}
    io["out"] = nc.dram_tensor("out_x", (B, S, D), F32, kind="ExternalOutput").ap()
    program(nc, io)
    r = run_bass_kernel_spmd(nc, [{f"in_{n}": v for n, v in arrays.items()}], core_ids=[0])
    return r.results[0]["out_x"]
```

```python
from contextlib import ExitStack

import concourse.bass as bass
from concourse import mybir

F32 = mybir.dt.float32
BF16 = mybir.dt.bfloat16
I32 = mybir.dt.int32
U32 = mybir.dt.uint32
ALU = mybir.AluOpType
ACT = mybir.ActivationFunctionType
AX_X = mybir.AxisListType.X

P = 128
B, S, D = 8, 256, 128
TOK = B * S
NT = TOK // P
HALVES = 2
NS = 16
RANK = 8
TAPS = 4
LAYERS = 4
PAIR = 2 * S
NPAIR = B // 2
SLOTS = LAYERS * NPAIR
LN_EPS = 1e-5
Q_EPS = 1e-5
BIG = 1.0e30
FF = 512
FC = FF // P
NE = 8
MC = 96
NH, HS = 16, 64
HD = NH * HS
SCALE = HS ** -0.5
TRI = 3 * P
ROUND = 1.5 * 2 ** 23
RT, RT_DIFF = 18, 12

XPN = 3 * 2 * NS + RANK
BC3 = 3 * 2 * NS
FC_TAP = 0
FC_Z = TAPS * 2 * P
FC_XP = FC_Z + 2 * P
FC_DTB = FC_XP + HALVES * XPN
FC_CB = FC_DTB + HALVES
FC_END = FC_CB + HALVES
SC_D = 0
SC_OUT = HALVES * P
SC_END = SC_OUT + HALVES * P


def wait(eng, sem, value):
    if isinstance(value, int) and value <= 0:
        return
    eng.wait_ge(sem, value)


def program(nc, io):
    with ExitStack() as ctx:
        def sb(name, shape, dt=F32):
            return ctx.enter_context(nc.sbuf_tensor(name, shape, dt))

        def pb(name, shape, dt=F32):
            return ctx.enter_context(nc.psum_tensor(name, shape, dt))

        sems = {}

        def sem(name):
            if name not in sems:
                sems[name] = ctx.enter_context(nc.semaphore(name))
            return sems[name]

        banks = pb("banks", [P, 8, 512])
        ps_B = [banks[:, 2 * i:2 * i + 2, :].rearrange("p a (b l) -> p (a b) l", b=2) for i in range(2)]
        ps_C = banks[:, 4, :].rearrange("p (a l) -> p a l", a=2)
        ps_Y = banks[:, 5, :].rearrange("p (a l) -> p a l", a=2)
        ps_F = [banks[:, 6 + i, :] for i in range(2)]

        ident = sb("ident", [P, P])
        mean_w = sb("mean_w", [P, P])
        center_w = sb("center_w", [P, P])
        ypad = sb("ypad", [P, B, S + 2])
        xs = sb("xs", [P, TOK])

        zb = sb("zb", [P, 3, B])
        lng = sb("lng", [P, 1])
        lnb = sb("lnb", [P, 1])
        eps = sb("eps", [P, 1])
        sel = sb("sel", [BC3, 2 * NS, P], BF16)
        h = [sb(f"h{i}", [P, NS, S]) for i in range(4)]
        dA = [sb(f"dA{i}", [P, NS, S]) for i in range(2)]
        Cb = [sb(f"Cb{i}", [P, NS, S]) for i in range(2)]
        wF = sb("wF", [P, FC_END])
        wS = sb("wS", [P, SC_END])
        wdt = sb("wdt", [P, HALVES * P])
        A_all = sb("A_all", [P, LAYERS, HALVES * NS])
        A_cur = [sb(f"A_cur{i}", [P, HALVES * NS]) for i in range(2)]
        xm = [sb(f"xm{i}", [P, HALVES, PAIR]) for i in range(2)]
        zs = [sb(f"zs{i}", [P, HALVES, PAIR]) for i in range(2)]
        dt = sb("dt", [P, HALVES, PAIR])
        u = sb("u", [P, HALVES, PAIR])
        bc = [sb(f"bc{i}", [BC3, PAIR], BF16) for i in range(2)]
        xc = sb("xc", [P, PAIR])
        rstd = sb("rstd", [P, PAIR])
        xn = sb("xn", [P, 2, S + TAPS - 1])
        xh = sb("xh", [P, HALVES, PAIR])
        th = sb("th", [P, HALVES, PAIR])
        yz = sb("yz", [P, HALVES, 2, S])
        ids = sb("ids", [1, B], I32)
        smx2 = sb("smx2", [P, 2, NH])
        r1 = xc[0:BC3, :]
        r2 = th[0:BC3, 0, 0:PAIR // 2].bitcast(BF16)
        tri = Cb[0][:, 0, 0:P]
        dt8 = rstd[BC3:BC3 + RANK, :]

        flat = [t[:, :, :].rearrange("p a b -> p (a b)") for t in (*h, *dA)]
        widths = (2 * P, TAPS * 2 * P, HALVES * P, 2 * HALVES, FC_END, SC_END)
        raw_in, raw_cw, raw_out, raw_sm, bunF, bunS = (
            flat[3][:, sum(widths[:i]):sum(widths[:i + 1])] for i in range(len(widths)))
        xtok = flat[2][:, 0:TOK].rearrange("p (a b) -> p a b", a=NT)
        lapx, lapy = (flat[0][:, k * TOK:(k + 1) * TOK].rearrange("p (a b) -> p a b", a=B) for k in range(2))
        grow = flat[1][:, 0:TOK].rearrange("p (a b) -> p a b", a=B)
        scrF = nc.dram_tensor("scrF", [LAYERS, P, FC_END], F32).ap()
        scrS = nc.dram_tensor("scrS", [LAYERS, P, SC_END], F32).ap()

        out_tok = io["out"].rearrange("b (c p) f -> p (b c) f", p=P)
        x_tok = io["x"].rearrange("b (c p) f -> p (b c) f", p=P)

        def layer_of(ap, L):
            return ap[bass.ds(L, 1)].rearrange("l p n -> (l p) n")


        a_h0, a_h1, a_h2, a_h3, a_dA0, a_dA1, a_Cb0, a_Cb1 = (
            t[:, :, :].rearrange("p a b -> p (a b)") for t in (*h, *dA, *Cb))

        def carve(area, *widths):
            at, got = 0, []
            for w in widths:
                got.append(area[:, at:at + w])
                at += w
            assert at <= area.shape[1], (at, area.shape)
            return got

        def fold(ap, a):
            return ap.rearrange("p (a b) -> p a b", a=a)

        xcF, rsF = a_h2[:, 0:TOK], a_h3[:, 0:TOK]
        xt_, rT = carve(a_Cb0, TOK, TOK)
        xt = fold(xt_, NT)
        mW1, mWa, mWb, mHa, mHb, mBias, mB1 = carve(a_Cb1, FF, FF, FF, FC * S, FC * S, B, FC)
        mWcat, mH = [fold(mWa, FC), fold(mWb, FC)], [fold(mHa, FC), fold(mHb, FC)]
        gw, lg_, io_, oh1_, oh2_, tmp_, m1, m2, i1, w1_, w2_, dn = carve(
            a_dA1, NE, NT * NE, NE, NT * NE, NT * NE, NT * NE, NT, NT, NT, NT, NT, NT)
        lg, oh1, oh2, tmp = (fold(t, NT) for t in (lg_, oh1_, oh2_, tmp_))
        ex = []
        for area in (a_h0, a_h1):
            a0, a1, ao = carve(area, FF, FF, FF)
            ex.append((a0, a1, fold(ao, FC)))
        sil = carve(a_h1[:, 3 * FF:], 512, 512)
        inter = [fold(t, FC) for t in carve(a_h2, FC * 512, FC * 512)]
        x2T, at_ = carve(a_h3, TOK, TOK)
        pm_, PT0, PT1, PT2, PT3, fq2T_, fo_, pcnt, pone, pcb, pmx, psm, prc, pcf = carve(
            a_dA0, 3 * PAIR, *[TRI] * 4, FF, S, 3 * 2, 3 * B, 2 * B, 2, 2, 4, B)
        PT = [PT0, PT1, PT2, PT3]
        one = fold(pone, 3)
        cnt_b = fold(pcb, B)
        Sall = a_dA1[:, 2048:4096]
        pStage_, pTb, cW1, cv, cb1, cid = carve(a_dA1[:, 1024:1728], S, S, 32, P, 1, B)
        pStage = fold(pStage_, 2)
        Wk, Wv, Wq, Wo_ = carve(a_h0, HD, HD, HD, 8 * P)
        Wo = fold(Wo_, 8)
        Wd, latT, V_, ssum, sinv, smx, _, pM_, pPT_, pT2 = carve(
            a_h1, P, S, 2 * HD, 2 * NH, 2 * NH, 2 * NH, 2 * NH, PAIR, PAIR, PAIR)
        V, pM, pPT, pMt = fold(V_, 2), fold(pM_, 2), fold(pPT_, 2), fold(pT2, 2)
        qT, kT = (fold(t, 8) for t in carve(a_h2, 8 * S, 8 * S))
        Pr0, Pr1, Pr2, Pr3, fg_, ft2_, fq2_ = carve(a_h3, *[TRI] * 4, 2 * FF, 2 * FF, FF)
        Pr = [Pr0, Pr1, Pr2, Pr3]
        sums, inv, negm = (t.rearrange("p (a b) -> p a b", a=2) for t in (ssum, sinv, smx))
        y_, yT_ = carve(a_Cb1, 2 * HD, 8 * S)
        y, yT = fold(y_, 2), fold(yT_, 8)
        idb, cmask = (t.bitcast(BF16) for t in carve(a_dA1[:, 1728:], P // 2, P // 2))
        cmraw = a_dA1[:, 1728 + P:1728 + 2 * P]
        f1raw, f2raw, f1q_, f2q_, fcw, fcb = carve(xs[:, :], FF, FF, FF // 2, FF // 2, P, P)
        f1q, f2q = f1q_.bitcast(BF16), fold(f2q_.bitcast(BF16), FC)
        fsc = yz[:].rearrange("p a b c -> p (a b c)")
        fsm, fst_ = carve(fsc, 64, S)
        fst = fold(fst_, 2)
        fx3T, fc = u[:, 0, 0:S], fold(u[:, 0, S:2 * S], 2)
        ft = fold(dt[:, 0, 0:S], 2)
        fq = fold(dt[:, 0, S:S + S // 2].bitcast(BF16), 2)
        fqT = dt[:, 0, S + S // 2:2 * S].bitcast(BF16)
        fg, ft2, fq2 = fold(fg_, 2), fold(ft2_, 2), fold(fq2_.bitcast(BF16), 2)
        fq2T = fq2T_.bitcast(BF16).rearrange("p (t c k) -> p t c k", t=2, c=FC)
        fo = fold(fo_, 2)
        fr = fold(fsm[:, 0:8], 4)

        def bank(k, n=512):
            return banks[:, k, 0:n]

        class Chain:
            def __init__(self, e, name, base=0):
                self.e, self.name, self.base, self.k = e, name, base, 0

            def __call__(self, ins):
                self.k += 1
                ins.then_inc(sem(self.name), 1)

            def sync(self):
                self.e.wait_ge(sem(self.name), self.base + self.k)

        def tail_sync(e):
            e.wait_ge(sem("res"), SLOTS + NPAIR)

            def dma(dst, src, name):
                e.dma_start(dst, src).then_inc(sem(name), 16)

            dma(ids[:], io["itok_B_0_7"].rearrange("(a b) -> a b", a=1), "ids_in")
            dma(mW1, io["L0_cond2_W1"], "mw_in")
            dma(mB1, io["b1c"], "mw_in")
            for k in range(2):
                dma(mWcat[k][:, :, 0:MC], io["L0_cond2_W2"].rearrange("(c p) o -> p c o", p=P), "mw_in")
            dma(mBias[0:MC, :], bass.AP(io["L0_cond2_b2"].tensor, 0, [[1, MC], [0, B], [1, 1]]), "mw_in")
            dma(pm_, io["pmask"], "pc_in")
            dma(pcnt, io["pcnt"], "pc_in")
            dma(cW1, io["L1_cond_W1"], "pc_in")
            dma(cb1[0:32, :], io["L1_cond_b1"].rearrange("(p a) -> p a", a=1), "pc_in")
            dma(cv[0:32, :], bass.AP(io["L1_cond_v"].tensor, 0, [[1, 32], [0, P], [1, 1]]), "pc_in")
            dma(cid.bitcast(I32), bass.AP(io["itok_B_0_2"].tensor, 0, [[0, P], [1, B]]), "pc_in")
            dma(cmraw, io["cmask"], "pc_in")
            e.wait_ge(sem("ids_in"), 16)
            with e.Fori(0, B // 2) as j:
                for q in range(2):
                    b = j * 2 + q
                    sid = e.value_load(ids[0:1, bass.ds(b, 1)], min_val=0, max_val=NE - 1)
                    e.wait_ge(sem("rT"), b + 7)
                    dma(mWcat[q][:, :, MC:P],
                        io["L0_cond2_We"][bass.ds(sid, 1)].rearrange("a (c p) o -> p (a c) o", p=P), f"we{q}")
                    dma(mBias[MC:P, bass.ds(b, 1)],
                        io["L0_cond2_be"][bass.ds(sid, 1)].rearrange("a o -> o a"), f"we{q}")
            dma(gw, io["L0_ffn_gate_kernel"], "gw_in")
            dma(io_, bass.AP(io["iota8"].tensor, 0, [[0, P], [1, NE]]), "gw_in")

            def expert(x, k):
                a0, a1, ao = ex[k]
                dma(a0, layer_of(io["L0_ffn_w0"], x), f"ex{k}")
                dma(a1, layer_of(io["L0_ffn_w1"], x), f"ex{k}")
                dma(ao, io["L0_ffn_wo"][bass.ds(x, 1)].rearrange("a (c p) o -> p (a c) o", p=P), f"ex{k}")

            expert(0, 0)
            expert(1, 1)
            e.wait_ge(sem("rT"), B + 8)
            dma(f1raw, io["f1t"], "fw_in")
            dma(f2raw, io["f2t"], "fw_in")
            with e.Fori(1, NE // 2) as j:
                for k in range(2):
                    e.wait_ge(sem("mo_dn"), 8 * j - 4 + 4 * k)
                    expert(j * 2 + k, k)
            e.wait_ge(sem("mo_dn"), 4 * (NE - 1))
            dma(Wk, io["L1_attn_w_kv_up"][:, 0:HD], "aw_in")
            dma(Wv, io["L1_attn_w_kv_up"][:, HD:2 * HD], "aw_in")
            dma(Wq, io["L1_attn_w_q"], "aw_in")
            dma(Wo, io["L1_attn_w_out"].rearrange("(c p) o -> p c o", p=P), "aw_in")
            e.wait_ge(sem("mo_dn"), 4 * NE)
            dma(Wd, io["L1_attn_w_kv_down"], "aw_in")
            e.sem_inc(sem("out"), 16)

            def conditioned(b):
                sid = e.value_load(ids[0:1, bass.ds(b, 1)], min_val=0, max_val=NE - 1)
                wait(e, sem("f_c"), b)
                dma(fcw, layer_of(io["cw"], sid), "cw")
                dma(fcb, bass.AP(io["L1_cond2_bias"].tensor, sid * P, [[0, P], [1, P]]), "cw")

            def result(b):
                e.wait_ge(sem("f_o"), 2 * b + 4)
                dma(out_tok[:, bass.ds(b * 2, 2), :], fo, "out")

            conditioned(0)
            with e.Fori(0, B - 1) as b:
                conditioned(b + 1)
                result(b)
            result(B - 1)
            e.wait_ge(sem("out"), 16 * B + 16)

        def tail_gpsimd(e):
            e.wait_ge(sem("pone"), 1)
            run(e, "gp", ATT_GP)

        def tail_tensor(e):
            for k in range(4):
                e.wait_ge(sem("res"), SLOTS + 1 + k)
                e.matmul(bank(k), center_w[:], xs[:, k * 512:(k + 1) * 512], start=True, stop=True
                         ).then_inc(sem("fm"), 1)
            for k in range(4):
                e.wait_ge(sem("fsq"), k + 1)
                e.matmul(bank(4 + k), mean_w[:], rsF[:, k * 512:(k + 1) * 512], start=True, stop=True
                         ).then_inc(sem("fv"), 1)
            for k in range(4):
                e.wait_ge(sem("x1"), k + 1)
                for j in range(4):
                    c = (4 * k + j) * P
                    m = e.transpose(bank(k)[:, j * P:(j + 1) * P], xs[:, c:c + P], ident[:])
                m.then_inc(sem("x1t_ps"), 1)

            def up(b, q):
                wait(e, sem("gelu"), 4 * b - 4)
                for c in range(FC):
                    m = e.matmul(fold(banks[:, 2 * q + c // 2, :], 2)[:, c % 2, :], mW1[:, c * P:(c + 1) * P],
                                 xs[:, bass.ds(b * S, S)], start=True, stop=True)
                m.then_inc(sem("up"), 1)

            def down(b, j, q):
                e.wait_ge(sem("gelu"), 4 * b + 4)
                e.wait_ge(sem(f"we{q}"), 32 * j + 32)
                e.wait_ge(sem("rT"), b + 7)
                for c in range(FC):
                    m = e.matmul(bank(4 + q, S), mWcat[q][:, c, :], mH[q][:, c, :], start=(c == 0), stop=(c == 3))
                m.then_inc(sem("dn"), 1)

            e.wait_ge(sem("mw_in"), 80)
            e.wait_ge(sem("x1t"), 4)
            up(0, 0)
            with e.Fori(0, B // 2 - 1) as j:
                up(j * 2 + 1, 1)
                down(j * 2, j, 0)
                up(j * 2 + 2, 0)
                down(j * 2 + 1, j, 1)
            up(B - 1, 1)
            down(B - 2, B // 2 - 1, 0)
            down(B - 1, B // 2 - 1, 1)

            e.wait_ge(sem("rT"), 8 + B)
            e.wait_ge(sem("gw_in"), 32)
            for t in range(NT):
                m = e.matmul(bank(6)[:, t * NE:(t + 1) * NE], rT[:, t * P:(t + 1) * P], gw, start=True, stop=True)
            m.then_inc(sem("lg_ps"), 1)

            def ex_up(G, g, k):
                for c in range(FC):
                    X = G * 4 + c
                    wait(e, sem("mo_int"), X - 1)
                    for w in range(2):
                        m = e.matmul(bank(2 * (c % 2) + w), ex[k][w][:, c * P:(c + 1) * P],
                                     rT[:, g * 512:(g + 1) * 512], start=True, stop=True)
                    m.then_inc(sem("mo_up"), 1)

            def ex_down(G, g, k):
                e.wait_ge(sem("mo_int"), 4 * G + 4)
                wait(e, sem("mo_acc"), 4 * G - 4)
                for j in range(4):
                    for c in range(FC):
                        m = e.matmul(bank(6 + g % 2)[:, j * P:(j + 1) * P], inter[g % 2][:, c, j * P:(j + 1) * P],
                                     ex[k][2][:, c, :], start=(c == 0), stop=(c == 3))
                m.then_inc(sem("mo_dn"), 1)

            def ex_body(j, first):
                for k in range(2):
                    e.wait_ge(sem(f"ex{k}"), 48 * j + 48)
                    for g in range(4):
                        G = j * 8 + k * 4 + g
                        ex_up(G, g, k)
                        if not (first and k == 0 and g == 0):
                            ex_down(G - 1, (g - 1) % 4, k if g else 1 - k)

            e.wait_ge(sem("lg"), 1)
            ex_body(0, True)
            e.wait_ge(sem("fwa"), 2)
            e.matmul(bank(4, 2), mean_w[:], fsm[:, 8:10], start=True, stop=True).then_inc(sem("fws_ps"), 1)
            with e.Fori(1, NE // 2) as j:
                ex_body(j, False)
            ex_down(4 * NE - 1, 3, 1)

            e.wait_ge(sem("mo_acc"), 4 * NE * 4)
            for k in range(4):
                for j in range(4):
                    m = e.transpose(bank(k)[:, j * P:(j + 1) * P], xt[:, 4 * k + j, :], ident[:])
                m.then_inc(sem("x2T_ps"), 1)
            e.wait_ge(sem("pc_in"), 112)
            for k in range(4):
                e.wait_ge(sem("x2T"), k + 1)
                e.matmul(bank(4 + k)[0:32, :], cW1, x2T[:, k * 512:(k + 1) * 512], start=True, stop=True
                         ).then_inc(sem("at_ps"), 1)
            for k in range(4):
                e.wait_ge(sem("at"), k + 1)
                e.matmul(bank(k), cv[0:32, :], at_[0:32, k * 512:(k + 1) * 512], start=True, stop=True
                         ).then_inc(sem("S_ps"), 1)
            e.wait_ge(sem("Sall"), 4)
            e.wait_ge(sem("aw_in"), 80)
            e.wait_ge(sem("acon"), 1)
            e.wait_ge(sem("fwq"), 9)
            run(e, "pe", ATT_PE)

        def tail_scalar(e):
            for k in range(4):
                e.wait_ge(sem("fm"), k + 1)
                e.activation(rsF[:, k * 512:(k + 1) * 512], bank(k), ACT.Square).then_inc(sem("fsq"), 1)
            for k in range(4):
                e.wait_ge(sem("fv"), k + 1)
                e.activation(rsF[:, k * 512:(k + 1) * 512], bank(4 + k), ACT.Ln, bias=eps[:, 0:1]).then_inc(sem("frs"), 1)
            for k in range(4):
                e.wait_ge(sem("frs"), 4 + k)
                e.activation(rsF[:, k * 512:(k + 1) * 512], rsF[:, k * 512:(k + 1) * 512], ACT.Exp, scale=-0.5
                             ).then_inc(sem("frs"), 1)
            for k in range(4):
                e.wait_ge(sem("x1t_ps"), k + 1)
                e.activation(xt_[:, k * 512:(k + 1) * 512], bank(k), ACT.Copy).then_inc(sem("x1t"), 1)

            def gelu(b, q):
                e.wait_ge(sem("up"), b + 1)
                wait(e, sem("dn"), b - 1)
                for c in range(FC):
                    e.activation(mH[q][:, c, :], fold(banks[:, 2 * q + c // 2, :], 2)[:, c % 2, :], ACT.Gelu,
                                 bias=mB1[:, c:c + 1]).then_inc(sem("gelu"), 1)

            e.wait_ge(sem("mw_in"), 80)
            gelu(0, 0)
            gelu(1, 1)
            with e.Fori(1, B // 2) as j:
                gelu(j * 2, 0)
                gelu(j * 2 + 1, 1)

            def silu(G, first):
                for c in range(FC):
                    X = G * 4 + c
                    e.wait_ge(sem("mo_up"), X + 1)
                    if not (first and c < 2):
                        e.wait_ge(sem("mo_int"), X - 1)
                    e.activation(sil[c % 2], bank(2 * (c % 2)), ACT.Silu).then_inc(sem("mo_sil"), 1)

            silu(0, True)
            silu(1, False)
            e.wait_ge(sem("rt"), RT_DIFF)
            e.activation(w2_, dn, ACT.Exp).then_inc(sem("rexp"), 1)
            silu(2, False)
            with e.Fori(3, 4 * NE) as G:
                silu(G, False)

            for k in range(4):
                e.wait_ge(sem("x2T_ps"), k + 1)
                e.activation(x2T[:, k * 512:(k + 1) * 512], bank(k), ACT.Copy).then_inc(sem("x2T"), 1)
            for k in range(4):
                e.wait_ge(sem("at_ps"), k + 1)
                e.activation(at_[0:32, k * 512:(k + 1) * 512], bank(4 + k)[0:32, :], ACT.Tanh, bias=cb1[0:32, :]
                             ).then_inc(sem("at"), 1)
            for k in range(4):
                e.wait_ge(sem("S_ps"), k + 1)
                e.activation(Sall[:, k * 512:(k + 1) * 512], bank(k), ACT.Copy).then_inc(sem("Sall"), 1)
            run(e, "act", ATT_ACT)

        def tail_vector(e):
            for k in range(4):
                e.wait_ge(sem("frs"), 5 + k)
                c = slice(k * 512, (k + 1) * 512)
                e.scalar_tensor_tensor(out=xcF[:, c], in0=bank(k), scalar=lng[:, 0:1], in1=rsF[:, c],
                                       op0=ALU.mult, op1=ALU.mult).then_inc(sem("fx1"), 1)
                e.wait_ge(sem("fx1"), k + 1)
                e.scalar_tensor_tensor(out=fold(xs[:, c], 2), in0=fold(xcF[:, c], 2), scalar=lnb[:, 0:1],
                                       in1=ypad[:, 2 * k:2 * k + 2, 1:S + 1], op0=ALU.add, op1=ALU.add
                                       ).then_inc(sem("x1"), 1)
            pooling_constants(e)
            e.sem_inc(sem("rT"), 8)
            e.wait_ge(sem("mw_in"), 80)
            with e.Fori(0, B // 2) as j:
                for q in range(2):
                    b = j * 2 + q
                    e.wait_ge(sem("dn"), b + 1)
                    e.wait_ge(sem(f"we{q}"), 32 * j + 32)
                    e.tensor_scalar(rT[:, bass.ds(b * S, S)], bank(4 + q, S), mBias[:, bass.ds(b, 1)], None, ALU.add
                                    ).then_inc(sem("rT"), 1)

            r = Chain(e, "rt")

            def each(ap):
                return ap.unsqueeze(2).to_broadcast([P, NT, NE])

            iota = io_.unsqueeze(1).to_broadcast([P, NT, NE])

            def top(m, oh):
                r(e.tensor_reduce(m, lg, AX_X, ALU.max)); r.sync()
                r(e.tensor_tensor(tmp, lg, each(m), ALU.is_equal)); r.sync()
                r(e.scalar_tensor_tensor(out=tmp, in0=tmp, scalar=-100.0, in1=iota, op0=ALU.mult, op1=ALU.add)); r.sync()
                r(e.tensor_reduce(i1, tmp, AX_X, ALU.min)); r.sync()
                r(e.tensor_tensor(oh, tmp, each(i1), ALU.is_equal)); r.sync()

            e.wait_ge(sem("lg_ps"), 1)
            e.tensor_copy(lg, fold(bank(6, NT * NE), NT)).then_inc(sem("lg"), 1)
            e.wait_ge(sem("lg"), 1)
            e.wait_ge(sem("gw_in"), 32)

            def choose():
                top(m1, oh1)
                r(e.scalar_tensor_tensor(out=lg, in0=oh1, scalar=-BIG, in1=lg, op0=ALU.mult, op1=ALU.add)); r.sync()
                top(m2, oh2)
                r(e.tensor_tensor(dn, m2, m1, ALU.subtract)); r.sync()

            def weigh():
                e.wait_ge(sem("rexp"), 1)
                r(e.tensor_scalar(dn, w2_, 1.0, None, ALU.add)); r.sync()
                r(e.reciprocal(w1_, dn)); r.sync()
                r(e.tensor_tensor(w2_, w2_, w1_, ALU.mult)); r.sync()
                r(e.tensor_tensor(oh1, oh1, each(w1_), ALU.mult))
                r(e.tensor_tensor(oh2, oh2, each(w2_), ALU.mult)); r.sync()
                r(e.tensor_tensor(oh1, oh1, oh2, ALU.add)); r.sync()
                assert r.k == RT

            def ex_mul(G, g):
                for c in range(FC):
                    e.wait_ge(sem("mo_sil"), G * 4 + c + 1)
                    e.tensor_tensor(inter[g % 2][:, c, :], sil[c % 2], bank(2 * (c % 2) + 1), ALU.mult
                                    ).then_inc(sem("mo_int"), 1)

            def ex_acc(G, g, x):
                e.wait_ge(sem("mo_dn"), G + 1)
                for j in range(4):
                    t = 4 * g + j
                    e.scalar_tensor_tensor(out=xt[:, t, :], in0=bank(6 + g % 2)[:, j * P:(j + 1) * P],
                                           scalar=oh1[:, t, bass.ds(x, 1)], in1=xt[:, t, :], op0=ALU.mult, op1=ALU.add
                                           ).then_inc(sem("mo_acc"), 1)

            def ex_body(j, first):
                for k in range(2):
                    for g in range(4):
                        G = j * 8 + k * 4 + g
                        ex_mul(G, g)
                        if first and k == 0 and g < 2:
                            (choose, weigh)[g]()
                        if not (first and k == 0 and g == 0):
                            ex_acc(G - 1, (g - 1) % 4, j * 2 + k - (0 if g else 1))

            e.wait_ge(sem("fw_in"), 32)
            e.tensor_reduce(fsm[:, 8:9], f1raw, AX_X, ALU.add, apply_absolute_value=True).then_inc(sem("fwa"), 1)
            e.tensor_reduce(fsm[:, 9:10], f2raw, AX_X, ALU.add, apply_absolute_value=True).then_inc(sem("fwa"), 1)
            ex_body(0, True)
            weights_levels(e)
            with e.Fori(1, NE // 2) as j:
                ex_body(j, False)
            ex_acc(4 * NE - 1, 3, NE - 1)

            e.sem_inc(sem("f_o"), 2)
            run(e, "dve", ATT_DVE)

        def pooling_constants(e):
            c_ = Chain(e, "pcst")
            e.wait_ge(sem("pc_in"), 112)
            c_(e.tensor_copy(pcf, cid.bitcast(I32))); c_.sync()
            c_(e.tensor_scalar(one[:, 0, :], pcf, 0.0, None, ALU.is_equal))
            c_(e.tensor_scalar(one[:, 1, :], pcf, 1.0, None, ALU.is_equal)); c_.sync()
            c_(e.tensor_tensor(one[:, 2, :], one[:, 0, :], one[:, 1, :], ALU.add)); c_.sync()
            c_(e.tensor_scalar(one[:, 2, :], one[:, 2, :], -1.0, 1.0, ALU.mult, ALU.add)); c_.sync()
            for jc in range(2):
                c_(e.tensor_scalar(cnt_b[:, :, jc], one[:, 0, :], pcnt[:, jc:jc + 1], None, ALU.mult)); c_.sync()
                for k in (1, 2):
                    c_(e.scalar_tensor_tensor(out=cnt_b[:, :, jc], in0=one[:, k, :], scalar=pcnt[:, 2 * k + jc:2 * k + jc + 1],
                                              in1=cnt_b[:, :, jc], op0=ALU.mult, op1=ALU.add)); c_.sync()
            c_(e.tensor_copy(idb, ident[:]))
            c_(e.tensor_copy(cmask, cmraw)); c_.sync()
            e.sem_inc(sem("pone"), 1)
            e.sem_inc(sem("acon"), 1)

        def weights_levels(e):
            w = Chain(e, "fwq")
            e.wait_ge(sem("fws_ps"), 1)
            w(e.tensor_scalar(fsm[:, 10:12], bank(4, 2), 1.0 / FF, Q_EPS, ALU.mult, ALU.max)); w.sync()
            w(e.reciprocal(fsm[:, 12:14], fsm[:, 10:12])); w.sync()
            for k, (raw, dst) in enumerate(((f1raw, f1q_), (f2raw, f2q_))):
                w(e.tensor_scalar(raw, raw, fsm[:, 12 + k:13 + k], ROUND, ALU.mult, ALU.add)); w.sync()
                w(e.tensor_scalar(raw, raw, -ROUND, -1.0, ALU.add, ALU.max)); w.sync()
                w(e.tensor_scalar(dst.bitcast(BF16), raw, 1.0, None, ALU.min)); w.sync()
            w(e.tensor_scalar(fsm[:, 14:16], fsm[:, 10:12], 1.0 / 127.0, None, ALU.mult)); w.sync()

        def gp_stage(e, b):
            e.wait_ge(sem("mo_acc"), 4 * NE * 4)
            wait(e, sem("pT_ps"), b)
            e.tensor_copy(pStage, xt[:, bass.ds(b * 2, 2), :]).then_inc(sem("pst"), 1)

        def gp_mask(e, b):
            wait(e, sem("pPT_ps"), b)
            for k in range(3):
                dst = pM_ if k == 0 else pT2
                if k == 2:
                    e.wait_ge(sem("pmk"), 5 * b + 3)
                e.tensor_tensor(dst, pm_[:, k * PAIR:(k + 1) * PAIR], one[:, k, bass.ds(b, 1)].to_broadcast([P, PAIR]),
                                ALU.mult).then_inc(sem("pmk"), 1)
                if k:
                    e.wait_ge(sem("pmk"), 5 * b + 2 * k)
                    e.tensor_tensor(pM_, pM_, pT2, ALU.add).then_inc(sem("pmk"), 1)
            e.wait_ge(sem("pmk"), 5 * b + 5)
            e.wait_ge(sem("Sall"), 4)
            e.tensor_tensor(pM, pM, Sall[:, bass.ds(b * S, S)].unsqueeze(1).to_broadcast([P, 2, S]), ALU.add
                            ).then_inc(sem("pm"), 1)

        def dve_pmax(e, b):
            e.wait_ge(sem("pm"), b + 1)
            e.tensor_reduce(pmx, pM, AX_X, ALU.max, negate=True).then_inc(sem("pmx"), 1)

        def act_pexp(e, b):
            e.wait_ge(sem("pmx"), b + 1)
            for jc in range(2):
                e.activation(pM[:, jc, :], pM[:, jc, :], ACT.Exp, bias=pmx[:, jc:jc + 1],
                             accum_out=psm[:, jc:jc + 1]).then_inc(sem("pexp"), 1)

        def dve_pnorm(e, b):
            e.wait_ge(sem("pexp"), 2 * b + 2)
            e.tensor_tensor(prc[:, 0:2], psm, cnt_b[:, bass.ds(b, 1), :].rearrange("p a b -> p (a b)"), ALU.mult
                            ).then_inc(sem("pch"), 1)
            e.wait_ge(sem("pch"), 2 * b + 1)
            e.reciprocal(prc[:, 2:4], prc[:, 0:2]).then_inc(sem("pch"), 1)
            e.wait_ge(sem("pch"), 2 * b + 2)
            e.tensor_tensor(pM, pM, prc[:, 2:4].unsqueeze(2).to_broadcast([P, 2, S]), ALU.mult).then_inc(sem("pP"), 1)

        def pe_pturn(e, b):
            e.wait_ge(sem("pP"), b + 1)
            wait(e, sem("v_sb"), 4 * b)
            for jc in range(2):
                for lc in range(2):
                    m = e.transpose(bank(6)[:, lc * S + jc * P:lc * S + (jc + 1) * P],
                                    pM[:, jc, lc * P:(lc + 1) * P], ident[:])
            m.then_inc(sem("pPT_ps"), 1)

        def act_pturned(e, b):
            e.wait_ge(sem("pPT_ps"), b + 1)
            e.activation(pPT, fold(bank(6), 2), ACT.Copy).then_inc(sem("pPT"), 1)

        def pe_pool(e, b):
            e.wait_ge(sem("pPT"), b + 1)
            e.wait_ge(sem("pst"), b + 1)
            for lc in range(2):
                m = e.matmul(bank(6, S), pStage[:, lc, :], pPT[:, lc, :], start=(lc == 0), stop=(lc == 1))
            m.then_inc(sem("pT_ps"), 1)

        def dve_pool(e, b):
            e.wait_ge(sem("pT_ps"), b + 1)
            e.tensor_copy(pTb, bank(6, S)).then_inc(sem("pT"), 1)

        def pe_lat(e, b):
            e.wait_ge(sem("pT"), b + 1)
            wait(e, sem("yTv"), 2 * b - 2)
            wait(e, sem("yTa"), 2 * b - 2)
            e.matmul(bank(5, S), Wd, pTb, start=True, stop=True).then_inc(sem("lat_ps"), 1)

        def act_lat(e, b):
            e.wait_ge(sem("lat_ps"), b + 1)
            e.activation(latT, bank(5, S), ACT.Copy).then_inc(sem("lat"), 1)

        def pe_q(e, b, c):
            if c == 0:
                e.wait_ge(sem("pT"), b + 1)
            elif c == 1:
                e.wait_ge(sem("lat"), b + 1)
            else:
                e.wait_ge(sem("q_sb"), 4 * b + c - 1)
            for i in range(2):
                m = e.matmul(fold(bank(6 - c % 2), 2)[:, i, :], Wq[:, (2 * c + i) * P:(2 * c + i + 1) * P], pTb,
                             start=True, stop=True)
            m.then_inc(sem("q_ps"), 1)

        def act_q(e, b, c):
            e.wait_ge(sem("q_ps"), 4 * b + c + 1)
            wait(e, sem("S_h"), 16 * b - 12 + 4 * c)
            e.activation(qT[:, 2 * c:2 * c + 2, :], fold(bank(6 - c % 2), 2), ACT.Copy).then_inc(sem("q_sb"), 1)

        def pe_k(e, b, c):
            e.wait_ge(sem("lat"), b + 1)
            if c < 2:
                e.wait_ge(sem("q_sb"), 4 * b + c + 3)
            else:
                e.wait_ge(sem("kv_sb" if c == 2 else "ka_sb"), 2 * b + 1)
            for i in range(2):
                m = e.matmul(fold(bank(6 - c % 2), 2)[:, i, :], Wk[:, (2 * c + i) * P:(2 * c + i + 1) * P], latT,
                             start=True, stop=True)
            m.then_inc(sem("k_ps"), 1)

        def k_out(e, b, c):
            e.wait_ge(sem("k_ps"), 4 * b + c + 1)
            wait(e, sem("S_h"), 16 * b - 12 + 4 * c)
            dst, src = kT[:, 2 * c:2 * c + 2, :], fold(bank(6 - c % 2), 2)
            if c % 2 == 0:
                e.tensor_copy(dst, src).then_inc(sem("kv_sb"), 1)
            else:
                e.activation(dst, src, ACT.Copy).then_inc(sem("ka_sb"), 1)

        def v_bank(c):
            return 5 if c == 1 else 6

        def pe_v(e, b, c):
            if c == 0:
                e.wait_ge(sem("kv_sb"), 2 * b + 2)
            elif c == 1:
                e.wait_ge(sem("ka_sb"), 2 * b + 2)
            else:
                e.wait_ge(sem("v_sb"), 4 * b + (1 if c == 2 else 3))
            e.matmul(bank(v_bank(c)), latT[:, (c % 2) * P:(c % 2 + 1) * P], Wv[:, (c // 2) * 512:(c // 2 + 1) * 512],
                     start=True, stop=True).then_inc(sem("v_ps"), 1)

        def act_v(e, b, c):
            e.wait_ge(sem("v_ps"), 4 * b + c + 1)
            wait(e, sem("av"), 16 * b - 8 + 8 * (c // 2))
            e.activation(V[:, c % 2, (c // 2) * 512:(c // 2 + 1) * 512], bank(v_bank(c)), ACT.Copy
                         ).then_inc(sem("v_sb"), 1)

        def pe_score(e, b, hd):
            if hd % 4 == 0:
                e.wait_ge(sem("q_sb"), 4 * b + hd // 4 + 1)
                e.wait_ge(sem("ka_sb" if hd // 4 % 2 else "kv_sb"), 2 * b + hd // 8 + 1)
            wait(e, sem("P"), 16 * b + hd - 1)
            out_, c, r = bank(hd % 2), hd // 2, (hd % 2) * HS
            for jc in range(2):
                lo, n = (0, P) if jc == 0 else (P, 2 * P)
                e.matmul(out_[:, lo:lo + n], qT[r:r + HS, c, jc * P:(jc + 1) * P], kT[r:r + HS, c, 0:n],
                         start=(jc == 0), stop=False, skip_group_check=True)
                m = e.matmul(out_[:, 2 * jc * P:(2 * jc + 1) * P], idb, cmask,
                             start=False, stop=(jc == 1), skip_group_check=True)
            m.then_inc(sem("S_h"), 1)

        def dve_max(e, b, hp):
            e.wait_ge(sem("S_h"), 16 * b + 2 * hp + 2)
            wait(e, sem("P"), 16 * b + 2 * hp - 14)
            for jc in range(2):
                c0, n = (0, P) if jc == 0 else (P, 2 * P)
                e.tensor_reduce(smx2[:, jc, 2 * hp:2 * hp + 2], banks[:, 0:2, c0:c0 + n], AX_X, ALU.max
                                ).then_inc(sem("smax"), 1)
            e.wait_ge(sem("smax"), 16 * b + 2 * hp + 2)
            e.tensor_scalar(negm[:, :, 2 * hp:2 * hp + 2], smx2[:, :, 2 * hp:2 * hp + 2], -SCALE, None, ALU.mult
                            ).then_inc(sem("negm"), 1)

        def act_prob(e, b, hd):
            e.wait_ge(sem("negm"), 8 * b + hd // 2 + 1)
            wait(e, sem("PT_ps"), 16 * b + hd - 3)
            if hd % 8 == 0:
                wait(e, sem("inv"), 2 * b - 1 + hd // 8)
            for jc in range(2):
                lo, n = (0, P) if jc == 0 else (P, 2 * P)
                m = e.activation(Pr[hd % 4][:, lo:lo + n], bank(hd % 2)[:, lo:lo + n], ACT.Exp,
                                 bias=negm[:, jc, hd:hd + 1], scale=SCALE, accum_out=sums[:, jc, hd:hd + 1])
            m.then_inc(sem("P"), 1)

        def pe_turn(e, b, hd):
            e.wait_ge(sem("P"), 16 * b + hd + 1)
            if hd:
                e.wait_ge(sem("PTa" if hd % 2 else "PTv"), 8 * b + (hd + 1) // 2)
            else:
                wait(e, sem("PTv"), 8 * b)
            for k in range(3):
                m = e.transpose(bank(2)[:, k * P:(k + 1) * P], Pr[hd % 4][:, k * P:(k + 1) * P], ident[:])
            m.then_inc(sem("PT_ps"), 1)

        def turned(e, b, hd):
            e.wait_ge(sem("PT_ps"), 16 * b + hd + 1)
            wait(e, sem("av"), 16 * b + hd - 3)
            if hd % 2 == 0:
                e.activation(PT[hd % 4], bank(2, TRI), ACT.Copy).then_inc(sem("PTa"), 1)
            else:
                e.tensor_copy(PT[hd % 4], bank(2, TRI)).then_inc(sem("PTv"), 1)

        def pe_values(e, b, hd):
            if hd % 8 == 0:
                e.wait_ge(sem("v_sb"), 4 * b + 2 + hd // 4)
                wait(e, sem("att_y"), 4 * b + hd // 4)
            e.wait_ge(sem("PTv" if hd % 2 else "PTa"), 8 * b + hd // 2 + 1)
            c, pt, v = (hd % 8) * HS, PT[hd % 4], hd * HS
            e.matmul(bank(3)[:, c:c + HS], pt[:, 0:P], V[:, 0, v:v + HS], start=True, stop=True)
            e.matmul(bank(4)[:, c:c + HS], pt[:, P:2 * P], V[:, 0, v:v + HS], start=True, stop=False)
            e.matmul(bank(4)[:, c:c + HS], pt[:, 2 * P:3 * P], V[:, 1, v:v + HS], start=False, stop=True
                     ).then_inc(sem("av"), 1)

        def dve_y(e, b, half):
            e.wait_ge(sem("av"), 16 * b + 8 * half + 8)
            if half == 0:
                wait(e, sem("yT_ps"), 4 * b)
            hs = slice(8 * half, 8 * half + 8)
            e.reciprocal(inv[:, :, hs], sums[:, :, hs]).then_inc(sem("inv"), 1)
            e.wait_ge(sem("inv"), 2 * b + half + 1)
            for jc in range(2):
                e.tensor_tensor(y[:, jc, half * 512:(half + 1) * 512].rearrange("p (h d) -> p h d", h=8),
                                bank(3 + jc).rearrange("p (h d) -> p h d", h=8),
                                inv[:, jc, hs].unsqueeze(2).to_broadcast([P, 8, HS]), ALU.mult
                                ).then_inc(sem("att_y"), 1)

        def pe_yturn(e, b, c):
            if c == 0:
                e.wait_ge(sem("att_y"), 4 * b + 4)
                if not isinstance(b, int) or b + 1 < B:
                    e.wait_ge(sem("v_sb"), 4 * b + 6)
            else:
                e.wait_ge(sem("yTa" if c == 2 else "yTv"), 2 * b + (c + 1) // 2)
            for i in range(2):
                for jc in range(2):
                    at = 2 * c + i
                    m = e.transpose(bank(5)[:, i * S + jc * P:i * S + (jc + 1) * P],
                                    y[:, jc, at * P:(at + 1) * P], ident[:])
            m.then_inc(sem("yT_ps"), 1)

        def y_turned(e, b, c):
            e.wait_ge(sem("yT_ps"), 4 * b + c + 1)
            dst, src = yT[:, 2 * c:2 * c + 2, :], fold(bank(5), 2)
            if c % 2 == 0:
                e.tensor_copy(dst, src).then_inc(sem("yTv"), 1)
            else:
                e.activation(dst, src, ACT.Copy).then_inc(sem("yTa"), 1)

        def pe_o2(e, b):
            e.wait_ge(sem("yTv"), 2 * b + 2)
            e.wait_ge(sem("yTa"), 2 * b + 2)
            e.wait_ge(sem("f_o"), 2 * b + 2)
            for jc in range(2):
                for c in range(8):
                    m = e.matmul(bank(7)[:, jc * P:(jc + 1) * P], yT[:, c, jc * P:(jc + 1) * P], Wo[:, c, :],
                                 start=(c == 0), stop=(c == 7))
            m.then_inc(sem("o2"), 1)

        def dve_x3(e, b):
            e.wait_ge(sem("o2"), b + 1)
            e.tensor_tensor(fst, xt[:, bass.ds(b * 2, 2), :], fold(bank(7, S), 2), ALU.add).then_inc(sem("x3"), 1)

        def pe_fx(e, b):
            e.wait_ge(sem("x3"), b + 1)
            for t in range(2):
                m = e.transpose(bank(7)[:, t * P:(t + 1) * P], fst[:, t, :], ident[:])
            m.then_inc(sem("fx_ps"), 1)

        def act_fx(e, b):
            e.wait_ge(sem("fx_ps"), b + 1)
            e.activation(fx3T, bank(7, S), ACT.Copy).then_inc(sem("fx"), 1)

        def pe_fc(e, b):
            e.wait_ge(sem("fx"), b + 1)
            e.wait_ge(sem("cw"), 32 * b + 32)
            for t in range(2):
                m = e.matmul(bank(7)[:, t * P:(t + 1) * P], fx3T[:, t * P:(t + 1) * P], fcw, start=True, stop=True)
            m.then_inc(sem("fc_ps"), 1)

        def dve_fc(e, b):
            e.wait_ge(sem("fc_ps"), b + 1)
            e.wait_ge(sem("cw"), 32 * b + 32)
            e.tensor_tensor(fc, fold(bank(7, S), 2), fcb.unsqueeze(1).to_broadcast([P, 2, P]), ALU.add
                            ).then_inc(sem("f_c"), 1)

        def quantise(m, src, tmp_t, dst, row):
            m(m.e.tensor_reduce(fr[:, 2, :], src, AX_X, ALU.max, apply_absolute_value=True)); m.sync()
            m(m.e.tensor_scalar(fr[:, 2, :], fr[:, 2, :], Q_EPS, None, ALU.max)); m.sync()
            m(m.e.reciprocal(fr[:, 3, :], fr[:, 2, :]))
            m(m.e.tensor_scalar(fr[:, row, :], fr[:, 2, :], fsm[:, 14 + (row != 1):15 + (row != 1)], None, ALU.mult)); m.sync()
            m(m.e.tensor_scalar(fr[:, 3, :], fr[:, 3, :], 127.0, None, ALU.mult)); m.sync()
            for t in range(2):
                m(m.e.tensor_scalar(tmp_t[:, t, :], src[:, t, :], fr[:, 3, t:t + 1], ROUND, ALU.mult, ALU.add))
            m.sync()
            m(m.e.tensor_scalar(tmp_t, tmp_t, -ROUND, 127.0, ALU.add, ALU.min)); m.sync()
            m.e.tensor_scalar(dst, tmp_t, -128.0, None, ALU.max).then_inc(sem("f_q" if row == 1 else "f_q2"), 1)

        def dve_fq(e, b):
            e.wait_ge(sem("f_c"), b + 1)
            quantise(Chain(e, "fch", b * 16), fc, ft, fq, 1)

        def pe_fqturn(e, b):
            e.wait_ge(sem("f_q"), b + 1)
            for t in range(2):
                m = e.transpose(bank(7).bitcast(BF16)[:, t * P:(t + 1) * P], fq[:, t, :], idb)
            m.then_inc(sem("fqT_ps"), 1)

        def act_fqturned(e, b):
            e.wait_ge(sem("fqT_ps"), b + 1)
            e.activation(fqT, bank(7).bitcast(BF16)[:, 0:S], ACT.Copy).then_inc(sem("fqT"), 1)

        def pe_fu(e, b, t):
            if t == 0:
                e.wait_ge(sem("fqT"), b + 1)
            else:
                e.wait_ge(sem("f_g"), 2 * b + 1)
            e.matmul(bank(7), fqT[:, t * P:(t + 1) * P], f1q, start=True, stop=True).then_inc(sem("fu_ps"), 1)

        def act_fg(e, b, t):
            e.wait_ge(sem("fu_ps"), 2 * b + t + 1)
            e.activation(fg[:, t, :], bank(7), ACT.Gelu, scale=fr[:, 1, t:t + 1]).then_inc(sem("f_g"), 1)

        def dve_fq2(e, b):
            e.wait_ge(sem("f_g"), 2 * b + 2)
            quantise(Chain(e, "fch", b * 16 + 8), fg, ft2, fq2, 0)

        def pe_fq2turn(e, b):
            e.wait_ge(sem("f_q2"), b + 1)
            for t in range(2):
                for c in range(FC):
                    k = t * FC + c
                    m = e.transpose(bank(7).bitcast(BF16)[:, k * P:(k + 1) * P], fq2[:, t, c * P:(c + 1) * P], idb)
            m.then_inc(sem("fq2T_ps"), 1)

        def dve_fq2turned(e, b):
            e.wait_ge(sem("fq2T_ps"), b + 1)
            e.tensor_copy(fq2T_.bitcast(BF16), bank(7).bitcast(BF16)).then_inc(sem("fq2T"), 1)

        def pe_fd(e, b):
            e.wait_ge(sem("fq2T"), b + 1)
            for t in range(2):
                for c in range(FC):
                    m = e.matmul(bank(7)[:, t * P:(t + 1) * P], fq2T[:, t, c, :], f2q[:, c, :],
                                 start=(c == 0), stop=(c == 3))
            m.then_inc(sem("fd_ps"), 1)

        def dve_fo(e, b):
            e.wait_ge(sem("fd_ps"), b + 1)
            e.wait_ge(sem("out"), 16 * b + 16)
            for t in range(2):
                e.scalar_tensor_tensor(out=fo[:, t, :], in0=bank(7)[:, t * P:(t + 1) * P],
                                       scalar=fr[:, 0, t:t + 1], in1=fst[:, t, :], op0=ALU.mult, op1=ALU.add
                                       ).then_inc(sem("f_o"), 1)

        PIECES = dict(
            gp=dict(stage=(1, gp_stage), mask=(1, gp_mask)),
            pe=dict(pturn=(1, pe_pturn), pool=(1, pe_pool), lat=(1, pe_lat), q=(1, pe_q), k=(1, pe_k), v=(1, pe_v),
                    V=(0, pe_v), score=(0, pe_score), turn=(0, pe_turn), values=(0, pe_values),
                    yturn=(-1, pe_yturn), o2=(-1, pe_o2), fx=(-1, pe_fx), fc=(-1, pe_fc), fqturn=(-1, pe_fqturn),
                    fu=(-1, pe_fu), fq2turn=(-1, pe_fq2turn), fd=(-1, pe_fd)),
            act=dict(pexp=(1, act_pexp), pturned=(1, act_pturned), lat=(1, act_lat), q=(1, act_q), k=(1, k_out),
                     v=(1, act_v), V=(0, act_v), prob=(0, act_prob), turned=(0, turned), yturned=(-1, y_turned),
                     fx=(-1, act_fx), fqturned=(-1, act_fqturned), fg=(-1, act_fg)),
            dve=dict(pmax=(1, dve_pmax), pnorm=(1, dve_pnorm), pool=(1, dve_pool), k=(1, k_out), max=(0, dve_max),
                     turned=(0, turned), y=(0, dve_y), Y=(-1, dve_y), yturned=(-1, y_turned), x3=(-1, dve_x3),
                     fc=(-1, dve_fc), fq=(-1, dve_fq), fq2=(-1, dve_fq2), fq2turned=(-1, dve_fq2turned),
                     fo=(-1, dve_fo)))

        def run(e, engine, order):
            def slot(k):
                for token in order.split():
                    name, _, arg = token.partition(":")
                    shift, fn = PIECES[engine][name]
                    if not isinstance(k, int) or 0 <= k + shift < B:
                        fn(e, k + shift, *((int(arg),) if arg else ()))
            slot(-1)
            slot(0)
            with e.Fori(1, B - 1) as k:
                slot(k)
            slot(B - 1)
            slot(B)


        block = ctx.enter_context(nc.Block())

        @block.sync
        def _(e):
            e.dma_start(xtok, x_tok).then_inc(sem("x_in"), 16)
            for j, n in enumerate(("condB_zX", "condB_zY", "condB_zR")):
                e.dma_start(zb[:, j, :], bass.AP(io[n].tensor, 0, [[0, P], [1, B]])).then_inc(sem("z_in"), 16)
            e.dma_start(lng[:], io["L0_attn_ln_g"].rearrange("(p a) -> p a", a=1)).then_inc(sem("ln_in"), 16)
            e.dma_start(lnb[:], io["L0_attn_ln_b"].rearrange("(p a) -> p a", a=1)).then_inc(sem("ln_in"), 16)
            e.dma_start(A_all[:].rearrange("p l s -> p (l s)"), io["A_log"]).then_inc(sem("alog_in"), 16)

            def prepare(L):
                e.wait_ge(sem("scr"), 32 * L + 32)
                e.dma_start(raw_in, layer_of(io["in_w"], L)).then_inc(sem("raw"), 16)
                e.dma_start(raw_cw, bass.AP(io["conv_w"].tensor, L * (TAPS * 2 * P), [[0, P], [1, TAPS * 2 * P]])
                            ).then_inc(sem("raw"), 16)
                e.dma_start(bunF[:, FC_Z:FC_CB], layer_of(io["zxp_w"], L)).then_inc(sem("raw"), 16)
                e.dma_start(raw_out, layer_of(io["out_w"], L)).then_inc(sem("raw"), 16)
                e.dma_start(raw_sm, layer_of(io["small"], L)).then_inc(sem("raw"), 16)
                e.wait_ge(sem("bun"), 5 * L + 5)
                e.dma_start(layer_of(scrF, L), bunF).then_inc(sem("scr"), 16)
                e.dma_start(layer_of(scrS, L), bunS).then_inc(sem("scr"), 16)

            def load(L):
                wait(e, sem("dt"), L * (2 * NPAIR))
                wait(e, sem("dt_ps"), L * (2 * NPAIR))
                e.dma_start(wF[:], layer_of(scrF, L)).then_inc(sem("wF"), 16)
                e.dma_start(wdt[BC3:BC3 + RANK, :], layer_of(io["dt_w"], L)).then_inc(sem("wF"), 16)
                wait(e, sem("o_ps"), L * NPAIR)
                e.dma_start(wS[:], layer_of(scrS, L)).then_inc(sem("wS"), 16)

            e.sem_inc(sem("scr"), 32)
            prepare(0)
            e.wait_ge(sem("scr"), 64)
            load(0)
            with e.Fori(1, LAYERS) as L:
                prepare(L)
            e.wait_ge(sem("scr"), 32 * LAYERS + 32)
            with e.Fori(1, LAYERS) as L:
                load(L)
            tail_sync(e)

        @block.gpsimd
        def _(e):
            count = [0]

            def const(ins):
                count[0] += 1
                ins.then_inc(sem("const"), 1)
                e.wait_ge(sem("const"), count[0])

            def diagonal(t, value, base, cols):
                const(e.affine_select(out=t, in_=t, compare_op=ALU.not_equal, fill=value, base=base,
                                      pattern=cols, channel_multiplier=1))

            const(e.memset(ident[:], 0.0))
            diagonal(ident[:], 1.0, 0, [[-1, P]])
            const(e.memset(tri, 0.0))
            diagonal(tri, -2.0, 0, [[-1, P]])
            diagonal(tri, 1.0, 1, [[-1, P]])
            diagonal(tri, 1.0, -1, [[-1, P]])
            diagonal(tri[:, 0:1], 2.0, -1, [[0, 1]])
            diagonal(tri[:, P - 1:P], 2.0, 2 - P, [[0, 1]])
            const(e.memset(mean_w[:], 1.0 / P))
            const(e.tensor_tensor(center_w[:], ident[:], mean_w[:], ALU.subtract))
            const(e.memset(eps[:], LN_EPS))
            const(e.memset(xn[:, :, 0:TAPS - 1], 0.0))
            assert count[0] == CONSTS - 4
            const(e.memset(sel[:], 0.0))
            for part in range(3):
                diagonal(sel[:], 1.0, -2 * NS * part, [[-1, 2 * NS], [0, P]])
            assert count[0] == CONSTS
            for half in range(HALVES):
                e.memset(dA[half][:, :, 0:1], 0.0).then_inc(sem("dA0"), 1)

            def slot(p, q):
                for i in range(2):
                    n = 2 * p + i
                    for half in range(HALVES):
                        hb = h[2 * i + half]
                        e.wait_ge(sem("scan"), 2 * n + half + 1)
                        e.wait_ge(sem("C"), 8 * n + 8)
                        e.tensor_tensor(hb[:], hb[:], Cb[i][:], ALU.mult).then_inc(sem("hC"), 1)
                        e.wait_ge(sem("hC"), 4 * p + 2 * i + half + 1)
                        e.tensor_tensor(hb[:, PRE:2 * PRE, :], hb[:, 0:PRE, :], hb[:, PRE:2 * PRE, :], ALU.add
                                        ).then_inc(sem("pre"), 1)

            with e.Fori(0, SLOTS) as p:
                slot(p, 0)
            tail_gpsimd(e)

        def cols(t):
            c = (t % NPAIR) * PAIR
            return bass.ds(c, PAIR)

        def pe_center(e, t, q):
            e.wait_ge(sem("res"), t + 1)
            wait(e, sem("dt"), 2 * t)
            e.matmul(ps_F[0][:], center_w[:], xs[:, cols(t)], start=True, stop=True).then_inc(sem("cen"), 1)

        def act_square(e, t, q):
            e.wait_ge(sem("cen"), t + 1)
            e.activation(rstd[:], ps_F[0][:], ACT.Square).then_inc(sem("sq"), 1)

        def pe_var(e, t, q):
            e.wait_ge(sem("sq"), t + 1)
            e.matmul(ps_F[1][:], mean_w[:], rstd[:], start=True, stop=True).then_inc(sem("var"), 1)

        def act_lnv(e, t, q):
            e.wait_ge(sem("var"), t + 1)
            e.activation(rstd[:], ps_F[1][:], ACT.Ln, bias=eps[:, 0:1]).then_inc(sem("lnv"), 1)

        def act_rstd(e, t, q):
            e.wait_ge(sem("lnv"), t + 1)
            e.activation(rstd[:], rstd[:], ACT.Exp, scale=-0.5).then_inc(sem("rstd"), 1)

        def dve_norm(e, t, q):
            e.wait_ge(sem("rstd"), t + 1)
            e.scalar_tensor_tensor(out=xc[:], in0=ps_F[0][:], scalar=lng[:, 0:1], in1=rstd[:],
                                   op0=ALU.mult, op1=ALU.mult).then_inc(sem("xg"), 1)
            e.wait_ge(sem("xg"), t + 1)
            e.tensor_scalar(xn[:, :, TAPS - 1:], xc[:].rearrange("p (b l) -> p b l", b=2), lnb[:, 0:1], None,
                            ALU.add).then_inc(sem("xn"), 1)

        def pe_conv(e, t, q, half):
            if half == 0:
                e.wait_ge(sem("xn"), t + 1)
                e.wait_ge(sem("wF"), 32 * (t // NPAIR) + 32)
            for k in range(TAPS):
                m = e.matmul(ps_F[half][:].rearrange("p (b l) -> p b l", b=2),
                             wF[:, FC_TAP + k * 2 * P + half * P:FC_TAP + k * 2 * P + (half + 1) * P],
                             xn[:, :, k:k + S], start=(k == 0), stop=(k == TAPS - 1))
            m.then_inc(sem("conv"), 1)

        def act_xh(e, t, q, half):
            e.wait_ge(sem("conv"), 2 * t + half + 1)
            e.activation(xh[:, half, :], ps_F[half][:], ACT.Identity, bias=wF[:, FC_CB + half:FC_CB + half + 1]
                         ).then_inc(sem("xh"), 1)

        def act_th(e, t, q):
            e.wait_ge(sem("xh"), 2 * t + 2)
            e.activation(th[:], xh[:], ACT.Tanh).then_inc(sem("th"), 1)

        def dve_xm(e, t, q):
            e.wait_ge(sem("th"), t + 1)
            e.scalar_tensor_tensor(out=xm[q][:], in0=th[:], scalar=1.0, in1=xh[:],
                                   op0=ALU.add, op1=ALU.mult).then_inc(sem("xm"), 1)

        def pe_z(e, t, q, half):
            e.wait_ge(sem("xh"), 2 * t + half + 1)
            c = FC_Z + half * P
            e.matmul(ps_F[half][:].rearrange("p (b l) -> p b l", b=2), wF[:, c:c + P],
                     xn[:, :, TAPS - 1:], start=True, stop=True).then_inc(sem("z_ps"), 1)

        def act_zt(e, t, q, half):
            if half == 0:
                e.wait_ge(sem("xm"), t + 1)
            e.wait_ge(sem("z_ps"), 2 * t + half + 1)
            e.activation(th[:, half, :], ps_F[half][:], ACT.Tanh, scale=0.5).then_inc(sem("zt"), 1)

        def dve_zs(e, t, q, half):
            e.wait_ge(sem("zt"), 2 * t + half + 1)
            e.scalar_tensor_tensor(out=zs[q][:, half, :], in0=th[:, half, :], scalar=1.0,
                                   in1=ps_F[half][:], op0=ALU.add, op1=ALU.mult).then_inc(sem("zs"), 1)

        def pe_xproj(e, t, q):
            e.wait_ge(sem("zs"), 2 * t + 1)
            e.wait_ge(sem("xm"), t + 1)
            for half in range(HALVES):
                c = FC_XP + half * XPN
                m = e.matmul(ps_F[0][0:XPN, :], wF[:, c:c + XPN], xm[q][:, half, :],
                             start=(half == 0), stop=(half == 1))
            m.then_inc(sem("xd"), 1)

        def act_high(e, t, q):
            e.wait_ge(sem("xd"), t + 1)
            e.activation(bc[q][:, :], ps_F[0][0:BC3, :], ACT.Copy).then_inc(sem("hi"), 1)

        def act_rank8(e, t, q):
            e.wait_ge(sem("xd"), t + 1)
            e.activation(dt8, ps_F[0][BC3:XPN, :], ACT.Copy).then_inc(sem("hi"), 1)

        def dve_split(e, t, q):
            e.wait_ge(sem("hi"), 2 * t + 1)
            m = 2 * NS
            e.tensor_tensor(r1, ps_F[0][0:BC3, :], bc[q][:, :], ALU.subtract).then_inc(sem("split"), 1)
            e.wait_ge(sem("split"), 3 * t + 1)
            e.tensor_copy(r2[2 * m:BC3, :], r1[2 * m:BC3, :]).then_inc(sem("split"), 1)
            e.tensor_copy(bc[q][m:2 * m, :], r1[m:2 * m, :]).then_inc(sem("split"), 1)
            e.wait_ge(sem("split"), 3 * t + 2)
            e.tensor_tensor(bc[q][2 * m:BC3, :], r1[2 * m:BC3, :], r2[2 * m:BC3, :],
                            ALU.subtract).then_inc(sem("bc"), 1)

        def pe_dt(e, t, q, half):
            if half == 0:
                e.wait_ge(sem("hi"), 2 * t + 2)
                e.wait_ge(sem("zs"), 2 * t + 2)
                if not isinstance(t, int) or t >= 2:
                    e.wait_ge(sem("res"), t - 1 + NPAIR)
            else:
                e.wait_ge(sem("bc"), t + 1)
            e.matmul(ps_F[1 - half][:], wdt[BC3:BC3 + RANK, half * P:(half + 1) * P], dt8,
                     start=True, stop=True).then_inc(sem("dt_ps"), 1)

        def dve_amin(e, t, q, half):
            e.wait_ge(sem("dt_ps"), 2 * t + half + 1)
            e.tensor_scalar(xh[:, half, :], ps_F[1 - half][:], wF[:, FC_DTB + half:FC_DTB + half + 1], 40.0,
                            ALU.add, ALU.min).then_inc(sem("amin"), 1)

        def act_sp_exp(e, t, q):
            e.wait_ge(sem("amin"), 2 * t + 2)
            e.activation(xh[:], xh[:], ACT.Exp).then_inc(sem("sp"), 1)

        def act_sp_ln(e, t, q):
            e.wait_ge(sem("sp"), 2 * t + 1)
            e.activation(xh[:], xh[:], ACT.Ln, bias=1.0).then_inc(sem("sp"), 1)

        def dve_dt(e, t, q):
            e.wait_ge(sem("sp"), 2 * t + 2)
            wait(e, sem("dA"), 4 * t)
            for half in range(HALVES):
                e.scalar_tensor_tensor(out=dt[:, half, :], in0=ps_F[1 - half][:],
                                       scalar=wF[:, FC_DTB + half:FC_DTB + half + 1], in1=xh[:, half, :],
                                       op0=ALU.add, op1=ALU.max).then_inc(sem("dt"), 1)

        def dve_u(e, t, q):
            e.wait_ge(sem("dt"), 2 * t + 2)
            e.tensor_tensor(u[:], dt[:], xm[q][:], ALU.mult).then_inc(sem("u"), 1)

        def pe_B(e, p, q, i, g):
            n = 2 * p + i
            if i == 0 and g == 0:
                e.wait_ge(sem("bc"), p + 1)
            wait(e, sem("mul"), 8 * n + 2 * g - 2)
            for j in range(4):
                m = e.matmul(ps_B[g % 2][:, j, :], sel[:, 4 * g + j, :], bc[q][:, i * S:(i + 1) * S],
                             start=True, stop=True)
            m.then_inc(sem("B"), 1)

        def pe_C(e, p, q, i, c):
            n = 2 * p + i
            if i == 0 and c == 0:
                e.wait_ge(sem("bc"), p + 1)
            wait(e, sem("C"), 8 * n + c)
            for j in range(2):
                m = e.matmul(ps_C[:, j, :], sel[:, NS + 2 * c + j, :], bc[q][:, i * S:(i + 1) * S],
                             start=True, stop=True)
            m.then_inc(sem("C_ps"), 1)

        def act_C(e, p, q, i, c):
            n = 2 * p + i
            if c == 0:
                wait(e, sem("hC"), 2 * n - 2)
            e.wait_ge(sem("C_ps"), 8 * n + c + 1)
            e.activation(Cb[i][:, 2 * c:2 * c + 2, :], ps_C, ACT.Copy).then_inc(sem("C"), 1)

        def act_dA(e, p, q, i, half, part):
            n = 2 * p + i
            if i == 0 and half == 0 and part == 0:
                wait(e, sem("dA"), 4 * p)
                e.activation(A_cur[q][:], A_all[:, bass.ds(p // NPAIR, 1), :].rearrange("p l s -> p (l s)"),
                             ACT.Copy).then_inc(sem("A_cur"), 1)
                e.wait_ge(sem("A_cur"), p + 1)
                e.wait_ge(sem("dt"), 2 * p + 2)
            if part == 0:
                wait(e, sem("scan"), 2 * n + half - 1)
                if isinstance(p, int) and p == 0:
                    e.wait_ge(sem("dA0"), 2)
            for s in range(4 * part, 4 * part + 4):
                m = e.activation(dA[half][:, s, 1:S], dt[:, half, i * S + 1:(i + 1) * S], ACT.Exp,
                                 scale=A_cur[q][:, half * NS + s:half * NS + s + 1])
            if part == 3:
                m.then_inc(sem("dA"), 1)

        def dve_mul(e, p, q, i, g, half):
            n = 2 * p + i
            e.wait_ge(sem("B"), 4 * n + g + 1)
            if isinstance(p, int) and p == 0 and i == 1 and g == 0 and half == 0:
                e.wait_ge(sem("scr"), 32 * LAYERS + 32)
            if g == 0 and half == 0:
                e.wait_ge(sem("u"), p + 1)
                if isinstance(p, int) and p == 0:
                    e.wait_ge(sem("res"), NPAIR)
            e.tensor_tensor(h[2 * i + half][:, 4 * g:4 * g + 4, :], ps_B[g % 2],
                            u[:, half, i * S:(i + 1) * S].unsqueeze(1).to_broadcast([P, 4, S]),
                            ALU.mult).then_inc(sem("mul"), 1)

        def dve_scan(e, p, q, i, half):
            n = 2 * p + i
            e.wait_ge(sem("dA"), 2 * n + half + 1)
            e.wait_ge(sem("mul"), 8 * n + 8)
            hb = h[2 * i + half][:, :, :].rearrange("p s l -> p (s l)")
            e.tensor_tensor_scan(hb, dA[half][:, :, :].rearrange("p s l -> p (s l)"), hb, 0.0,
                                 ALU.mult, ALU.add).then_inc(sem("scan"), 1)

        def pe_sum(e, p, q, i, half, part):
            n = 2 * p + i
            if part == 0:
                e.wait_ge(sem("pre"), 2 * n + half + 1)
                if half == 0:
                    wait(e, sem("gate"), n)
            for s in SUM_PARTS[part]:
                e.matmul(ps_Y[:, half, :], ident[:], h[2 * i + half][:, s, :], start=(s == PRE), stop=False)
            if part == 3:
                if i == 0 and half == 0:
                    e.wait_ge(sem("wS"), 16 * (p // NPAIR) + 16)
                e.matmul(ps_Y[:, half, :], wS[:, SC_D + half * P:SC_D + (half + 1) * P],
                         xm[q][:, half, i * S:(i + 1) * S], start=False, stop=True).then_inc(sem("y"), 1)

        def dve_gate(e, p, q, i):
            n = 2 * p + i
            e.wait_ge(sem("y"), 2 * n + 2)
            e.tensor_tensor(yz[:, :, i, :], ps_Y, zs[q][:, :, i * S:(i + 1) * S],
                            ALU.mult).then_inc(sem("gate"), 1)

        def pe_out(e, p, q):
            e.wait_ge(sem("gate"), 2 * p + 2)
            if isinstance(p, int) and p >= SLOTS - 2:
                e.wait_ge(sem("dt"), 2 * SLOTS)
                wait(e, sem("res"), p + NPAIR)
            else:
                e.wait_ge(sem("zs"), 2 * p + 6)
            for half in range(HALVES):
                m = e.matmul(ps_F[1][:], wS[:, SC_OUT + half * P:SC_OUT + (half + 1) * P],
                             yz[:, half, :, :].rearrange("p i l -> p (i l)"), start=(half == 0), stop=(half == 1))
            m.then_inc(sem("o_ps"), 1)

        def dve_res(e, p, q):
            e.wait_ge(sem("o_ps"), p + 1)
            e.tensor_tensor(xs[:, cols(p)], xs[:, cols(p)], ps_F[1][:], ALU.add).then_inc(sem("res"), 1)
            e.wait_ge(sem("res"), p + 1 + NPAIR)

        def piece(e, table, token, p, q):
            name, _, arg = token.partition(":")
            front, fn = table[name]
            if front:
                return fn(e, p + 1, 1 - q, *map(int, arg))
            if name in ("out", "res"):
                return fn(e, p - 1, 1 - q)
            at, args = arg[0], map(int, arg[1:])
            pair, par, i = {"l": (p - 1, 1 - q, 1), "a": (p, q, 0), "b": (p, q, 1), "n": (p + 1, 1 - q, 0)}[at]
            fn(e, pair, par, i, *args)

        PE = dict(center=(1, pe_center), var=(1, pe_var), conv=(1, pe_conv), z=(1, pe_z), xproj=(1, pe_xproj),
                  dt=(1, pe_dt), B=(0, pe_B), C=(0, pe_C), sum=(0, pe_sum), out=(0, pe_out))
        ACTE = dict(square=(1, act_square), lnv=(1, act_lnv), rstd=(1, act_rstd), xh=(1, act_xh), th=(1, act_th),
                    zt=(1, act_zt), high=(1, act_high), rank8=(1, act_rank8), sp_exp=(1, act_sp_exp),
                    sp_ln=(1, act_sp_ln), dA=(0, act_dA), C=(0, act_C))
        DVE = dict(norm=(1, dve_norm), xm=(1, dve_xm), zs=(1, dve_zs), split=(1, dve_split), amin=(1, dve_amin),
                   dt=(1, dve_dt), u=(1, dve_u), mul=(0, dve_mul), scan=(0, dve_scan), gate=(0, dve_gate),
                   res=(0, dve_res))

        def in_order(table, order):
            def slot(e, p, q, prev, nxt):
                for token in order.split():
                    name, _, arg = token.partition(":")
                    ahead = table[name][0] or arg[:1] == "n"
                    behind = name in ("out", "res") or arg[:1] == "l"
                    if (ahead and not nxt) or (behind and not prev):
                        continue
                    piece(e, table, token, p, q)
            return slot

        def first(e, table, order):
            for token in order.split():
                piece(e, table, token, -1, 1)

        def slots(e, slot):
            slot(e, 0, 0, False, True)
            with e.Fori(0, (SLOTS - 2) // 2) as j:
                slot(e, j * 2 + 1, 1, True, True)
                slot(e, j * 2 + 2, 0, True, True)
            slot(e, SLOTS - 1, 1, True, False)

        LAST, LQ = SLOTS - 1, 1

        @block.tensor
        def _(e):
            e.wait_ge(sem("x_in"), 16)
            e.wait_ge(sem("const"), CONSTS - 4)
            for k in range(4):
                wait(e, sem("xT"), k - 1)
                for j in range(4):
                    m = e.transpose(ps_F[k % 2][:, j * P:(j + 1) * P], xtok[:, 4 * k + j, :], ident[:])
                m.then_inc(sem("xT_ps"), 1)
            for k in range(4):
                e.wait_ge(sem("xT"), max(k, 2 + k % 2) + 1)
                wait(e, sem("lapx"), k - 1)
                e.matmul(ps_F[k % 2][:].rearrange("p (b l) -> p b l", b=2), tri,
                         ypad[:, 2 * k:2 * k + 2, 1:S + 1], start=True, stop=True).then_inc(sem("lapx_ps"), 1)
            e.wait_ge(sem("lapx"), 4)
            first(e, PE, "center var conv:0 conv:1 z:0 z:1 xproj dt:0 dt:1")
            e.wait_ge(sem("const"), CONSTS)
            first(e, PE, "C:n0 C:n1 C:n2 C:n3 C:n4 C:n5 C:n6 C:n7 B:n0 B:n1")
            slots(e, in_order(PE, PE_ORDER))
            for part in range(4):
                pe_sum(e, LAST, LQ, 1, 1, part)
            pe_out(e, LAST, LQ)
            tail_tensor(e)

        @block.scalar
        def _(e):
            for k in range(4):
                e.wait_ge(sem("xT_ps"), k + 1)
                e.activation(ypad[:, 2 * k:2 * k + 2, 1:S + 1], ps_F[k % 2][:].rearrange("p (b l) -> p b l", b=2),
                             ACT.Copy).then_inc(sem("xT"), 1)
            for k in range(4):
                e.wait_ge(sem("lapx_ps"), k + 1)
                e.activation(lapx[:, 2 * k:2 * k + 2, :], ps_F[k % 2][:].rearrange("p (b l) -> p b l", b=2),
                             ACT.Copy).then_inc(sem("lapx"), 1)
            e.wait_ge(sem("alog_in"), 16)
            e.activation(A_all[:], A_all[:], ACT.Exp).then_inc(sem("A"), 1)
            e.wait_ge(sem("A"), 1)
            e.activation(A_all[:], A_all[:], ACT.Copy, scale=-1.0).then_inc(sem("A"), 1)
            e.wait_ge(sem("A"), 2)
            first(e, ACTE, "square lnv rstd xh:0 xh:1 th zt:0 zt:1 high rank8 "
                           "C:n0 C:n1 C:n2 C:n3 C:n4 C:n5 C:n6 C:n7 sp_exp sp_ln dA:n00 dA:n01 dA:n02 dA:n03")
            slots(e, in_order(ACTE, ACT_ORDER))
            tail_scalar(e)

        @block.vector
        def _(e):
            count = [0]

            def du(ins):
                count[0] += 1
                ins.then_inc(sem("du"), 1)
                e.wait_ge(sem("du"), count[0])

            def reaction(k):
                bb = slice(2 * k, 2 * k + 2)
                y, lx, ly, g = ypad[:, bb, 1:S + 1], lapx[:, bb, :], lapy[:, bb, :], grow[:, bb, :]

                def per_batch(j):
                    return zb[:, j, bb].unsqueeze(2).to_broadcast([P, 2, S])

                e.wait_ge(sem("xT"), k + 1)
                du(e.tensor_copy(ypad[:, bb, 0:1], ypad[:, bb, 2:3]))
                du(e.tensor_copy(ypad[:, bb, S + 1:S + 2], ypad[:, bb, S - 1:S]))
                du(e.tensor_tensor(ly, ypad[:, bb, 0:S], ypad[:, bb, 2:S + 2], ALU.add))
                du(e.scalar_tensor_tensor(out=ly, in0=y, scalar=-2.0, in1=ly, op0=ALU.mult, op1=ALU.add))
                e.wait_ge(sem("z_in"), 48)
                du(e.tensor_tensor(ly, ly, per_batch(1), ALU.mult))
                du(e.scalar_tensor_tensor(out=g, in0=y, scalar=-1.0, in1=y, op0=ALU.add, op1=ALU.mult))
                du(e.tensor_tensor(g, g, per_batch(2), ALU.mult))
                du(e.tensor_tensor(g, ly, g, ALU.subtract))
                e.wait_ge(sem("lapx"), k + 1)
                du(e.tensor_tensor(lx, lx, per_batch(0), ALU.mult))
                e.tensor_tensor(xs[:, k * PAIR:(k + 1) * PAIR].rearrange("p (b l) -> p b l", b=2), lx, g, ALU.add
                                ).then_inc(sem("res"), 1)

            def bundle(L):
                e.wait_ge(sem("raw"), 80 * L + 80)
                e.scalar_tensor_tensor(out=bunF[:, 0:FC_Z].rearrange("p (k e) -> p k e", k=TAPS),
                                       in0=raw_in.unsqueeze(1).to_broadcast([P, TAPS, 2 * P]), scalar=0.5,
                                       in1=raw_cw.rearrange("p (k e) -> p k e", k=TAPS),
                                       op0=ALU.mult, op1=ALU.mult).then_inc(sem("bun"), 1)
                e.tensor_scalar(bunF[:, FC_CB:FC_END], raw_sm[:, 0:HALVES], 0.5, None, ALU.mult
                                ).then_inc(sem("bun"), 1)
                for half in range(HALVES):
                    e.tensor_scalar(bunS[:, SC_D + half * P:SC_D + (half + 1) * P], ident[:],
                                    raw_sm[:, HALVES + half:HALVES + half + 1], None, ALU.mult
                                    ).then_inc(sem("bun"), 1)
                e.tensor_scalar(bunS[:, SC_OUT:SC_END], raw_out, 0.5, None, ALU.mult).then_inc(sem("bun"), 1)

            e.wait_ge(sem("const"), CONSTS - 4)
            reaction(0)
            bundle(0)
            e.wait_ge(sem("ln_in"), 32)
            first(e, DVE, "norm")
            reaction(1)
            bundle(1)
            reaction(2)
            first(e, DVE, "xm zs:0 zs:1 split amin:0 amin:1")
            bundle(2)
            first(e, DVE, "dt u")
            reaction(3)
            bundle(3)
            slots(e, in_order(DVE, DVE_ORDER))
            dve_gate(e, LAST, LQ, 1)
            dve_res(e, LAST, LQ)
            tail_vector(e)


ATT_GP = """
mask stage"""
ATT_PE = """
score:0 score:1 V:2 yturn:0 V:3 score:2 score:3 turn:0 yturn:1 values:0 pturn turn:1 yturn:2 score:4
score:5 turn:2 values:1 yturn:3 values:2 turn:3 pool turn:4 score:6 score:7 turn:5 o2 score:8
score:9 fx turn:6 values:3 fc turn:7 lat values:4 q:0 score:10 score:11 values:5 turn:8 fqturn
values:6 q:1 turn:9 fu:0 values:7 score:12 score:13 turn:10 values:8 fu:1 turn:11 values:9 q:2
values:10 values:11 q:3 score:14 score:15 k:0 turn:12 k:1 fq2turn turn:13 values:12 k:2 fd k:3
turn:14 v:0 turn:15 values:13 values:14 v:1 values:15"""
ATT_ACT = """
pexp V:2 prob:0 prob:1 V:3 turned:0 yturned:1 prob:2 prob:3 turned:2 pturned prob:4 prob:5 turned:4
yturned:3 prob:6 prob:7 fx turned:6 prob:8 prob:9 lat turned:8 q:0 fqturned prob:10 prob:11 fg:0
turned:10 q:1 fg:1 prob:12 prob:13 q:2 q:3 turned:12 prob:14 k:1 prob:15 turned:14 k:3 v:0 v:1"""
ATT_DVE = """
pmax Y:1 max:0 yturned:0 pnorm max:1 turned:1 yturned:2 max:2 turned:3 pool max:3 turned:5 x3 max:4
fc turned:7 fq max:5 turned:9 y:0 max:6 turned:11 fq2 k:0 max:7 fq2turned turned:13 k:2 fo turned:15"""

PE_ORDER = """
B:a2 B:a3 C:b0 center var sum:l10 sum:l11 sum:l12 sum:l13 C:b1 B:b0 B:b1 C:b2 conv:0 C:b3 conv:1
B:b2 C:b4 B:b3 C:b5 z:0 sum:a00 C:b6 z:1 sum:a01 C:b7 sum:a02 xproj out sum:a03 dt:0 sum:a10 C:n0
dt:1 C:n1 sum:a11 C:n2 sum:a12 C:n3 sum:a13 C:n4 B:n0 B:n1 C:n5 sum:b00 sum:b01 C:n6 sum:b02 sum:b03
C:n7"""
ACT_ORDER = """
square dA:a10 lnv C:b0 rstd dA:a11 C:b1 dA:a12 C:b2 dA:a13 dA:b00 xh:0 C:b3 dA:b01 C:b4 xh:1 th C:b5
dA:b02 C:b6 zt:0 zt:1 dA:b03 dA:b10 high C:b7 rank8 dA:b11 dA:b12 dA:b13 C:n0 C:n1 sp_exp C:n2 sp_ln
C:n3 C:n4 C:n5 dA:n00 dA:n01 C:n6 dA:n02 C:n7 dA:n03"""
DVE_ORDER = """
mul:a00 mul:a01 mul:a10 mul:a11 mul:a20 mul:a21 mul:a30 mul:a31 scan:a0 norm gate:l mul:b00 mul:b01
mul:b10 mul:b11 scan:a1 mul:b20 mul:b21 xm mul:b30 mul:b31 zs:0 zs:1 scan:b0 res split amin:0 amin:1
scan:b1 gate:a dt u"""
PRE = 3
STEP = (NS - PRE) // 4
SUM_PARTS = [range(PRE + part * STEP, NS if part == 3 else PRE + (part + 1) * STEP) for part in range(4)]
CONSTS = 16

def laid_out(a):
    import numpy as np

    def halves_first(w):
        n = w.shape[2]
        return w.reshape(LAYERS, HALVES, P, n).transpose(0, 2, 1, 3).reshape(LAYERS, P, HALVES * n)

    in_t = a["L0_attn_in_proj_w"].transpose(0, 2, 1)
    xp = a["L0_attn_x_proj_w"].transpose(0, 2, 1)
    xp = np.concatenate([xp[:, :, RANK:]] * 3 + [xp[:, :, :RANK]], axis=2)
    col = lambda n: a[n].reshape(LAYERS, HALVES, P).transpose(0, 2, 1)
    return {
        "in_w": in_t[:, :, :2 * P],
        "conv_w": a["L0_attn_conv_w"].transpose(0, 2, 1),
        "zxp_w": np.concatenate([in_t[:, :, 2 * P:], halves_first(xp), col("L0_attn_dt_proj_b")], axis=2),
        "out_w": halves_first(a["L0_attn_out_proj_w"].transpose(0, 2, 1)),
        "small": np.concatenate([col("L0_attn_conv_b"), col("L0_attn_D_skip")], axis=2),
        "dt_w": a["L0_attn_dt_proj_w"].transpose(0, 2, 1),
        "b1c": a["L0_cond2_b1"].reshape(FC, P).T,
        "cw": a["L1_cond2_weight"].transpose(0, 2, 1),
        "f1t": a["L1_ffn_w1"].T,
        "f2t": a["L1_ffn_w2"].T.reshape(FC, P, P).transpose(1, 0, 2).reshape(P, FF),
        "A_log": a["L0_attn_A_log"].reshape(LAYERS, HALVES, P, NS).transpose(2, 0, 1, 3).reshape(P, -1),
    }


def constants():
    import numpy as np
    j, l = np.arange(S)[:, None], np.arange(S)[None, :]
    keep = np.stack([l <= j, l >= j, l != j])
    by_part = keep.reshape(3, 2, P, S).transpose(2, 0, 1, 3)
    return {
        "iota8": (100 + np.arange(NE)).astype(np.float32),
        "pmask": np.where(by_part, 0, -BIG).astype(np.float32).reshape(P, -1),
        "pcnt": by_part.sum(-1).astype(np.float32).reshape(P, -1),
        "cmask": np.where(np.arange(P)[None, :] <= np.arange(P)[:, None], 0, -BIG).astype(np.float32),
    }


SAME = ["x", "condB_zX", "condB_zY", "condB_zR", "itok_B_0_7", "itok_B_0_2", "L0_attn_ln_g", "L0_attn_ln_b",
        "L0_cond2_W1", "L0_cond2_W2", "L0_cond2_b2", "L0_cond2_We", "L0_cond2_be", "L0_ffn_gate_kernel",
        "L0_ffn_w0", "L0_ffn_w1", "L0_ffn_wo", "L1_cond_W1", "L1_cond_b1", "L1_cond_v", "L1_attn_w_kv_down",
        "L1_attn_w_kv_up", "L1_attn_w_q", "L1_attn_w_out", "L1_cond2_bias"]


def kernel(**inputs):
    import numpy as np
    import concourse.bacc as bacc
    from concourse.bass_utils import run_bass_kernel_spmd

    nc = bacc.Bacc("TRN2", target_bir_lowering=False, num_devices=1)
    given = {n: np.asarray(v) for n, v in inputs.items()}
    arrays = {n: np.ascontiguousarray(v) for n, v in {**{n: given[n] for n in SAME}, **laid_out(given), **constants()}.items()}
    io = {n: nc.dram_tensor(f"in_{n}", v.shape, mybir.dt.from_np(v.dtype), kind="ExternalInput").ap()
          for n, v in arrays.items()}
    io["out"] = nc.dram_tensor("out_x", (B, S, D), F32, kind="ExternalOutput").ap()
    program(nc, io)
    r = run_bass_kernel_spmd(nc, [{f"in_{n}": v for n, v in arrays.items()}], core_ids=[0])
    return r.results[0]["out_x"]
```
